# Optimizing a Trainium2 kernel written in Bass

```python
import numpy as np
import jax
import jax.numpy as jnp

def _softmax(x, axis=-1):
    return jax.nn.softmax(x, axis=axis)

def _gelu(x):
    return jax.nn.gelu(x, approximate=True)

def _silu(x):
    return jax.nn.silu(x)

def _sigmoid(x):
    return jax.nn.sigmoid(x)

def _layernorm(x, axis=-1, eps=1e-05):
    m = jnp.mean(x, axis=axis, keepdims=True)
    v = jnp.var(x, axis=axis, keepdims=True)
    return (x - m) / jnp.sqrt(v + eps)

def _scatter_add(tgt, idx, src, axis=0):
    return tgt.at[idx].add(src)

def _segment_sum(src, seg, n):
    return jax.ops.segment_sum(src, seg, n)
kernel_name = 'mk_gps_d2_gnn_r8_033a6d'

def setup_inputs(seed: int=0):
    np.random.seed(seed)
    _w = jnp.asarray

    def _rec_inputs():
        import jax
        import jax.numpy as jnp
        _gk = jax.random.key(seed)
        x = -0.0003713 + 1 * jax.random.normal(jax.random.fold_in(_gk, 1), (6250, 256), jnp.float32)
        src = jax.random.randint(jax.random.fold_in(_gk, 2), (200000,), 0, 6250, jnp.int32)
        dst = jnp.minimum((6250 * jax.random.uniform(jax.random.fold_in(_gk, 3), (200000,)) ** 2.0).astype(jnp.int32), 49999)
        _o = jnp.argsort(dst, stable=True)
        src = src[_o]
        dst = dst[_o]
        edge_weight = jax.random.uniform(jax.random.fold_in(_gk, 12), (200000,), jnp.float32, 0.0, 0.999998)
        return (x, src, dst, edge_weight)
    x, src, dst, edge_weight = _rec_inputs()

    def _L0_gnn_setup():
        import jax, jax.numpy as jnp
        import numpy as np
        N_NODES = 6250
        N_EDGES = 37500
        D_IN = 256
        D_OUT = 256
        key = jax.random.key(seed)
        k1, k2, k3, k4 = jax.random.split(key, 4)
        x = jax.random.normal(k1, (N_NODES, D_IN), dtype=jnp.float32)
        edge_index = jax.random.randint(k2, (2, N_EDGES), 0, N_NODES, dtype=jnp.int64)
        edge_weight = jax.random.uniform(k3, (N_EDGES,), dtype=jnp.float32)
        W = jax.random.normal(k4, (D_OUT, D_IN), dtype=jnp.float32) * (1.0 / np.sqrt(D_IN))
        return {'x': x, 'edge_index': edge_index, 'edge_weight': edge_weight, 'W': W}
    _L0_gnn_all = _L0_gnn_setup()
    _L0_gnn_in = {k: v for k, v in _L0_gnn_all.items() if k in ('W',)}
    del _L0_gnn_all

    def _L0_mix_setup():
        import jax, jax.numpy as jnp
        import numpy as np
        D_MODEL = 256
        NUM_HEADS = 8
        DEPTH = D_MODEL // NUM_HEADS
        B, L = (32, 512)

        def _feature_map(x):
            return jax.nn.elu(x) + 1.0
        key = jax.random.key(seed)
        ks = jax.random.split(key, 9)
        sc = 1.0 / np.sqrt(D_MODEL)
        return {'x': jax.random.normal(ks[0], (B, L, D_MODEL), dtype=jnp.float32), 'wq': jax.random.normal(ks[1], (D_MODEL, D_MODEL), dtype=jnp.float32) * sc, 'bq': jnp.zeros((D_MODEL,), dtype=jnp.float32), 'wk': jax.random.normal(ks[2], (D_MODEL, D_MODEL), dtype=jnp.float32) * sc, 'bk': jnp.zeros((D_MODEL,), dtype=jnp.float32), 'wv': jax.random.normal(ks[3], (D_MODEL, D_MODEL), dtype=jnp.float32) * sc, 'bv': jnp.zeros((D_MODEL,), dtype=jnp.float32), 'wo': jax.random.normal(ks[4], (D_MODEL, D_MODEL), dtype=jnp.float32) * sc, 'bo': jnp.zeros((D_MODEL,), dtype=jnp.float32)}
    _L0_mix_all = _L0_mix_setup()
    _L0_mix_in = {k: v for k, v in _L0_mix_all.items() if k in ('wq', 'bq', 'wk', 'bk', 'wv', 'bv', 'wo', 'bo')}
    del _L0_mix_all

    def _L0_ffn_setup():
        import jax, jax.numpy as jnp
        import numpy as np
        NUM_EXPERTS = 8
        TOP_K = 2
        B, S, D = (8, 1024, 256)

        def _moe(tokens, router_w, w1, b1, w2, b2):
            N = tokens.shape[0]
            E = router_w.shape[0]
            logits = tokens.astype(jnp.float32) @ router_w.astype(jnp.float32).T
            probs = jax.nn.softmax(logits, axis=-1)
            rw, re = jax.lax.top_k(probs, TOP_K)
            if TOP_K > 1:
                rw = rw / jnp.maximum(rw.sum(-1, keepdims=True), 1e-12)
            rw = rw.astype(tokens.dtype)
            combine = jnp.zeros((N, E), tokens.dtype).at[jnp.arange(N)[:, None], re].set(rw)
            out = tokens
            for e in range(E):
                h = jax.nn.gelu(tokens @ w1[e] + b1[e], approximate=False)
                y = h @ w2[e] + b2[e]
                out = out + combine[:, e:e + 1] * y
            return out
        key = jax.random.key(seed)
        ks = jax.random.split(key, 4)
        scale = 1.0 / np.sqrt(D).astype(np.float32)
        return {'input_embeddings': jax.random.normal(ks[0], (B, S, D), jnp.float32), 'router_w': jax.random.normal(ks[1], (NUM_EXPERTS, D), jnp.float32) * scale, 'w1': jax.random.normal(ks[2], (NUM_EXPERTS, D, D), jnp.float32) * scale, 'b1': jnp.zeros((NUM_EXPERTS, D), jnp.float32), 'w2': jax.random.normal(ks[3], (NUM_EXPERTS, D, D), jnp.float32) * scale, 'b2': jnp.zeros((NUM_EXPERTS, D), jnp.float32)}
    _L0_ffn_all = _L0_ffn_setup()
    _L0_ffn_in = {k: v for k, v in _L0_ffn_all.items() if k in ('router_w', 'w1', 'b1', 'w2', 'b2')}
    del _L0_ffn_all

    def _L1_gnn_setup():
        import jax, jax.numpy as jnp
        import numpy as np
        N_NODES = 12500
        N_EDGES = 200000
        D = 256
        key = jax.random.key(seed)
        ks = jax.random.split(key, 8)
        h6_all = jax.random.normal(ks[0], (N_NODES, D), dtype=jnp.float32)
        edge_index = jax.random.randint(ks[1], (2, N_EDGES), 0, N_NODES, dtype=jnp.int64)
        edge_weight = jax.random.uniform(ks[2], (N_EDGES,), dtype=jnp.float32)
        s = 1.0 / np.sqrt(D)
        W = jax.random.normal(ks[3], (D, D), dtype=jnp.float32) * s
        b = jnp.zeros((D,), dtype=jnp.float32)
        W1 = jax.random.normal(ks[4], (D, D), dtype=jnp.float32) * s
        b1 = jnp.zeros((D,), dtype=jnp.float32)
        W2 = jax.random.normal(ks[5], (D, D), dtype=jnp.float32) * s
        b2 = jnp.zeros((D,), dtype=jnp.float32)
        return {'h6_all': h6_all, 'edge_index': edge_index, 'edge_weight': edge_weight, 'W': W, 'b': b, 'W1': W1, 'b1': b1, 'W2': W2, 'b2': b2}
    _L1_gnn_all = _L1_gnn_setup()
    _L1_gnn_in = {k: v for k, v in _L1_gnn_all.items() if k in ('W', 'b', 'W1', 'b1', 'W2', 'b2')}
    del _L1_gnn_all

    def _L1_mix_setup():
        import jax, jax.numpy as jnp
        import numpy as np
        DIM = 256
        HEADS = 4
        HEAD_DIM = DIM // HEADS
        MLP_HIDDEN = DIM * 3
        B, N = (8, 512)
        EPS = 1e-05

        def _layernorm(x, g, b):
            mu = jnp.mean(x, axis=-1, keepdims=True)
            var = jnp.mean(jnp.square(x - mu), axis=-1, keepdims=True)
            return (x - mu) * jax.lax.rsqrt(var + EPS) * g + b
        key = jax.random.key(seed)
        ks = jax.random.split(key, 8)
        s = 0.02
        return {'x': jax.random.normal(ks[0], (B, N, DIM), dtype=jnp.float32), 'w_qkv': jax.random.normal(ks[1], (DIM, 3 * DIM), dtype=jnp.float32) * s, 'b_qkv': jnp.zeros((3 * DIM,), dtype=jnp.float32), 'norm_g': jnp.ones((DIM,), dtype=jnp.float32), 'norm_b': jnp.zeros((DIM,), dtype=jnp.float32), 'w_fc1': jax.random.normal(ks[2], (DIM, MLP_HIDDEN), dtype=jnp.float32) * s, 'b_fc1': jnp.zeros((MLP_HIDDEN,), dtype=jnp.float32), 'w_fc2': jax.random.normal(ks[3], (MLP_HIDDEN, DIM), dtype=jnp.float32) * s, 'b_fc2': jnp.zeros((DIM,), dtype=jnp.float32)}
    _L1_mix_all = _L1_mix_setup()
    _L1_mix_in = {k: v for k, v in _L1_mix_all.items() if k in ('w_qkv', 'b_qkv', 'norm_g', 'norm_b', 'w_fc1', 'b_fc1', 'w_fc2', 'b_fc2')}
    del _L1_mix_all

    def _L1_ffn_setup():
        import jax, jax.numpy as jnp
        import numpy as np
        E, D, H, TOP_K = (6, 256, 256, 2)
        ROUTER_H = D // 2
        key = jax.random.key(seed)
        ks = jax.random.split(key, 12)
        s = 1.0 / np.sqrt(D)
        sh = 1.0 / np.sqrt(H)
        sr = 1.0 / np.sqrt(ROUTER_H)
        return {'features': jax.random.normal(ks[0], (8, 512, D), dtype=jnp.float32), 'router_w1': jax.random.uniform(ks[1], (D, ROUTER_H), jnp.float32, -s, s), 'router_b1': jnp.zeros((ROUTER_H,), jnp.float32), 'router_w2': jax.random.uniform(ks[2], (ROUTER_H, E), jnp.float32, -sr, sr), 'router_b2': jnp.zeros((E,), jnp.float32), 'expert_w1': jax.random.uniform(ks[3], (E, D, H), jnp.float32, -s, s), 'expert_b1': jnp.zeros((E, H), jnp.float32), 'expert_w2': jax.random.uniform(ks[4], (E, H, H), jnp.float32, -sh, sh), 'expert_b2': jnp.zeros((E, H), jnp.float32), 'expert_w3': jax.random.uniform(ks[5], (E, H, D), jnp.float32, -sh, sh), 'expert_b3': jnp.zeros((E, D), jnp.float32)}
    _L1_ffn_all = _L1_ffn_setup()
    _L1_ffn_in = {k: v for k, v in _L1_ffn_all.items() if k in ('router_w1', 'router_b1', 'router_w2', 'router_b2', 'expert_w1', 'expert_b1', 'expert_w2', 'expert_b2', 'expert_w3', 'expert_b3')}
    del _L1_ffn_all
    return {'x': x, 'src': src, 'dst': dst, 'edge_weight': edge_weight, 'L0_gnn_W': _L0_gnn_in['W'], 'L0_mix_wq': _L0_mix_in['wq'], 'L0_mix_bq': _L0_mix_in['bq'], 'L0_mix_wk': _L0_mix_in['wk'], 'L0_mix_bk': _L0_mix_in['bk'], 'L0_mix_wv': _L0_mix_in['wv'], 'L0_mix_bv': _L0_mix_in['bv'], 'L0_mix_wo': _L0_mix_in['wo'], 'L0_mix_bo': _L0_mix_in['bo'], 'L0_ffn_router_w': _L0_ffn_in['router_w'], 'L0_ffn_w1': _L0_ffn_in['w1'], 'L0_ffn_b1': _L0_ffn_in['b1'], 'L0_ffn_w2': _L0_ffn_in['w2'], 'L0_ffn_b2': _L0_ffn_in['b2'], 'L1_gnn_W': _L1_gnn_in['W'], 'L1_gnn_b': _L1_gnn_in['b'], 'L1_gnn_W1': _L1_gnn_in['W1'], 'L1_gnn_b1': _L1_gnn_in['b1'], 'L1_gnn_W2': _L1_gnn_in['W2'], 'L1_gnn_b2': _L1_gnn_in['b2'], 'L1_mix_w_qkv': _L1_mix_in['w_qkv'], 'L1_mix_b_qkv': _L1_mix_in['b_qkv'], 'L1_mix_norm_g': _L1_mix_in['norm_g'], 'L1_mix_norm_b': _L1_mix_in['norm_b'], 'L1_mix_w_fc1': _L1_mix_in['w_fc1'], 'L1_mix_b_fc1': _L1_mix_in['b_fc1'], 'L1_mix_w_fc2': _L1_mix_in['w_fc2'], 'L1_mix_b_fc2': _L1_mix_in['b_fc2'], 'L1_ffn_router_w1': _L1_ffn_in['router_w1'], 'L1_ffn_router_b1': _L1_ffn_in['router_b1'], 'L1_ffn_router_w2': _L1_ffn_in['router_w2'], 'L1_ffn_router_b2': _L1_ffn_in['router_b2'], 'L1_ffn_expert_w1': _L1_ffn_in['expert_w1'], 'L1_ffn_expert_b1': _L1_ffn_in['expert_b1'], 'L1_ffn_expert_w2': _L1_ffn_in['expert_w2'], 'L1_ffn_expert_b2': _L1_ffn_in['expert_b2'], 'L1_ffn_expert_w3': _L1_ffn_in['expert_w3'], 'L1_ffn_expert_b3': _L1_ffn_in['expert_b3']}

def reference(x, src, dst, edge_weight, L0_gnn_W, L0_mix_wq, L0_mix_bq, L0_mix_wk, L0_mix_bk, L0_mix_wv, L0_mix_bv, L0_mix_wo, L0_mix_bo, L0_ffn_router_w, L0_ffn_w1, L0_ffn_b1, L0_ffn_w2, L0_ffn_b2, L1_gnn_W, L1_gnn_b, L1_gnn_W1, L1_gnn_b1, L1_gnn_W2, L1_gnn_b2, L1_mix_w_qkv, L1_mix_b_qkv, L1_mix_norm_g, L1_mix_norm_b, L1_mix_w_fc1, L1_mix_b_fc1, L1_mix_w_fc2, L1_mix_b_fc2, L1_ffn_router_w1, L1_ffn_router_b1, L1_ffn_router_w2, L1_ffn_router_b2, L1_ffn_expert_w1, L1_ffn_expert_b1, L1_ffn_expert_w2, L1_ffn_expert_b2, L1_ffn_expert_w3, L1_ffn_expert_b3):
    import jax
    import jax.numpy as jnp

    def _L0_gnn_ref(x, edge_index, edge_weight, W):
        import jax, jax.numpy as jnp
        import numpy as np
        N_NODES = 6250
        N_EDGES = 37500
        D_IN = 256
        D_OUT = 256
        x_proj = jnp.einsum('nd,od->no', x, W)
        dst = edge_index[0]
        src = edge_index[1]
        msgs = edge_weight[:, None] * x_proj[src]
        out = jax.ops.segment_sum(msgs, dst, num_segments=N_NODES)
        return out

    def _L0_mix_ref(x, wq, bq, wk, bk, wv, bv, wo, bo):
        import jax, jax.numpy as jnp
        import numpy as np
        D_MODEL = 256
        NUM_HEADS = 8
        DEPTH = D_MODEL // NUM_HEADS
        B, L = (32, 512)

        def _feature_map(x):
            return jax.nn.elu(x) + 1.0
        b, l, _ = x.shape
        q = (x @ wq + bq).reshape(b, l, NUM_HEADS, DEPTH)
        k = (x @ wk + bk).reshape(b, l, NUM_HEADS, DEPTH)
        v = (x @ wv + bv).reshape(b, l, NUM_HEADS, DEPTH)
        q = _feature_map(q)
        k = _feature_map(k)
        kv = jnp.einsum('blhd,blhe->bhde', k, v)
        k_sum = jnp.sum(k, axis=1)
        qkv = jnp.einsum('blhd,bhde->blhe', q, kv)
        normalizer = jnp.einsum('blhd,bhd->blh', q, k_sum) + 1e-06
        out = qkv / normalizer[..., None]
        out = out.reshape(b, l, D_MODEL)
        return out @ wo + bo

    def _L0_ffn_ref(input_embeddings, router_w, w1, b1, w2, b2):
        import jax, jax.numpy as jnp
        import numpy as np
        NUM_EXPERTS = 8
        TOP_K = 2
        B, S, D = (8, 1024, 256)

        def _moe(tokens, router_w, w1, b1, w2, b2):
            N = tokens.shape[0]
            E = router_w.shape[0]
            logits = tokens.astype(jnp.float32) @ router_w.astype(jnp.float32).T
            probs = jax.nn.softmax(logits, axis=-1)
            rw, re = jax.lax.top_k(probs, TOP_K)
            if TOP_K > 1:
                rw = rw / jnp.maximum(rw.sum(-1, keepdims=True), 1e-12)
            rw = rw.astype(tokens.dtype)
            combine = jnp.zeros((N, E), tokens.dtype).at[jnp.arange(N)[:, None], re].set(rw)
            out = tokens
            for e in range(E):
                h = jax.nn.gelu(tokens @ w1[e] + b1[e], approximate=False)
                y = h @ w2[e] + b2[e]
                out = out + combine[:, e:e + 1] * y
            return out
        b, s, d = input_embeddings.shape
        tokens = input_embeddings.reshape(b * s, d)
        return _moe(tokens, router_w, w1, b1, w2, b2).reshape(b, s, d)

    def _L1_gnn_ref(h6_all, edge_index, edge_weight, W, b, W1, b1, W2, b2):
        import jax, jax.numpy as jnp
        import numpy as np
        N_NODES = 12500
        N_EDGES = 200000
        D = 256
        'GCNConv(256->256, weighted, self-loops, symmetric norm) + 2-layer MLP head.'
        N = h6_all.shape[0]
        row, col = (edge_index[0], edge_index[1])
        sl = jnp.arange(N, dtype=edge_index.dtype)
        row_sl = jnp.concatenate([row, sl])
        col_sl = jnp.concatenate([col, sl])
        ew_sl = jnp.concatenate([edge_weight, jnp.ones((N,), dtype=edge_weight.dtype)])
        deg = jax.ops.segment_sum(ew_sl, row_sl, num_segments=N)
        dinv = jnp.where(deg > 0, jax.lax.rsqrt(deg), 0.0)
        norm = dinv[row_sl] * ew_sl * dinv[col_sl]
        xw = h6_all @ W
        msgs = xw[col_sl] * norm[:, None]
        h7 = jax.ops.segment_sum(msgs, row_sl, num_segments=N) + b
        h = jax.nn.relu(h7 @ W1 + b1)
        out = h @ W2 + b2
        return out

    def _L1_mix_ref(x, w_qkv, b_qkv, norm_g, norm_b, w_fc1, b_fc1, w_fc2, b_fc2):
        import jax, jax.numpy as jnp
        import numpy as np
        DIM = 256
        HEADS = 4
        HEAD_DIM = DIM // HEADS
        MLP_HIDDEN = DIM * 3
        B, N = (8, 512)
        EPS = 1e-05

        def _layernorm(x, g, b):
            mu = jnp.mean(x, axis=-1, keepdims=True)
            var = jnp.mean(jnp.square(x - mu), axis=-1, keepdims=True)
            return (x - mu) * jax.lax.rsqrt(var + EPS) * g + b
        Bx, Nx, C = x.shape
        scale = HEAD_DIM ** (-0.5)
        qkv = (x @ w_qkv + b_qkv).reshape(Bx, Nx, 3, HEADS, HEAD_DIM)
        qkv = jnp.transpose(qkv, (2, 0, 3, 1, 4))
        q, k, v = (qkv[0], qkv[1], qkv[2])
        k = k * scale
        attn = jnp.einsum('bhnd,bhne->bhde', k, v)
        attn = jax.nn.softmax(attn, axis=-1)
        xf = jnp.einsum('bhde,bhne->bhnd', attn, q)
        xf = jnp.transpose(xf, (0, 2, 1, 3)).reshape(Bx, Nx, C)
        x = x + xf
        h = _layernorm(x, norm_g, norm_b)
        h = jax.nn.gelu(h @ w_fc1 + b_fc1, approximate=False) @ w_fc2 + b_fc2
        return x + h

    def _L1_ffn_ref(features, router_w1, router_b1, router_w2, router_b2, expert_w1, expert_b1, expert_w2, expert_b2, expert_w3, expert_b3):
        import jax, jax.numpy as jnp
        import numpy as np
        E, D, H, TOP_K = (6, 256, 256, 2)
        ROUTER_H = D // 2
        rh = jax.nn.relu(features @ router_w1 + router_b1)
        expert_logits = jax.nn.softmax(rh @ router_w2 + router_b2, axis=-1)
        top_w, top_i = jax.lax.top_k(expert_logits, TOP_K)
        routing_weights = jax.nn.softmax(top_w, axis=-1)
        h1 = jax.nn.relu(jnp.einsum('bsd,edh->bseh', features, expert_w1) + expert_b1)
        h2 = jax.nn.relu(jnp.einsum('bseh,ehf->bsef', h1, expert_w2) + expert_b2)
        expert_out = jnp.einsum('bsef,efo->bseo', h2, expert_w3) + expert_b3
        sel = jnp.take_along_axis(expert_out, top_i[:, :, :, None], axis=2)
        combined = jnp.sum(sel * routing_weights[..., None], axis=2)
        return combined
    edge_index = jnp.stack([src, dst])
    xn = _layernorm(x, axis=-1)
    x = x + _L0_gnn_ref(xn, edge_index, edge_weight, L0_gnn_W) + _L0_mix_ref(xn[None], L0_mix_wq, L0_mix_bq, L0_mix_wk, L0_mix_bk, L0_mix_wv, L0_mix_bv, L0_mix_wo, L0_mix_bo)[0]
    x = x + _L0_ffn_ref(_layernorm(x, axis=-1)[None], L0_ffn_router_w, L0_ffn_w1, L0_ffn_b1, L0_ffn_w2, L0_ffn_b2)[0]
    xn = _layernorm(x, axis=-1)
    x = x + _L1_gnn_ref(xn, edge_index, edge_weight, L1_gnn_W, L1_gnn_b, L1_gnn_W1, L1_gnn_b1, L1_gnn_W2, L1_gnn_b2) + _L1_mix_ref(xn[None], L1_mix_w_qkv, L1_mix_b_qkv, L1_mix_norm_g, L1_mix_norm_b, L1_mix_w_fc1, L1_mix_b_fc1, L1_mix_w_fc2, L1_mix_b_fc2)[0]
    x = x + _L1_ffn_ref(_layernorm(x, axis=-1)[None], L1_ffn_router_w1, L1_ffn_router_b1, L1_ffn_router_w2, L1_ffn_router_b2, L1_ffn_expert_w1, L1_ffn_expert_b1, L1_ffn_expert_w2, L1_ffn_expert_b2, L1_ffn_expert_w3, L1_ffn_expert_b3)[0]
    return x

_drawn_inputs = setup_inputs


def setup_inputs(seed=0):
    import zlib

    import numpy as np

    out = dict(_drawn_inputs(seed))
    spreads = {'L0_mix_bq': (0.0, 0.8),
     'L0_mix_bk': (0.0, 0.8),
     'L0_mix_bv': (0.0, 0.1),
     'L0_mix_bo': (0.0, 0.1),
     'L0_ffn_b1': (0.0, 0.672),
     'L0_ffn_b2': (0.0, 0.455),
     'L1_gnn_b': (0.0, 0.587),
     'L1_gnn_b1': (0.0, 0.678),
     'L1_gnn_b2': (0.0, 0.404),
     'L1_mix_b_qkv': (0.0, 0.1),
     'L1_mix_norm_g': (1.0, 0.6),
     'L1_mix_norm_b': (0.0, 0.8),
     'L1_mix_b_fc1': (0.0, 0.8),
     'L1_mix_b_fc2': (0.0, 0.467),
     'L1_ffn_router_b1': (0.0, 0.8),
     'L1_ffn_router_b2': (0.0, 0.8),
     'L1_ffn_expert_b1': (0.0, 0.8),
     'L1_ffn_expert_b2': (0.0, 0.8),
     'L1_ffn_expert_b3': (0.0, 0.632)}
    factors = {'L0_mix_wq': 8.0,
     'L0_mix_wk': 8.0,
     'L0_mix_wv': 7.876,
     'L1_mix_w_fc1': 3.185,
     'L1_mix_w_fc2': 2.986,
     'L1_ffn_router_w1': 3.521,
     'L1_ffn_router_w2': 3.314,
     'L1_ffn_expert_w1': 5.754,
     'L1_ffn_expert_w2': 4.98,
     'L1_ffn_expert_w3': 3.825}
    for name, (base, spread) in spreads.items():
        noise = np.random.default_rng([zlib.crc32(name.encode()), seed]).standard_normal(out[name].shape)
        drawn = base * np.exp(spread * noise) if base else spread * noise
        out[name] = jnp.asarray(drawn.astype(out[name].dtype))
    for name, factor in factors.items():
        out[name] = (out[name] * factor).astype(out[name].dtype)
    return out
```

```python
from contextlib import ExitStack

import numpy as np
import concourse.bass as bass
from concourse import mybir

F32, I32, U32 = mybir.dt.float32, mybir.dt.int32, mybir.dt.uint32
ALU = mybir.AluOpType
ACT = mybir.ActivationFunctionType
AX = mybir.AxisListType

P = 128
N, D, E = 6250, 256, 200000
T = 125
NT = N // T
G = NT // 2
GN = 2 * T
KD = D // P
EC = -(-E // P)
TAIL = E - (P - 1) * EC
HALF = 8
CHUNKS = -(-((P * EC + NT * (P - 1)) // P) // (2 * HALF)) * 2 * HALF
RING = 2 * HALF
BANKS = 4
SC = 16
MAGIC = 1.5 * 2.0 ** 23
EPS = 1e-5
E0, E1 = 8, 6
KC = (P - 1 + CHUNKS) // P


class Chain:

    def __init__(self, engine, sem):
        self.engine, self.sem, self.base, self.n = engine, sem, 0, 0

    def begin(self, index, steps):
        self.start, self.steps = self.base + self.n, steps
        self.base, self.n = index * steps + self.start, 0

    def end(self, trips):
        assert self.n == self.steps, (self.n, self.steps)
        self.base, self.n = self.start + trips * self.steps, 0

    def did(self, instruction):
        instruction.then_inc(self.sem, 1)
        self.n += 1

    def settle(self):
        self.engine.wait_ge(self.sem, self.base + self.n)

    def settle_apart(self):
        self.settle()
        self.apart()

    def apart(self):
        self.engine.memset(self.spare, 0.0)

    def link(self, instruction):
        self.did(instruction)
        self.settle()


def apart(nc, m):
    nc.gpsimd.tensor_tensor(m.pool_spare, m.pool_spare, m.pool_spare, ALU.mult)


def tile_of(view, t, width):
    return view[0:T, bass.ds(t, 1), 0:width].rearrange("p a b -> p (a b)")


class Memory:

    def __init__(self, nc, ctx):
        def sb(name, shape, dt=F32):
            return ctx.enter_context(nc.sbuf_tensor(name, shape, dt))

        self.x = sb("x_res", [P, NT, D + 1])
        self.acc = sb("acc", [P, NT, D])
        self.flat = self.acc[:, :, :].rearrange("p a b -> p (a b)")
        self.dst = sb("sorted_dst", [P, CHUNKS], I32)
        self.lew = sb("sorted_local_weight", [P, CHUNKS + HALF, 2])
        self.blk = sb("chunk_tile", [1, KC * P], I32)
        self.rows = sb("rows", [P, RING, D + 1])
        self.hot = sb("hot", [P, RING, T])
        self.idx = sb("idx_stage", [P, 2, HALF], I32)
        self.w = sb("weights", [P, 12, KD, D])
        self.ident = sb("ident", [P, P])
        self.iota = sb("iota_free", [P, P])
        self.iota_i = sb("iota_int", [P, P], I32)
        self.row_bias = sb("row_bias", [P, 7, D])
        self.col_bias = sb("col_bias", [P, 48])
        self.mean = sb("mean", [P, NT])
        self.rstd = sb("rstd", [P, NT])
        self.dinv = sb("dinv", [P, NT])
        self.stats = sb("stats", [P, 2, 6])
        self.mv = sb("mean_var", [P, 2, 2])
        self.work = sb("work", [P, 22, D])
        self.small = sb("small", [P, 256])
        self.chain = Chain(nc.vector, ctx.enter_context(nc.semaphore("vector_done")))
        self.pool_spare = sb("pool_spare", [1, 1])[0:1, 0:1]
        self.chain.spare = sb("spare", [1, 1])[0:1, 0:1]
        self.row_in = [ctx.enter_context(nc.semaphore(f"row_in_{s}")) for s in range(RING)]
        self.ps = ctx.enter_context(nc.psum_tensor("ps", [P, 8, 512], F32))
        self.table = [nc.dram_tensor(f"table{n}", (N, D), F32, kind="Internal").ap() for n in range(2)]
        self.sorted = nc.dram_tensor("sorted_edges", (P * CHUNKS, 2), F32, kind="Internal").ap()
        self.chunk_dram = nc.dram_tensor("chunk_tile_dram", (P * KC,), I32, kind="Internal").ap()


COL = {"bq": 0, "gnn_b": 2, "gnn_b1": 4, "bq1": 6, "norm_g": 8, "norm_b": 10, "fc1": 12,
       "router_b1": 18, "expert": 20}
ROW = {"bk": 0, "bv": 1, "bo": 2, "bk1": 3, "bv1": 4, "fc2": 5, "gnn_b2": 6}


def rank_edges(nc, m, sem, a):
    ec = [m.flat[:, n * EC:(n + 1) * EC] for n in range(8)]
    src_i, dst_i, ew, blk, loc, mask, scan, pos = ec
    src_i, dst_i = src_i.bitcast(I32), dst_i.bitcast(I32)
    rec = m.flat[:, 5 * EC:7 * EC].rearrange("p (e f) -> p e f", f=2)
    small = m.small
    cnt, base, start, tri = small[:, 0:NT], small[:, NT:2 * NT], small[:, 2 * NT:3 * NT], m.rows[:, 0, 0:P]
    chunks, incl = small[:, 3 * NT:4 * NT], small[:, 4 * NT:5 * NT]
    ones = m.rows[:, 1, 0:P]
    zeros = m.lew[:, :, :].rearrange("p a b -> p (a b)")
    flag = m.rows[:, 2:5, :].rearrange("p a b -> p (a b)")[:, 0:KC * NT].rearrange("p (j b) -> p j b", j=KC)
    of = m.hot[:, 0, 0:KC]
    of_i = m.hot[:, 1, 0:KC].bitcast(I32)
    at = m.hot[:, 2, 0:KC]
    pads_set, edges_in, zeroed, sorted_zero = sem("pads_set"), sem("edges_in"), sem("zero_set"), sem("sorted_zeroed")
    made, counted, summed, of_ready, of_out, of_in, x_in = (
        sem("constants_made"), sem("counted"), sem("summed"), sem("tile_of_chunk"), sem("chunk_tile_out"),
        sem("chunk_tile_in"), sem("x_in"))
    x_dram = a["x"].rearrange("(t p) d -> p t d", p=T)
    with nc.Block() as block:

        @block.sync
        def _(sp):
            sp.wait_ge(pads_set, 3)
            for src, to in ((a["src"], src_i), (a["dst"], dst_i), (a["edge_weight"], ew)):
                for lo, hi in ((0, 112), (112, P - 1)):
                    sp.dma_start(to[lo:hi, :], src[lo * EC:hi * EC].rearrange("(p c) -> p c", c=EC)).then_inc(edges_in, 16)
                sp.dma_start(to[P - 1:P, 0:TAIL], src[(P - 1) * EC:E].rearrange("(p c) -> p c", c=TAIL)).then_inc(edges_in, 16)
            sp.wait_ge(zeroed, 1)
            sp.dma_start(m.sorted.rearrange("(p c) f -> p (c f)", p=P), zeros[:, 0:2 * CHUNKS]).then_inc(sorted_zero, 16)
            for c in range(5):
                sp.dma_start(m.x[0:T, 10 * c:10 * c + 10, 0:D], x_dram[:, 10 * c:10 * c + 10, :]).then_inc(x_in, 16)
            for n, name in enumerate(("L0_gnn_W", "L0_mix_wk", "L0_mix_wv", "L0_mix_wq", "L0_mix_wo")):
                sp.dma_start(m.w[:, n, :, :], a[name].rearrange("(k p) n -> p k n", p=P)).then_inc(x_in, 16)
            for name, src in (("bk", a["L0_mix_bk"]), ("bv", a["L0_mix_bv"]), ("bo", a["L0_mix_bo"]),
                              ("bk1", a["L1_mix_b_qkv"][D:2 * D]), ("bv1", a["L1_mix_b_qkv"][2 * D:3 * D]),
                              ("fc2", a["L1_mix_b_fc2"]), ("gnn_b2", a["L1_gnn_b2"])):
                sp.dma_start(m.row_bias[:, ROW[name], :], src.rearrange("(a d) -> a d", a=1).to_broadcast([P, D])).then_inc(x_in, 16)
            for name, src, n in (("bq", a["L0_mix_bq"], 2), ("gnn_b", a["L1_gnn_b"], 2), ("gnn_b1", a["L1_gnn_b1"], 2),
                                 ("bq1", a["L1_mix_b_qkv"][0:D], 2), ("norm_g", a["L1_mix_norm_g"], 2),
                                 ("norm_b", a["L1_mix_norm_b"], 2), ("fc1", a["L1_mix_b_fc1"], 6),
                                 ("router_b1", a["L1_ffn_router_b1"], 1)):
                with nc.allow_non_contiguous_dma(reason="a bias, one channel in each partition"):
                    sp.dma_start(m.col_bias[:, COL[name]:COL[name] + n], src.rearrange("(h p) -> p h", p=P)).then_inc(x_in, 16)
            sp.wait_ge(of_ready, 1)
            sp.dma_start(m.chunk_dram.rearrange("(p j) -> p j", p=P), of_i).then_inc(of_out, 16)
            sp.wait_ge(of_out, 16)
            sp.dma_start(m.blk[:, :], m.chunk_dram.rearrange("(a c) -> a c", a=1)).then_inc(of_in, 16)
            sp.wait_ge(of_in, 16)
            sp.wait_ge(x_in, 16 * (5 + 5 + 7 + 8))
            sp.wait_ge(sorted_zero, 16)

        @block.gpsimd
        def _(pool):
            nc.gpsimd.iota(m.iota_i[:, :], [[1, P]], base=0, channel_multiplier=0).then_inc(made, 1)
            nc.gpsimd.memset(m.ident[:, :], 0.0).then_inc(made, 1)
            nc.gpsimd.memset(ones, 1.0).then_inc(made, 1)
            nc.gpsimd.memset(m.pool_spare, 0.0)
            nc.gpsimd.memset(m.x[:, :, D:D + 1], 0.0).then_inc(made, 1)
            nc.gpsimd.iota(of_i, [[1, KC]], base=0, channel_multiplier=KC).then_inc(made, 1)
            pool.wait_ge(made, 5)
            nc.gpsimd.tensor_copy(m.iota[:, :], m.iota_i[:, :]).then_inc(made, 1)
            nc.gpsimd.tensor_copy(at, of_i).then_inc(made, 1)
            nc.gpsimd.affine_select(out=m.ident[:, :], in_=m.ident[:, :], compare_op=ALU.not_equal, fill=1.0,
                                    base=0, pattern=[[-1, P]], channel_multiplier=1).then_inc(made, 1)
            nc.gpsimd.affine_select(out=tri, in_=ones, compare_op=ALU.is_ge, fill=0.0,
                                    base=-1, pattern=[[1, P]], channel_multiplier=-1).then_inc(made, 1)
            nc.gpsimd.memset(zeros, 0.0).then_inc(zeroed, 1)

        @block.vector
        def _(dve):
            chain = m.chain
            nc.vector.memset(src_i[:, TAIL:EC], N - 1).then_inc(pads_set, 1)
            nc.vector.memset(dst_i[:, TAIL:EC], 0).then_inc(pads_set, 1)
            nc.vector.memset(ew[:, TAIL:EC], 0.0).then_inc(pads_set, 1)
            dve.wait_ge(made, 9)
            dve.wait_ge(edges_in, 16 * 9)
            chain.link(nc.vector.tensor_copy(mask, src_i))
            chain.link(nc.vector.tensor_scalar(blk, mask, 1.0 / T, 0.5 / T - 0.5, ALU.mult, ALU.add))
            chain.link(nc.vector.tensor_scalar(blk, blk, MAGIC, None, ALU.add))
            chain.link(nc.vector.tensor_scalar(blk, blk, -MAGIC, None, ALU.add))
            chain.link(nc.vector.scalar_tensor_tensor(loc, blk, -float(T), mask, ALU.mult, ALU.add))
            with dve.Fori(0, NT) as b:
                chain.begin(b, 1)
                chain.link(nc.vector.tensor_scalar(mask, blk, m.iota[:, bass.ds(b, 1)], None, ALU.is_equal, ALU.add,
                                                   accum_out=cnt[:, bass.ds(b, 1)]))
                chain.end(NT)
            nc.vector.memset(small[:, 5 * NT:5 * NT + 1], 0.0).then_inc(counted, 1)
            dve.wait_ge(summed, 1)
            chain.link(nc.vector.tensor_scalar(chunks, m.ps[:, 1, 0:NT], 1.0 / P, (P - 1.0) / P - 0.5 + 0.5 / P, ALU.mult, ALU.add))
            chain.link(nc.vector.tensor_scalar(chunks, chunks, MAGIC, None, ALU.add))
            chain.link(nc.vector.tensor_scalar(chunks, chunks, -MAGIC, None, ALU.add))
            chain.link(nc.vector.tensor_tensor_scan(incl, chunks, chunks, 0.0, ALU.add, ALU.bypass))
            chain.link(nc.vector.tensor_tensor(start, incl, chunks, ALU.subtract))
            chain.link(nc.vector.scalar_tensor_tensor(base, start, float(P), m.ps[:, 0, 0:NT], ALU.mult, ALU.add))
            chain.link(nc.vector.tensor_scalar(base, base, -1.0, None, ALU.add))
            chain.link(nc.vector.tensor_tensor(flag, start.unsqueeze(1).to_broadcast([P, KC, NT]),
                                               at.unsqueeze(2).to_broadcast([P, KC, NT]), ALU.is_le))
            chain.link(nc.vector.tensor_reduce(of, flag, AX.X, ALU.add))
            chain.link(nc.vector.tensor_scalar(of, of, -1.0, None, ALU.add))
            nc.vector.tensor_copy(of_i, of).then_inc(of_ready, 1)
            with dve.Fori(0, NT) as b:
                chain.begin(b, 3)
                chain.link(nc.vector.tensor_scalar(mask, blk, m.iota[:, bass.ds(b, 1)], None, ALU.is_equal))
                chain.link(nc.vector.tensor_tensor_scan(scan, mask, mask, base[:, bass.ds(b, 1)], ALU.add, ALU.bypass))
                chain.apart()
                chain.link(nc.vector.copy_predicated(pos, mask.bitcast(U32), scan))
                chain.end(NT)
            low, high = mask.bitcast(I32), scan.bitcast(I32)
            chain.link(nc.vector.tensor_copy(src_i, pos))
            chain.link(nc.vector.tensor_scalar(high, src_i, 7, None, ALU.arith_shift_right))
            chain.link(nc.vector.tensor_scalar(low, src_i, P - 1, None, ALU.bitwise_and))
            chain.link(nc.vector.scalar_tensor_tensor(src_i, low, float(CHUNKS), high, ALU.mult, ALU.add))
            chain.link(nc.vector.tensor_copy(pos, dst_i))
            chain.link(nc.vector.scalar_tensor_tensor(rec[:, :, 0], pos, float(P), loc, ALU.mult, ALU.add))
            chain.link(nc.vector.tensor_copy(rec[:, :, 1], ew))

        @block.tensor
        def _(pe):
            pe.wait_ge(made, 9)
            pe.wait_ge(counted, 1)
            nc.tensor.matmul(m.ps[:, 0, 0:NT], tri, cnt, start=True, stop=True)
            nc.tensor.matmul(m.ps[:, 1, 0:NT], ones, cnt, start=True, stop=True).then_inc(summed, 1)


def norm_stats(nc, dve, chain, m):
    var = m.small[:, 0:NT]
    with dve.Fori(0, G) as g:
        chain.begin(g, 6)
        for k in range(2):
            chain.did(nc.vector.bn_stats(m.stats[0:T, k, :], tile_of(m.x, g * 2 + k, D)))
        chain.settle_apart()
        for k in range(2):
            chain.did(nc.vector.bn_aggr(m.mv[0:T, k, :], m.stats[0:T, k, :]))
        chain.settle()
        chain.did(nc.vector.tensor_copy(m.mean[0:T, bass.ds(g * 2, 2)], m.mv[0:T, :, 0]))
        chain.did(nc.vector.tensor_copy(var[0:T, bass.ds(g * 2, 2)], m.mv[0:T, :, 1]))
        chain.settle()
        chain.end(G)
    inverse_root(nc, chain, m.rstd[0:T, :], var[0:T, :], EPS, m.small[0:T, 64:64 + NT], m.small[0:T, 128:128 + NT])


def inverse_root(nc, chain, out, value, add, half, guess):
    chain.link(nc.vector.tensor_scalar(half, value, add, None, ALU.add))
    chain.link(nc.vector.tensor_scalar(guess.bitcast(I32), half.bitcast(I32), 1, None, ALU.arith_shift_right))
    chain.link(nc.vector.tensor_scalar(out.bitcast(I32), guess.bitcast(I32), -1.0, float(0x5F3759DF), ALU.mult, ALU.add))
    chain.link(nc.vector.tensor_scalar(half, half, -0.5, None, ALU.mult))
    for _ in range(4):
        chain.link(nc.vector.tensor_tensor(guess, out, out, ALU.mult))
        chain.link(nc.vector.tensor_tensor(guess, guess, half, ALU.mult))
        chain.link(nc.vector.scalar_tensor_tensor(out, guess, 1.5, out, ALU.add, ALU.mult))


def normalise(nc, m, out, g, k):
    t = g * 2 + k
    return nc.vector.tensor_scalar(out, tile_of(m.x, t, D), m.mean[0:T, bass.ds(t, 1)], m.rstd[0:T, bass.ds(t, 1)],
                                   ALU.subtract, ALU.mult)


def transpose_group(nc, m, bank, tiles):
    for h in range(KD):
        for k in range(2):
            last = nc.tensor.transpose(m.ps[:, bank, h * GN + k * T:h * GN + (k + 1) * T],
                                       tiles[0:T, k, h * P:(h + 1) * P], m.ident[0:T, 0:T])
    return last


def rows_times(nc, out, xT, w, start=True, stop=True):
    for h in range(KD):
        last = nc.tensor.matmul(out, xT(h), w(h), start=start and h == 0, stop=stop and h == KD - 1)
    return last


def scatter_and_mix0(nc, m, sem):
    ec = [m.flat[:, n * EC:(n + 1) * EC] for n in range(8)]
    addr = ec[0].bitcast(I32)
    rec = m.flat[:, 5 * EC:7 * EC]
    W = m.work
    xn, xT = W[:, 0:2, :], W[:, 2:4, 0:GN]
    table_sb, kb, ke, kf = W[:, 4:6, :], W[:, 6:8, :], W[:, 8:10, :], W[:, 10:12, :]
    v = W[:, 12:15, :].rearrange("p a b -> p (a b)")[:, 0:2 * 258].rearrange("p (k c) -> p k c", k=2)
    kvd = W[:, 15, :].rearrange("p (h e) -> p h e", h=2)
    ksd = W[:, 16, :].rearrange("p (h e) -> p h e", h=2)
    same = W[:, 17, 0:P]
    st_addr = W[:, 18, 0:2 * SC].bitcast(I32).rearrange("p (h c) -> p h c", h=2)
    st_rec = W[:, 19, 0:4 * SC].rearrange("p (h c f) -> p h c f", h=2, f=2)
    qe, qf, oT = W[:, 6:8, 0:GN], W[:, 8:10, 0:GN], W[:, 10:12, 0:GN]
    qm, rn = W[:, 4:6, 0:GN], W[:, 12:14, 0:GN]
    ps = m.ps
    staged, scattered = sem("scatter_staged"), [sem(f"scattered{h}") for h in range(2)]
    set_up = sem("set_up0")
    xn_ready, tp_done, xT_ready = sem("xn0"), sem("xn0_transposed"), sem("xT0")
    proj, km_ready, ke_ready, kf_ready, v_ready, kv_done = (
        sem("table_k_v"), sem("k_min"), sem("k_exp"), sem("kf"), sem("v_ready"), sem("kv_summed"))
    table_ready, table_out = sem("table0_ready"), sem("table0_out")
    kvd_ready, qxn, qtp, qxT, q_done, qm_ready, qe_ready, qf_ready, o_done, oT_ready, y_done, y_added = (
        sem("kv_diag"), sem("q_xn"), sem("q_transposed"), sem("q_xT"), sem("q_done"), sem("q_min"), sem("q_exp"),
        sem("qf"), sem("o_done"), sem("oT"), sem("y_done"), sem("y_added"))
    bq = [m.col_bias[:, COL["bq"] + h:COL["bq"] + h + 1] for h in range(2)]

    def scatter(pool, first, h, count, stage_count):
        nc.gpsimd.tensor_copy(st_addr[:, h, 0:count], addr[:, bass.ds(first, count)]).then_inc(staged, 1)
        nc.gpsimd.tensor_copy(st_rec[:, h, 0:count, :].rearrange("p c f -> p (c f)"),
                              rec[:, bass.ds(first * 2, 2 * count)]).then_inc(staged, 1)
        pool.wait_ge(staged, stage_count)
        apart(nc, m)
        for j in range(count):
            nc.gpsimd.indirect_dma_start(
                out=m.sorted, out_offset=bass.IndirectOffsetOnAxis(ap=st_addr[:, h, j:j + 1], axis=0),
                in_=st_rec[:, h, j, :], in_offset=None).then_inc(scattered[h], 16)

    with nc.Block() as block:

        @block.gpsimd
        def _(pool):
            trips = EC // (2 * SC)
            with pool.Fori(0, trips) as i:
                for h in range(2):
                    pool.wait_ge(scattered[h], i * (16 * SC))
                    scatter(pool, i * (2 * SC) + h * SC, h, SC, i * 4 + 2 * (h + 1))
            left = EC - trips * 2 * SC
            for h in range(2):
                count = min(SC, left - h * SC)
                if count > 0:
                    pool.wait_ge(scattered[h], trips * 16 * SC)
                    scatter(pool, trips * 2 * SC + h * SC, h, count, trips * 4 + 2 * (h + 1))
            pool.wait_ge(scattered[0], 16 * (trips * SC + min(SC, left)))
            pool.wait_ge(scattered[1], 16 * (trips * SC + max(0, left - SC)))

        @block.sync
        def _(sp):
            to = m.table[0].rearrange("(t p) d -> p t d", p=T)
            with sp.Fori(0, G) as g:
                sp.wait_ge(table_ready, g + 1)
                sp.dma_start(to[:, bass.ds(g * 2, 2), :], table_sb[0:T, :, :]).then_inc(table_out, 16)
            sp.wait_ge(table_out, 16 * G)

        @block.vector
        def _(dve):
            chain = m.chain
            chain.did(nc.vector.memset(same, 0.0))
            for k in range(2):
                for h in range(2):
                    chain.did(nc.vector.memset(v[:, k, 129 * h + P:129 * h + P + 1], 1.0))
            chain.settle()
            for b in range(4):
                chain.did(nc.vector.memset(same[32 * b:32 * b + 32, 32 * b:32 * b + 32], 1.0))
            chain.did(nc.vector.memset(table_sb[:, 0, :], 0.0))
            chain.settle()
            nc.vector.memset(table_sb[:, 1, :], 0.0).then_inc(set_up, 1)
            norm_stats(nc, dve, chain, m)
            with dve.Fori(0, G) as g:
                chain.begin(g, 1)
                dve.wait_ge(tp_done, g)
                for k in range(2):
                    normalise(nc, m, xn[0:T, k, :], g, k).then_inc(xn_ready, 1)
                dve.wait_ge(proj, g * 3 + 2)
                dve.wait_ge(kv_done, g)
                chain.link(nc.vector.tensor_tensor(kb[0:T, :, :], ps[0:T, 2, :].rearrange("p (k d) -> p k d", k=2),
                                                   m.row_bias[0:T, ROW["bk"], :].unsqueeze(1).to_broadcast([T, 2, D]), ALU.add))
                nc.vector.tensor_scalar(kf[0:T, :, :], kb[0:T, :, :], 0.0, None, ALU.min).then_inc(km_ready, 1)
                dve.wait_ge(proj, g * 3 + 3)
                for h in range(2):
                    nc.vector.tensor_tensor(v[0:T, :, 129 * h:129 * h + P],
                                            ps[0:T, 3, :].rearrange("p (k d) -> p k d", k=2)[:, :, h * P:(h + 1) * P],
                                            m.row_bias[0:T, ROW["bv"], h * P:(h + 1) * P].unsqueeze(1).to_broadcast([T, 2, P]),
                                            ALU.add).then_inc(v_ready, 1)
                dve.wait_ge(ke_ready, g + 1)
                nc.vector.scalar_tensor_tensor(kf[0:T, :, :], kb[0:T, :, :], 0.0, ke[0:T, :, :], ALU.max, ALU.add).then_inc(kf_ready, 1)
                chain.end(G)
            dve.wait_ge(kv_done, G)
            for h in range(2):
                nc.vector.tensor_tensor(kvd[:, h, :], ps[:, 4, 129 * h:129 * h + P], same, ALU.mult).then_inc(kvd_ready, 1)
                nc.vector.tensor_scalar(ksd[:, h, :], same, ps[:, 4, 129 * h + P:129 * h + P + 1], None, ALU.mult).then_inc(kvd_ready, 1)
            with dve.Fori(0, G) as g:
                chain.begin(g, 5)
                dve.wait_ge(qtp, g)
                for k in range(2):
                    normalise(nc, m, xn[0:T, k, :], g, k).then_inc(qxn, 1)
                dve.wait_ge(q_done, g + 1)
                for h in range(2):
                    nc.vector.tensor_scalar(qm[:, h, :], ps[:, 2, h * GN:(h + 1) * GN], bq[h], 0.0, ALU.add, ALU.min).then_inc(qm_ready, 1)
                dve.wait_ge(o_done, g)
                for h in range(2):
                    chain.did(nc.vector.tensor_scalar(qf[:, h, :], ps[:, 2, h * GN:(h + 1) * GN], bq[h], 0.0, ALU.add, ALU.max))
                chain.settle()
                dve.wait_ge(qe_ready, g + 1)
                nc.vector.tensor_tensor(qf, qf, qe, ALU.add).then_inc(qf_ready, 1)
                dve.wait_ge(o_done, g + 1)
                chain.link(nc.vector.tensor_scalar(rn, ps[:, 6, 0:2 * GN].rearrange("p (h c) -> p h c", h=2), 1e-6, None, ALU.add))
                chain.link(nc.vector.reciprocal(rn, rn))
                dve.wait_ge(y_done, g)
                nc.vector.tensor_tensor(oT, ps[:, 5, 0:2 * GN].rearrange("p (h c) -> p h c", h=2), rn, ALU.mult).then_inc(oT_ready, 1)
                xg = m.x[0:T, bass.ds(g * 2, 2), 0:D]
                dve.wait_ge(y_done, g + 1)
                chain.link(nc.vector.tensor_tensor(xg, xg, ps[0:T, 7, :].rearrange("p (k d) -> p k d", k=2), ALU.add))
                nc.vector.tensor_tensor(xg, xg, m.row_bias[0:T, ROW["bo"], :].unsqueeze(1).to_broadcast([T, 2, D]), ALU.add).then_inc(y_added, 1)
                chain.end(G)

        @block.scalar
        def _(act):
            with act.Fori(0, G) as g:
                act.wait_ge(tp_done, g + 1)
                act.wait_ge(proj, g * 3)
                nc.scalar.copy(xT, ps[:, 0, 0:2 * GN].rearrange("p (h c) -> p h c", h=2)).then_inc(xT_ready, 1)
                act.wait_ge(proj, g * 3 + 1)
                act.wait_ge(table_out, g * 16)
                nc.scalar.copy(table_sb[0:T, :, :], ps[0:T, 1, :].rearrange("p (k d) -> p k d", k=2)).then_inc(table_ready, 1)
                act.wait_ge(km_ready, g + 1)
                nc.scalar.activation(ke[0:T, :, :], kf[0:T, :, :], ACT.Exp).then_inc(ke_ready, 1)
            act.wait_ge(table_out, 16 * G)
            with act.Fori(0, G) as g:
                act.wait_ge(qtp, g + 1)
                act.wait_ge(q_done, g)
                nc.scalar.copy(xT, ps[:, 0, 0:2 * GN].rearrange("p (h c) -> p h c", h=2)).then_inc(qxT, 1)
                act.wait_ge(qm_ready, g * 2 + 2)
                nc.scalar.activation(qe, qm, ACT.Exp).then_inc(qe_ready, 1)

        @block.tensor
        def _(pe):
            pe.wait_ge(set_up, 1)
            nc.tensor.matmul(ps[:, 4, 0:258], table_sb[:, 0, 0:P], table_sb[:, :, :].rearrange("p a b -> p (a b)")[:, 0:258],
                             start=True, stop=False, skip_group_check=True)
            with pe.Fori(0, G) as g:
                pe.wait_ge(xn_ready, g * 2 + 2)
                pe.wait_ge(xT_ready, g)
                transpose_group(nc, m, 0, xn).then_inc(tp_done, 1)
                pe.wait_ge(xT_ready, g + 1)
                pe.wait_ge(table_ready, g)
                for n in range(3):
                    if n == 1:
                        pe.wait_ge(km_ready, g)
                    if n == 2:
                        pe.wait_ge(v_ready, 2 * g)
                    for k in range(2):
                        last = rows_times(nc, ps[0:T, 1 + n, k * D:(k + 1) * D], lambda h: xT[:, h, k * T:(k + 1) * T],
                                          lambda h: m.w[:, n, h, :])
                    last.then_inc(proj, 1)
                pe.wait_ge(kf_ready, g + 1)
                pe.wait_ge(v_ready, 2 * g + 2)
                for k in range(2):
                    for h in range(2):
                        last = nc.tensor.matmul(ps[:, 4, 129 * h:129 * h + 129], kf[0:T, k, h * P:(h + 1) * P],
                                                v[0:T, k, 129 * h:129 * h + 129], start=False, stop=False, skip_group_check=True)
                last.then_inc(kv_done, 1)
            pe.wait_ge(kvd_ready, 4)
            with pe.Fori(0, G) as g:
                pe.wait_ge(qxn, g * 2 + 2)
                pe.wait_ge(qxT, g)
                transpose_group(nc, m, 0, xn).then_inc(qtp, 1)
                pe.wait_ge(qxT, g + 1)
                pe.wait_ge(qf_ready, g)
                for o in range(2):
                    for h in range(2):
                        last = nc.tensor.matmul(ps[:, 2, o * GN:(o + 1) * GN], m.w[:, 3, h, o * P:(o + 1) * P], xT[:, h, :],
                                                start=h == 0, stop=h == 1)
                last.then_inc(q_done, 1)
                pe.wait_ge(qf_ready, g + 1)
                pe.wait_ge(oT_ready, g)
                for bank, mat in ((5, kvd), (6, ksd)):
                    for h in range(2):
                        last = nc.tensor.matmul(ps[:, bank, h * GN:(h + 1) * GN], mat[:, h, :], qf[:, h, :], start=True, stop=True)
                last.then_inc(o_done, 1)
                pe.wait_ge(oT_ready, g + 1)
                pe.wait_ge(y_added, g)
                for k in range(2):
                    last = rows_times(nc, ps[0:T, 7, k * D:(k + 1) * D], lambda h: oT[:, h, k * T:(k + 1) * T],
                                      lambda h: m.w[:, 4, h, :])
                last.then_inc(y_done, 1)


def gather_sums(nc, m, sem, layer):
    width = D + 1 if layer == 0 else D
    into = m.x if layer == 0 else m.acc
    raw = m.flat[:, 0:2 * CHUNKS]
    raw_v = raw.rearrange("p (c f) -> p c f", f=2)
    vi = m.flat[:, 2 * CHUNKS:3 * CHUNKS].bitcast(I32)
    lo = m.flat[:, 3 * CHUNKS:4 * CHUNKS].bitcast(I32)
    loaded, decoded, ones_set, idx_in = sem(f"edges_loaded{layer}"), sem(f"decoded{layer}"), sem(f"ones_set{layer}"), sem(f"idx{layer}")
    row_in, before = m.row_in, 16 * (CHUNKS // RING) * layer
    hot_ready, summed, bank_free = sem(f"hot{layer}"), sem(f"chunk_sum{layer}"), sem(f"bank_free{layer}")
    trips = CHUNKS // RING
    with nc.Block() as block:

        if layer == 0:
            @block.sync
            def _(sp):
                sp.dma_start(raw, m.sorted.rearrange("(p c) f -> p (c f)", p=P)).then_inc(loaded, 16)
                sp.wait_ge(loaded, 16)

        @block.gpsimd
        def _(pool):
            nc.gpsimd.memset(m.rows[:, :, D:D + 1], 1.0).then_inc(ones_set, 1)
            pool.wait_ge(decoded, 1)

            def fetch(i, h, used):
                pool.wait_ge(summed, used)
                nc.gpsimd.tensor_copy(m.idx[:, h % 2, :], m.dst[:, bass.ds(i * RING + h * HALF, HALF)]).then_inc(idx_in, 1)
                pool.wait_ge(idx_in, i * 2 + h + 1)
                apart(nc, m)
                for j in range(HALF):
                    s = (h % 2) * HALF + j
                    nc.gpsimd.indirect_dma_start(
                        out=m.rows[:, s, 0:D], out_offset=None, in_=m.table[layer],
                        in_offset=bass.IndirectOffsetOnAxis(ap=m.idx[:, h % 2, j:j + 1], axis=0)).then_inc(row_in[s], 16)

            fetch(0, 0, 0)
            with pool.Fori(0, trips - 1) as i:
                fetch(i, 1, i * RING)
                fetch(i, 2, i * RING + HALF)
            fetch(trips - 1, 1, (trips - 1) * RING)
            for s in range(RING):
                pool.wait_ge(row_in[s], 16 * trips + before)

        @block.vector
        def _(dve):
            chain = m.chain
            if layer == 0:
                dve.wait_ge(loaded, 16)
                chain.did(nc.vector.memset(m.lew[:, CHUNKS:CHUNKS + HALF, :], 0.0))
                chain.link(nc.vector.tensor_copy(vi, raw_v[:, :, 0]))
                chain.did(nc.vector.tensor_scalar(lo, vi, P - 1, None, ALU.bitwise_and))
                chain.did(nc.vector.tensor_scalar(m.dst[:, :], vi, 7, None, ALU.arith_shift_right))
                chain.settle()
                chain.did(nc.vector.tensor_copy(m.lew[:, 0:CHUNKS, 0], lo))
                chain.did(nc.vector.tensor_copy(m.lew[:, 0:CHUNKS, 1], raw_v[:, :, 1]))
                chain.settle()
            for b in range(BANKS):
                nc.vector.memset(m.small[0:1, b:b + 1], 0.0).then_inc(bank_free, 1)
            nc.vector.memset(m.small[0:1, BANKS:BANKS + 1], 0.0).then_inc(decoded, 1)

            def build(i, h, used):
                dve.wait_ge(summed, used)
                for j in range(HALF):
                    c = i * RING + h * HALF + j
                    nc.vector.tensor_scalar(m.hot[:, (h % 2) * HALF + j, :], m.iota[:, 0:T],
                                            m.lew[:, bass.ds(c, 1), 0], m.lew[:, bass.ds(c, 1), 1],
                                            ALU.is_equal, ALU.mult).then_inc(hot_ready, 1)

            def add(i, h, regs):
                nc.vector.reg_load(regs, m.blk[0:1, bass.ds(i * RING + h * HALF, HALF)])
                for j in range(HALF):
                    t = nc.vector.snap(regs[j], min_val=0, max_val=NT - 1)
                    c = i * RING + (h * HALF + j)
                    dve.wait_ge(summed, c + 1)
                    dve.wait_ge(bank_free, c + BANKS)
                    to = tile_of(into, t, width)
                    nc.vector.tensor_tensor(to, to, m.ps[0:T, j % BANKS, 0:width], ALU.add).then_inc(bank_free, 1)

            regs = [nc.vector.alloc_register(f"tile{layer}_{j}") for j in range(HALF)]
            build(0, 0, 0)
            with dve.Fori(0, trips) as i:
                build(i, 1, i * RING)
                add(i, 0, regs)
                build(i, 2, i * RING + HALF)
                add(i, 1, regs)
            for r in regs:
                nc.vector.free_register(r)

        @block.tensor
        def _(pe):
            pe.wait_ge(ones_set, 1)
            with pe.Fori(0, trips) as i:
                for s in range(RING):
                    c = i * RING + s
                    pe.wait_ge(row_in[s], i * 16 + 16 + before)
                    pe.wait_ge(hot_ready, c + 1)
                    pe.wait_ge(bank_free, c + 1)
                    nc.tensor.matmul(m.ps[0:T, s % BANKS, 0:width], m.hot[:, s, :], m.rows[:, s, 0:width],
                                     start=True, stop=True).then_inc(summed, 1)


def table1(nc, m, sem, a):
    tiles_ready, stored, loaded = sem("table1_tiles"), sem("table1_stored"), sem("weights1_in")
    deg, pos, ry = m.small[0:T, 192:192 + NT], m.work[0:T, 0, 0:NT], m.work[0:T, 1, 0:NT]
    h, q = m.work[0:T, 2, 0:NT], m.work[0:T, 3, 0:NT]
    to = m.table[1].rearrange("(t p) d -> p t d", p=T)
    with nc.Block() as block:

        @block.sync
        def _(sp):
            parts = [(n, a[w]) for n, w in enumerate(("L1_gnn_W", "L1_gnn_W1", "L1_gnn_W2"))]
            parts += [(3 + n, a["L1_mix_w_qkv"][:, n * D:(n + 1) * D]) for n in range(3)]
            parts += [(6 + n, a["L1_mix_w_fc1"][:, n * D:(n + 1) * D]) for n in range(3)]
            parts += [(9 + n, a["L1_mix_w_fc2"][n * D:(n + 1) * D, :]) for n in range(3)]
            for n, src in parts:
                sp.dma_start(m.w[:, n, :, :], src.rearrange("(k p) n -> p k n", p=P)).then_inc(loaded, 16)
            with sp.Fori(0, 10) as i:
                sp.wait_ge(tiles_ready, i * 5 + 5)
                sp.dma_start(to[:, bass.ds(i * 5, 5), :], m.acc[0:T, bass.ds(i * 5, 5), :]).then_inc(stored, 16)
            sp.wait_ge(stored, 160)
            sp.wait_ge(loaded, 16 * len(parts))

        @block.vector
        def _(dve):
            chain = m.chain
            norm_stats(nc, dve, chain, m)
            chain.link(nc.vector.tensor_scalar(deg, m.x[0:T, :, D], 1.0, None, ALU.add))
            chain.link(nc.vector.tensor_scalar(pos, deg, 0.0, None, ALU.is_gt))
            chain.link(nc.vector.tensor_scalar(deg, deg, 1e-30, None, ALU.max))
            inverse_root(nc, chain, m.dinv[0:T, :], deg, 0.0, h, q)
            chain.link(nc.vector.tensor_tensor(m.dinv[0:T, :], m.dinv[0:T, :], pos, ALU.mult))
            chain.link(nc.vector.tensor_tensor(ry, m.dinv[0:T, :], m.rstd[0:T, :], ALU.mult))
            with dve.Fori(0, NT) as t:
                nc.vector.tensor_scalar(tile_of(m.acc, t, D), tile_of(m.x, t, D), m.mean[0:T, bass.ds(t, 1)],
                                        ry[:, bass.ds(t, 1)], ALU.subtract, ALU.mult).then_inc(tiles_ready, 1)


def mix1(nc, m, sem):
    W, ps = m.work, m.ps
    xn, xT, k_sb, v_sb = W[:, 0:2, :], W[:, 2:4, 0:GN], W[:, 4:6, :], W[:, 6:8, :]
    qT, x2, ln, hT = W[:, 4:6, 0:GN], W[:, 6:8, :], W[:, 8:10, :], W[:, 10:12, 0:GN]
    h1 = W[:, 12:18, 0:GN]
    logit, prob = W[:, 18, 0:P].rearrange("p (h e) -> p h e", h=2), W[:, 18, P:2 * P].rearrange("p (h e) -> p h e", h=2)
    diag, attnT = W[:, 19, :].rearrange("p (h e) -> p h e", h=2), W[:, 20, :].rearrange("p (h e) -> p h e", h=2)
    zero = W[:, 21, :]
    mx, sm = m.small[:, 0:2], m.small[:, 2:4]
    rs, rh, rq, ve = m.small[0:T, 8:10], m.small[0:T, 10:12], m.small[0:T, 12:14], m.small[0:T, 14:16]
    names = ("set xn tp xT k v k_sb v_sb kv logits exp attn attn_tp attnT bxn btp bxT q qT xf x2 ln ln_tp hT fc1 h1 fc2").split()
    s = {n: sem(f"mix1_{n}") for n in names}
    col = lambda name, h: m.col_bias[:, COL[name] + h:COL[name] + h + 1]
    both = lambda bank: ps[0:T, bank, :].rearrange("p (k d) -> p k d", k=2)
    halves = lambda bank: ps[:, bank, 0:2 * GN].rearrange("p (h c) -> p h c", h=2)
    row = lambda name: m.row_bias[0:T, ROW[name], :].unsqueeze(1).to_broadcast([T, 2, D])
    with nc.Block() as block:

        @block.vector
        def _(dve):
            chain = m.chain
            nc.vector.memset(zero, 0.0).then_inc(s["set"], 1)
            nc.vector.memset(diag, 0.0).then_inc(s["set"], 1)
            with dve.Fori(0, G) as g:
                dve.wait_ge(s["tp"], g)
                for k in range(2):
                    normalise(nc, m, xn[0:T, k, :], g, k).then_inc(s["xn"], 1)
                dve.wait_ge(s["kv"], g)
                for bank, to, name in ((1, k_sb, "k"), (2, v_sb, "v")):
                    dve.wait_ge(s[name], g + 1)
                    nc.vector.tensor_tensor(to[0:T, :, :], both(bank), row(name[0] == "k" and "bk1" or "bv1"), ALU.add).then_inc(s[name + "_sb"], 1)
            dve.wait_ge(s["kv"], G)
            for h in range(2):
                for b in range(2):
                    chain.did(nc.vector.tensor_copy(logit[64 * b:64 * b + 64, h, :],
                                                    ps[64 * b:64 * b + 64, 4, h * P + 64 * b:h * P + 64 * b + 64]))
            chain.settle()
            chain.link(nc.vector.tensor_reduce(mx, logit, AX.X, ALU.max))
            nc.vector.tensor_tensor(logit, logit, mx.unsqueeze(2).to_broadcast([P, 2, 64]), ALU.subtract).then_inc(s["logits"], 1)
            dve.wait_ge(s["exp"], 1)
            chain.link(nc.vector.tensor_reduce(sm, prob, AX.X, ALU.add))
            chain.link(nc.vector.reciprocal(sm, sm))
            dve.wait_ge(s["set"], 2)
            for h in range(2):
                for b in range(2):
                    lo, hi = 64 * b, 64 * b + 64
                    nc.vector.tensor_scalar(diag[lo:hi, h, lo:hi], prob[lo:hi, h, :], sm[lo:hi, h:h + 1], None, ALU.mult).then_inc(s["attn"], 1)
            with dve.Fori(0, G) as g:
                chain.begin(g, 1 + 2 + 2 + 16 + 3)
                dve.wait_ge(s["btp"], g)
                dve.wait_ge(s["x2"], g)
                for k in range(2):
                    normalise(nc, m, xn[0:T, k, :], g, k).then_inc(s["bxn"], 1)
                dve.wait_ge(s["xf"], g + 1)
                dve.wait_ge(s["bxn"], g * 2 + 2)
                chain.link(nc.vector.tensor_tensor(x2[0:T, :, :], both(2), xn[0:T, :, :], ALU.add))
                for k in range(2):
                    chain.did(nc.vector.bn_stats(m.stats[0:T, k, :], x2[0:T, k, :]))
                chain.settle_apart()
                for k in range(2):
                    chain.did(nc.vector.bn_aggr(m.mv[0:T, k, :], m.stats[0:T, k, :]))
                chain.settle()
                inverse_root(nc, chain, rs, m.mv[0:T, :, 1], EPS, rh, rq)
                dve.wait_ge(s["ln_tp"], g)
                for k in range(2):
                    nc.vector.tensor_scalar(ln[0:T, k, :], x2[0:T, k, :], m.mv[0:T, k, 0:1], rs[:, k:k + 1],
                                            ALU.subtract, ALU.mult).then_inc(s["ln"], 1)
                xg = m.x[0:T, bass.ds(g * 2, 2), 0:D]
                dve.wait_ge(s["ln"], 2 * g + 2)
                chain.link(nc.vector.tensor_tensor(x2[0:T, :, :], x2[0:T, :, :], row("fc2"), ALU.add))
                chain.link(nc.vector.tensor_tensor(xg, xg, x2[0:T, :, :], ALU.add))
                dve.wait_ge(s["fc2"], g + 1)
                chain.link(nc.vector.tensor_tensor(xg, xg, both(7), ALU.add))
                nc.vector.memset(m.small[0:1, 20:21], 0.0).then_inc(s["x2"], 1)
                chain.end(G)

        @block.scalar
        def _(act):
            with act.Fori(0, G) as g:
                act.wait_ge(s["tp"], g + 1)
                act.wait_ge(s["v"], g)
                nc.scalar.copy(xT, halves(0)).then_inc(s["xT"], 1)
            act.wait_ge(s["logits"], 1)
            nc.scalar.activation(prob, logit, ACT.Exp, scale=64.0 ** -0.5).then_inc(s["exp"], 1)
            act.wait_ge(s["attn_tp"], 1)
            nc.scalar.copy(attnT, ps[:, 5, 0:2 * P].rearrange("p (h e) -> p h e", h=2)).then_inc(s["attnT"], 1)
            with act.Fori(0, G) as g:
                act.wait_ge(s["btp"], g + 1)
                act.wait_ge(s["q"], g)
                nc.scalar.copy(xT, halves(0)).then_inc(s["bxT"], 1)
                act.wait_ge(s["q"], g + 1)
                act.wait_ge(s["xf"], g)
                for h in range(2):
                    nc.scalar.activation(qT[:, h, :], halves(1)[:, h, :], ACT.Identity, bias=col("bq1", h)).then_inc(s["qT"], 1)
                act.wait_ge(s["ln_tp"], g + 1)
                act.wait_ge(s["fc1"], 3 * g)
                for h in range(2):
                    nc.scalar.activation(hT[:, h, :], halves(3)[:, h, :], ACT.Identity, bias=col("norm_b", h),
                                         scale=col("norm_g", h)).then_inc(s["hT"], 1)
                act.wait_ge(s["fc2"], g)
                for o in range(6):
                    act.wait_ge(s["fc1"], 3 * g + o // 2 + 1)
                    nc.scalar.activation(h1[:, o, :], halves(4 + o // 2)[:, o % 2, :], ACT.Gelu, bias=col("fc1", o)).then_inc(s["h1"], 1)

        @block.tensor
        def _(pe):
            pe.wait_ge(s["set"], 2)
            nc.tensor.matmul(ps[:, 4, 0:D], zero[:, 0:P], zero, start=True, stop=False, skip_group_check=True)
            with pe.Fori(0, G) as g:
                pe.wait_ge(s["xn"], g * 2 + 2)
                pe.wait_ge(s["xT"], g)
                transpose_group(nc, m, 0, xn).then_inc(s["tp"], 1)
                pe.wait_ge(s["xT"], g + 1)
                for n, name in ((1, "k"), (2, "v")):
                    pe.wait_ge(s[name + "_sb"], g)
                    for k in range(2):
                        last = rows_times(nc, ps[0:T, n, k * D:(k + 1) * D], lambda h: xT[:, h, k * T:(k + 1) * T],
                                          lambda h: m.w[:, 3 + n, h, :])
                    last.then_inc(s[name], 1)
                pe.wait_ge(s["k_sb"], g + 1)
                pe.wait_ge(s["v_sb"], g + 1)
                for k in range(2):
                    for h in range(2):
                        last = nc.tensor.matmul(ps[:, 4, h * P:(h + 1) * P], k_sb[0:T, k, h * P:(h + 1) * P],
                                                v_sb[0:T, k, h * P:(h + 1) * P], start=False, stop=False, skip_group_check=True)
                last.then_inc(s["kv"], 1)
            pe.wait_ge(s["attn"], 4)
            for h in range(2):
                last = nc.tensor.transpose(ps[:, 5, h * P:(h + 1) * P], diag[:, h, :], m.ident[:, :])
            last.then_inc(s["attn_tp"], 1)
            pe.wait_ge(s["attnT"], 1)
            with pe.Fori(0, G) as g:
                pe.wait_ge(s["bxn"], g * 2 + 2)
                pe.wait_ge(s["bxT"], g)
                transpose_group(nc, m, 0, xn).then_inc(s["btp"], 1)
                pe.wait_ge(s["bxT"], g + 1)
                pe.wait_ge(s["qT"], 2 * g)
                for o in range(2):
                    for h in range(2):
                        last = nc.tensor.matmul(ps[:, 1, o * GN:(o + 1) * GN], m.w[:, 3, h, o * P:(o + 1) * P], xT[:, h, :],
                                                start=h == 0, stop=h == 1)
                last.then_inc(s["q"], 1)
                pe.wait_ge(s["qT"], 2 * g + 2)
                for k in range(2):
                    for h in range(2):
                        last = nc.tensor.matmul(ps[0:T, 2, k * D + h * P:k * D + (h + 1) * P], qT[:, h, k * T:(k + 1) * T],
                                                attnT[:, h, :], start=True, stop=True)
                last.then_inc(s["xf"], 1)
                pe.wait_ge(s["ln"], 2 * g + 2)
                pe.wait_ge(s["hT"], 2 * g)
                transpose_group(nc, m, 3, ln).then_inc(s["ln_tp"], 1)
                pe.wait_ge(s["hT"], 2 * g + 2)
                for o in range(6):
                    if o % 2 == 0:
                        pe.wait_ge(s["h1"], 6 * g)
                    for h in range(2):
                        last = nc.tensor.matmul(halves(4 + o // 2)[:, o % 2, :], m.w[:, 6 + o // 2, h, (o % 2) * P:(o % 2 + 1) * P],
                                                hT[:, h, :], start=h == 0, stop=h == 1)
                    if o % 2:
                        last.then_inc(s["fc1"], 1)
                pe.wait_ge(s["h1"], 6 * g + 6)
                pe.wait_ge(s["x2"], g)
                for k in range(2):
                    for c in range(6):
                        last = nc.tensor.matmul(ps[0:T, 7, k * D:(k + 1) * D], h1[:, c, k * T:(k + 1) * T],
                                                m.w[:, 9 + c // 2, c % 2, :], start=c == 0, stop=c == 5)
                last.then_inc(s["fc2"], 1)


def gnn_head(nc, m, sem):
    W, ps = m.work, m.ps
    agg, T0, T1, T2 = W[:, 0:2, :], W[:, 2:4, 0:GN], W[:, 4:6, 0:GN], W[:, 6:8, 0:GN]
    s = {n: sem(f"head_{n}") for n in "agg tp aT h7 h7T h hT out added".split()}
    halves = lambda bank: ps[:, bank, 0:2 * GN].rearrange("p (h c) -> p h c", h=2)
    col = lambda name, h: m.col_bias[:, COL[name] + h:COL[name] + h + 1]
    with nc.Block() as block:

        @block.vector
        def _(dve):
            chain = m.chain
            with dve.Fori(0, G) as g:
                chain.begin(g, 1)
                dve.wait_ge(s["tp"], g)
                for k in range(2):
                    t = g * 2 + k
                    nc.vector.tensor_scalar(agg[0:T, k, :], tile_of(m.acc, t, D), m.dinv[0:T, bass.ds(t, 1)], None, ALU.mult).then_inc(s["agg"], 1)
                dve.wait_ge(s["out"], g + 1)
                xg = m.x[0:T, bass.ds(g * 2, 2), 0:D]
                chain.link(nc.vector.tensor_tensor(xg, xg, ps[0:T, 4, :].rearrange("p (k d) -> p k d", k=2), ALU.add))
                nc.vector.tensor_tensor(xg, xg, m.row_bias[0:T, ROW["gnn_b2"], :].unsqueeze(1).to_broadcast([T, 2, D]), ALU.add).then_inc(s["added"], 1)
                chain.end(G)

        @block.scalar
        def _(act):
            with act.Fori(0, G) as g:
                act.wait_ge(s["tp"], g + 1)
                act.wait_ge(s["h7"], g)
                nc.scalar.copy(T0, halves(0)).then_inc(s["aT"], 1)
                act.wait_ge(s["h7"], g + 1)
                act.wait_ge(s["h"], g)
                for h in range(2):
                    nc.scalar.activation(T1[:, h, :], halves(1)[:, h, :], ACT.Identity, bias=col("gnn_b", h)).then_inc(s["h7T"], 1)
                act.wait_ge(s["h"], g + 1)
                act.wait_ge(s["out"], g)
                for h in range(2):
                    nc.scalar.activation(T2[:, h, :], halves(2)[:, h, :], ACT.Relu, bias=col("gnn_b1", h)).then_inc(s["hT"], 1)

        @block.tensor
        def _(pe):
            with pe.Fori(0, G) as g:
                pe.wait_ge(s["agg"], 2 * g + 2)
                pe.wait_ge(s["aT"], g)
                transpose_group(nc, m, 0, agg).then_inc(s["tp"], 1)
                for n, (ready, count, used, had, of, mine) in enumerate((("aT", 1, "h7T", 2, T0, "h7"), ("h7T", 2, "hT", 2, T1, "h"))):
                    pe.wait_ge(s[ready], count * (g + 1))
                    pe.wait_ge(s[used], had * g)
                    for o in range(2):
                        for h in range(2):
                            last = nc.tensor.matmul(ps[:, 1 + n, o * GN:(o + 1) * GN], m.w[:, n, h, o * P:(o + 1) * P], of[:, h, :],
                                                    start=h == 0, stop=h == 1)
                    last.then_inc(s[mine], 1)
                pe.wait_ge(s["hT"], 2 * g + 2)
                pe.wait_ge(s["added"], g)
                for k in range(2):
                    last = rows_times(nc, ps[0:T, 4, k * D:(k + 1) * D], lambda h: T2[:, h, k * T:(k + 1) * T], lambda h: m.w[:, 2, h, :])
                last.then_inc(s["out"], 1)


def experts(nc, m, sem, a, layer, out=None):
    EX, DEEP = (E0, 2) if layer == 0 else (E1, 3)
    W, ps = m.work, m.ps
    w = m.flat[:, 0:EX * DEEP * 2 * D].rearrange("p (e k n) -> p e k n", k=KD, n=D)
    xn, xT = W[:, 0:2, :], W[:, 2:4, 0:GN]
    hid = [W[:, 4 + 2 * i:6 + 2 * i, 0:GN] for i in range(2)]
    hid2 = [W[:, 8 + 2 * i:10 + 2 * i, 0:GN] for i in range(2)]
    rw = W[:, 12, :].rearrange("p (h n) -> p h n", h=2)
    rw2, rb2, rT = W[:, 13, 0:E1], W[:, 13, 16:16 + E1], W[:, 14, 0:GN]
    b_out = W[0:EX, 15, :]
    cT = W[0:EX, 16, 0:GN]
    r = W[0:T, 17, :]
    lg, best, comb, other = (r[:, 16 * n:16 * n + 16].rearrange("p (k e) -> p k e", k=2) for n in range(4))
    bi = r[:, 64:80].bitcast(U32).rearrange("p (k e) -> p k e", k=2)
    bif = r[:, 80:84].rearrange("p (k e) -> p k e", k=2)
    gap, th, w1, w2, mx, sm = (r[:, 84 + 2 * n:86 + 2 * n] for n in range(6))
    ex = r[:, 100:116].rearrange("p (k e) -> p k e", k=2)
    NR = 128 if layer else EX
    nsteps = EX + DEEP - 1
    names = "in xn tp xT logits gap th comb ctp cT u h y added"
    names += " rh rT v h2 stored group" if layer else " group"
    s = {n: sem(f"moe{layer}_{n}") for n in names.split()}
    halves = lambda bank: ps[:, bank, 0:2 * GN].rearrange("p (h c) -> p h c", h=2)
    col = lambda n: m.col_bias[:, COL["expert"] + n:COL["expert"] + n + 1]
    YS = EX + 1
    loads = 0
    if out is not None:
        to = out.rearrange("(t p) d -> p t d", p=T)
    with nc.Block() as block:

        if layer == 0:
            parts = [("L0_ffn_w1", 0), ("L0_ffn_w2", EX)]
            cols = [("L0_ffn_b1", 0)]
            rows = "L0_ffn_b2"
            n_loads = 2 + 1 + 1 + 1
        else:
            parts = [("L1_ffn_expert_w1", 0), ("L1_ffn_expert_w2", EX), ("L1_ffn_expert_w3", 2 * EX)]
            cols = [("L1_ffn_expert_b1", 0), ("L1_ffn_expert_b2", 2 * EX)]
            rows = "L1_ffn_expert_b3"
            n_loads = 3 + 2 + 1 + 3

        @block.sync
        def _(sp):
            with nc.allow_non_contiguous_dma(reason="biases and router weights, one channel in each partition"):
                if layer == 0:
                    sp.dma_start(rw[:, :, 0:EX], a["L0_ffn_router_w"].rearrange("(h p) e -> p h e", p=P)).then_inc(s["in"], 16)
                else:
                    sp.dma_start(rw, a["L1_ffn_router_w1"].rearrange("(h p) e -> p h e", p=P)).then_inc(s["in"], 16)
                    sp.dma_start(rw2, a["L1_ffn_router_w2"]).then_inc(s["in"], 16)
                    sp.dma_start(rb2, a["L1_ffn_router_b2"].rearrange("(a e) -> a e", a=1).to_broadcast([P, E1])).then_inc(s["in"], 16)
                for name, at in cols:
                    sp.dma_start(m.col_bias[:, COL["expert"] + at:COL["expert"] + at + 2 * EX],
                                 a[name].rearrange("e (h p) -> p (e h)", p=P)).then_inc(s["in"], 16)
            sp.dma_start(b_out, a[rows]).then_inc(s["in"], 16)
            for name, at in parts:
                sp.dma_start(w[:, at:at + EX, :, :].rearrange("p e k n -> p (e k) n"),
                             a[name].rearrange("e (k p) n -> p (e k) n", p=P)).then_inc(s["in"], 16)
            if out is not None:
                with sp.Fori(0, G) as g:
                    sp.wait_ge(s["group"], g + 1)
                    sp.dma_start(to[:, bass.ds(g * 2, 2), :], m.x[0:T, bass.ds(g * 2, 2), 0:D]).then_inc(s["stored"], 16)
                sp.wait_ge(s["stored"], 16 * G)

        @block.vector
        def _(dve):
            chain = m.chain
            norm_stats(nc, dve, chain, m)
            if layer == 1:
                chain.link(nc.vector.memset(r[:, 0:64], -1.0))
            for k in range(2):
                normalise(nc, m, xn[0:T, k, :], 0, k).then_inc(s["xn"], 1)

            def router(g):
                dve.wait_ge(s["logits"], g + 1)
                both = ps[0:T, 1, 0:16].rearrange("p (k e) -> p k e", k=2)[:, :, 0:EX]
                if layer == 0:
                    chain.link(nc.vector.tensor_copy(lg, both))
                    values = lg
                else:
                    chain.link(nc.vector.tensor_tensor(lg[:, :, 0:EX], both, rb2[0:T, :].unsqueeze(1).to_broadcast([T, 2, EX]), ALU.add))
                    chain.link(nc.vector.tensor_reduce(mx, lg[:, :, 0:EX], AX.X, ALU.max))
                    nc.vector.tensor_tensor(ex[:, :, 0:EX], lg[:, :, 0:EX], mx.unsqueeze(2).to_broadcast([T, 2, EX]), ALU.subtract).then_inc(s["gap"], 1)
                    dve.wait_ge(s["th"], 2 * g + 1)
                    chain.link(nc.vector.tensor_reduce(sm, ex[:, :, 0:EX], AX.X, ALU.add))
                    chain.link(nc.vector.reciprocal(sm, sm))
                    chain.link(nc.vector.tensor_tensor(other[:, :, 0:EX], ex[:, :, 0:EX], sm.unsqueeze(2).to_broadcast([T, 2, EX]), ALU.mult))
                    values = other
                chain.apart()
                for k in range(2):
                    chain.did(nc.vector.max(best[:, k, :], values[:, k, :]))
                chain.settle_apart()
                for k in range(2):
                    chain.did(nc.vector.max_index(bi[:, k, :], best[:, k, :], values[:, k, :]))
                chain.settle()
                chain.did(nc.vector.tensor_copy(bif, bi[:, :, 0:2]))
                nc.vector.tensor_tensor(gap, best[:, :, 0], best[:, :, 1], ALU.subtract).then_inc(s["gap"], 1)
                chain.settle()

            def weigh(g):
                if layer == 0:
                    dve.wait_ge(s["th"], g + 1)
                    chain.did(nc.vector.tensor_scalar(w1, th, 0.5, 0.5, ALU.mult, ALU.add))
                    chain.did(nc.vector.tensor_scalar(w2, th, -0.5, 0.5, ALU.mult, ALU.add))
                    chain.settle()
                else:
                    dve.wait_ge(s["th"], 2 * g + 2)
                    chain.link(nc.vector.tensor_scalar(w1, th, 1.0, None, ALU.add))
                    chain.link(nc.vector.reciprocal(w1, w1))
                    chain.link(nc.vector.tensor_tensor(w2, th, w1, ALU.mult))
                dve.wait_ge(s["ctp"], g)
                for k in range(2):
                    chain.did(nc.vector.tensor_scalar(comb[:, k, :], m.iota[0:T, 0:8], bif[:, k, 0:1], w1[:, k:k + 1], ALU.is_equal, ALU.mult))
                    chain.did(nc.vector.tensor_scalar(lg[:, k, :], m.iota[0:T, 0:8], bif[:, k, 1:2], w2[:, k:k + 1], ALU.is_equal, ALU.mult))
                chain.settle()
                nc.vector.tensor_tensor(comb, comb, lg, ALU.add).then_inc(s["comb"], 1)
                dve.wait_ge(s["comb"], g + 1)

            def turn(g, last):
                xg = m.x[0:T, bass.ds(g * 2, 2), 0:D]
                router(g)
                if layer == 0:
                    chain.link(nc.vector.tensor_tensor(xg, xg, xn[0:T, :, :], ALU.add))
                weigh(g)
                for n in range(YS):
                    if n == EX // 2 and not last:
                        for k in range(2):
                            normalise(nc, m, xn[0:T, k, :], g + 1, k).then_inc(s["xn"], 1)
                    dve.wait_ge(s["y"], g * YS + n + 1)
                    y = ps[0:T, 4 + n % 2, :].rearrange("p (k d) -> p k d", k=2)
                    if n < EX:
                        for k in range(2):
                            to = tile_of(m.x, g * 2 + k, D)
                            chain.did(nc.vector.scalar_tensor_tensor(to, y[:, k, :], comb[:, k, n:n + 1], to, ALU.mult, ALU.add))
                        chain.settle()
                        nc.vector.memset(m.small[0:1, 200:201], 0.0).then_inc(s["added"], 1)
                    else:
                        nc.vector.tensor_tensor(xg, xg, y, ALU.add).then_inc(s["added"], 1)
                        dve.wait_ge(s["added"], g * YS + YS)
                nc.vector.memset(m.small[0:1, 201:202], 0.0).then_inc(s["group"], 1)

            steps = (1 if layer == 0 else 5) + 2 + 2 + 1 + (1 if layer == 0 else 0) + (2 if layer == 0 else 3) + 4 + 2 * EX
            with dve.Fori(0, G - 1) as g:
                chain.begin(g, steps)
                turn(g, False)
                chain.end(G - 1)
            turn(G - 1, True)

        @block.scalar
        def _(act):
            act.wait_ge(s["tp"], 1)
            nc.scalar.copy(xT, halves(0)).then_inc(s["xT"], 1)

            def evacuate(g, e, bank, to, ready, wrote, readers, func, bias):
                act.wait_ge(s[ready], g * EX + e + 1)
                per, count = readers
                act.wait_ge(s[per], g * count + max(e - 1, 0))
                for h in range(2):
                    ins = nc.scalar.activation(to[:, h, :], halves(bank)[:, h, :], func, bias=col(bias + h))
                ins.then_inc(s[wrote], 1)

            def turn(g, last):
                if layer == 1:
                    act.wait_ge(s["rh"], g + 1)
                    nc.scalar.activation(rT, ps[:, 1, 16:16 + GN], ACT.Relu, bias=m.col_bias[:, COL["router_b1"]:COL["router_b1"] + 1]).then_inc(s["rT"], 1)
                for step in range(nsteps):
                    if step < EX:
                        evacuate(g, step, 2 + step % 2, hid[step % 2], "u", "h", ("y", YS) if DEEP == 2 else ("v", EX),
                                 ACT.Gelu if layer == 0 else ACT.Relu, 2 * step)
                    if DEEP == 3 and 1 <= step <= EX:
                        e = step - 1
                        evacuate(g, e, 6 + e % 2, hid2[e % 2], "v", "h2", ("y", YS), ACT.Relu, 2 * EX + 2 * e)
                    if step == 0:
                        act.wait_ge(s["gap"], (g + 1) if layer == 0 else (2 * g + 1))
                        if layer == 0:
                            nc.scalar.activation(th, gap, ACT.Tanh, scale=0.5).then_inc(s["th"], 1)
                        else:
                            nc.scalar.activation(ex[:, :, 0:EX], ex[:, :, 0:EX], ACT.Exp).then_inc(s["th"], 1)
                            act.wait_ge(s["gap"], 2 * g + 2)
                            nc.scalar.activation(th, gap, ACT.Exp, scale=-1.0).then_inc(s["th"], 1)
                    if step == 2:
                        act.wait_ge(s["ctp"], g + 1)
                        nc.scalar.copy(cT, ps[0:EX, 1, 0:GN]).then_inc(s["cT"], 1)
                    if step == EX - 1 and not last:
                        act.wait_ge(s["tp"], g + 2)
                        nc.scalar.copy(xT, halves(0)).then_inc(s["xT"], 1)

            with act.Fori(0, G - 1) as g:
                turn(g, False)
            turn(G - 1, True)

        @block.tensor
        def _(pe):
            pe.wait_ge(s["in"], 16 * n_loads)
            pe.wait_ge(s["xn"], 2)
            transpose_group(nc, m, 0, xn).then_inc(s["tp"], 1)

            def square(g, e, at, of, bank, done, free):
                pe.wait_ge(s[free], g * EX + max(e - 1, 0))
                for o in range(2):
                    for h in range(2):
                        last = nc.tensor.matmul(ps[:, bank, o * GN:(o + 1) * GN], w[:, at + e, h, o * P:(o + 1) * P], of[:, h, :],
                                                start=h == 0, stop=h == 1)
                last.then_inc(s[done], 1)

            def rows_out(g, e):
                pe.wait_ge(s["h" if DEEP == 2 else "h2"], g * EX + e + 1)
                pe.wait_ge(s["added"], g * YS + max(e - 1, 0))
                of = (hid if DEEP == 2 else hid2)[e % 2]
                for k in range(2):
                    last = rows_times(nc, ps[0:T, 4 + e % 2, k * D:(k + 1) * D], lambda h: of[:, h, k * T:(k + 1) * T],
                                      lambda h: w[:, (DEEP - 1) * EX + e, h, :])
                last.then_inc(s["y"], 1)

            def turn(g, last_turn):
                pe.wait_ge(s["xT"], g + 1)
                pe.wait_ge(s["cT"], g)
                if layer == 1:
                    for h in range(2):
                        last = nc.tensor.matmul(ps[:, 1, 16:16 + GN], rw[:, h, :], xT[:, h, :], start=h == 0, stop=h == 1)
                    last.then_inc(s["rh"], 1)
                    pe.wait_ge(s["rT"], g + 1)
                for k in range(2):
                    if layer == 0:
                        for h in range(2):
                            last = nc.tensor.matmul(ps[0:T, 1, 8 * k:8 * k + EX], xT[:, h, k * T:(k + 1) * T], rw[:, h, 0:EX],
                                                    start=h == 0, stop=h == 1)
                    else:
                        last = nc.tensor.matmul(ps[0:T, 1, 8 * k:8 * k + EX], rT[:, k * T:(k + 1) * T], rw2, start=True, stop=True)
                last.then_inc(s["logits"], 1)
                for step in range(nsteps):
                    if step < EX:
                        square(g, step, 0, xT, 2 + step % 2, "u", "h")
                    if step == EX - 1 and not last_turn:
                        pe.wait_ge(s["xn"], 2 * g + 4)
                        transpose_group(nc, m, 0, xn).then_inc(s["tp"], 1)
                    if DEEP == 3 and 1 <= step <= EX:
                        e = step - 1
                        pe.wait_ge(s["h"], g * EX + e + 1)
                        square(g, e, EX, hid[e % 2], 6 + e % 2, "v", "h2")
                    if step >= DEEP - 1:
                        rows_out(g, step - DEEP + 1)
                    if step == 2:
                        pe.wait_ge(s["comb"], g + 1)
                        for k in range(2):
                            last = nc.tensor.transpose(ps[0:EX, 1, k * T:(k + 1) * T], comb[:, k, 0:EX], m.ident[0:T, 0:T])
                        last.then_inc(s["ctp"], 1)
                pe.wait_ge(s["cT"], g + 1)
                pe.wait_ge(s["added"], g * YS + EX - 1)
                for k in range(2):
                    last = nc.tensor.matmul(ps[0:T, 4 + EX % 2, k * D:(k + 1) * D], cT[:, k * T:(k + 1) * T], b_out, start=True, stop=True)
                last.then_inc(s["y"], 1)

            with pe.Fori(0, G - 1) as g:
                turn(g, False)
            turn(G - 1, True)


def gps_kernel(nc, a, out):
    ctx = ExitStack()
    with ctx:
        m = Memory(nc, ctx)

        def sem(name):
            return ctx.enter_context(nc.semaphore(name))

        rank_edges(nc, m, sem, a)
        scatter_and_mix0(nc, m, sem)
        gather_sums(nc, m, sem, 0)
        experts(nc, m, sem, a, 0)
        table1(nc, m, sem, a)
        gather_sums(nc, m, sem, 1)
        mix1(nc, m, sem)
        gnn_head(nc, m, sem)
        experts(nc, m, sem, a, 1, out)


_INS = ("x src dst edge_weight L0_gnn_W L0_mix_wq L0_mix_bq L0_mix_wk L0_mix_bk L0_mix_wv L0_mix_bv L0_mix_wo L0_mix_bo "
        "L0_ffn_router_w L0_ffn_w1 L0_ffn_b1 L0_ffn_w2 L0_ffn_b2 L1_gnn_W L1_gnn_b L1_gnn_W1 L1_gnn_b1 L1_gnn_W2 L1_gnn_b2 "
        "L1_mix_w_qkv L1_mix_b_qkv L1_mix_norm_g L1_mix_norm_b L1_mix_w_fc1 L1_mix_b_fc1 L1_mix_w_fc2 L1_mix_b_fc2 "
        "L1_ffn_router_w1 L1_ffn_router_b1 L1_ffn_router_w2 L1_ffn_router_b2 L1_ffn_expert_w1 L1_ffn_expert_b1 "
        "L1_ffn_expert_w2 L1_ffn_expert_b2 L1_ffn_expert_w3 L1_ffn_expert_b3").split()


def kernel(**inputs):
    import concourse.bacc as bacc
    from concourse.bass_utils import run_bass_kernel_spmd

    nc = bacc.Bacc("TRN2", target_bir_lowering=False, num_devices=1)
    arrays, a = {}, {}
    for name in _INS:
        v = np.asarray(inputs[name])
        if name in ("L0_gnn_W", "L0_ffn_router_w"):
            v = v.T
        v = np.ascontiguousarray(v)
        arrays[f"in_{name}"] = v
        a[name] = nc.dram_tensor(f"in_{name}", v.shape, mybir.dt.from_np(v.dtype), kind="ExternalInput").ap()
    out = nc.dram_tensor("out", (N, D), F32, kind="ExternalOutput").ap()
    gps_kernel(nc, a, out)
    r = run_bass_kernel_spmd(nc, [arrays], core_ids=[0])
    return r.results[0]["out"]
```

```python
from contextlib import ExitStack

import numpy as np
import concourse.bass as bass
from concourse import mybir

F32, I32, U32 = mybir.dt.float32, mybir.dt.int32, mybir.dt.uint32
ALU = mybir.AluOpType
ACT = mybir.ActivationFunctionType
AX = mybir.AxisListType

P = 128
N, D, E = 6250, 256, 200000
T = 125
NT = N // T
G = NT // 2
GN = 2 * T
KD = D // P
EC = -(-E // P)
TAIL = E - (P - 1) * EC
HALF = 8
CHUNKS = -(-((P * EC + NT * (P - 1)) // P) // (2 * HALF)) * 2 * HALF
RING = 2 * HALF
FIRST = 9 * 32
SC = 16
MAGIC = 1.5 * 2.0 ** 23
EPS = 1e-5
E0, E1 = 8, 6
KC = (P - 1 + CHUNKS) // P


class Chain:

    def __init__(self, engine, sem):
        self.engine, self.sem, self.base, self.n = engine, sem, 0, 0

    def begin(self, index, steps):
        self.start, self.steps = self.base + self.n, steps
        self.base, self.n = index * steps + self.start, 0

    def end(self, trips):
        assert self.n == self.steps, (self.n, self.steps)
        self.base, self.n = self.start + trips * self.steps, 0

    def did(self, instruction):
        instruction.then_inc(self.sem, 1)
        self.n += 1

    def settle(self):
        self.engine.wait_ge(self.sem, self.base + self.n)

    def settle_apart(self):
        self.settle()
        self.apart()

    def apart(self):
        self.engine.sem_inc(self.spare, 1)

    def link(self, instruction):
        self.did(instruction)
        self.settle()


def apart(nc, m):
    nc.gpsimd.sem_inc(m.pool_spare, 1)


def tile_of(view, t, width):
    return view[0:T, bass.ds(t, 1), 0:width].rearrange("p a b -> p (a b)")


class Memory:

    def __init__(self, nc, ctx):
        def sb(name, shape, dt=F32):
            return ctx.enter_context(nc.sbuf_tensor(name, shape, dt))

        self.x = sb("x_res", [P, NT, D + 1])
        self.acc = sb("acc", [P, NT, D])
        self.flat = self.acc[:, :, :].rearrange("p a b -> p (a b)")
        parts = (RING * (D + 1), RING * T, CHUNKS, 2 * (CHUNKS + HALF))
        self.region = sb("gather_region", [P, sum(parts)])
        at = [sum(parts[:n]) for n in range(5)]
        rows, hot, dst, lew = (self.region[:, at[n]:at[n + 1]] for n in range(4))
        self.rows = rows.rearrange("p (s d) -> p s d", s=RING)
        self.hot = hot.rearrange("p (s n) -> p s n", s=RING)
        self.dst = dst.bitcast(I32)
        self.lew = lew.rearrange("p (c f) -> p c f", f=2)
        self.blk = sb("chunk_tile", [1, KC * P], I32)
        self.idx = sb("idx_stage", [P, 4, HALF], I32)
        self.w = sb("weights", [P, 12, KD, D])
        self.ident = sb("ident", [P, P])
        self.iota = sb("iota_free", [P, P])
        self.iota_i = sb("iota_int", [P, P], I32)
        self.row_bias = sb("row_bias", [P, 7, D])
        self.col_bias = sb("col_bias", [P, 48])
        self.mean = sb("mean", [P, NT])
        self.rstd = sb("rstd", [P, NT])
        self.dinv = sb("dinv", [P, NT])
        self.stats = sb("stats", [P, 2, 6])
        self.mv = sb("mean_var", [P, 2, 2])
        self.work = sb("work", [P, 22, D])
        self.small = sb("small", [P, 256])
        self.chain = Chain(nc.vector, ctx.enter_context(nc.semaphore("vector_done")))
        self.pool_spare = ctx.enter_context(nc.semaphore("pool_waited"))
        self.chain.spare = ctx.enter_context(nc.semaphore("vector_waited"))
        self.row_in = [ctx.enter_context(nc.semaphore(f"row_in_{s}")) for s in range(RING)]
        self.ps = ctx.enter_context(nc.psum_tensor("ps", [P, 8, 512], F32))
        self.table = [nc.dram_tensor(f"table{n}", (N, D), F32, kind="Internal").ap() for n in range(2)]
        self.sorted = nc.dram_tensor("sorted_edges", (P * CHUNKS, 2), F32, kind="Internal").ap()
        self.chunk_dram = nc.dram_tensor("chunk_tile_dram", (P * KC,), I32, kind="Internal").ap()


COL = {"bq": 0, "gnn_b": 2, "gnn_b1": 4, "bq1": 6, "norm_g": 8, "norm_b": 10, "fc1": 12,
       "router_b1": 18, "expert": 20}
ROW = {"bk": 0, "bv": 1, "bo": 2, "bk1": 3, "bv1": 4, "fc2": 5, "gnn_b2": 6}


def norm_stats(nc, dve, chain, m):
    var = m.small[:, 0:NT]
    with dve.Fori(0, G) as g:
        chain.begin(g, 6)
        for k in range(2):
            chain.did(nc.vector.bn_stats(m.stats[0:T, k, :], tile_of(m.x, g * 2 + k, D)))
        chain.settle_apart()
        for k in range(2):
            chain.did(nc.vector.bn_aggr(m.mv[0:T, k, :], m.stats[0:T, k, :]))
        chain.settle()
        chain.did(nc.vector.tensor_copy(m.mean[0:T, bass.ds(g * 2, 2)], m.mv[0:T, :, 0]))
        chain.did(nc.vector.tensor_copy(var[0:T, bass.ds(g * 2, 2)], m.mv[0:T, :, 1]))
        chain.settle()
        chain.end(G)
    inverse_root(nc, chain, m.rstd[0:T, :], var[0:T, :], EPS, m.small[0:T, 64:64 + NT], m.small[0:T, 128:128 + NT])


def inverse_root(nc, chain, out, value, add, half, guess):
    chain.link(nc.vector.tensor_scalar(half, value, add, None, ALU.add))
    chain.link(nc.vector.tensor_scalar(guess.bitcast(I32), half.bitcast(I32), 1, None, ALU.arith_shift_right))
    chain.link(nc.vector.tensor_scalar(out.bitcast(I32), guess.bitcast(I32), -1.0, float(0x5F3759DF), ALU.mult, ALU.add))
    chain.link(nc.vector.tensor_scalar(half, half, -0.5, None, ALU.mult))
    for _ in range(3):
        chain.link(nc.vector.tensor_tensor(guess, out, out, ALU.mult))
        chain.link(nc.vector.tensor_tensor(guess, guess, half, ALU.mult))
        chain.link(nc.vector.scalar_tensor_tensor(out, guess, 1.5, out, ALU.add, ALU.mult))


def group_stats(nc, chain, m, tiles, root):
    chain.apart()
    for k in range(2):
        chain.did(nc.vector.bn_stats(m.stats[0:T, k, :], tiles[k]))
    chain.settle_apart()
    for k in range(2):
        chain.did(nc.vector.bn_aggr(m.mv[0:T, k, :], m.stats[0:T, k, :]))
    chain.settle()
    inverse_root(nc, chain, root, m.mv[0:T, :, 1], EPS, m.small[0:T, 10:12], m.small[0:T, 12:14])


STATS_STEPS = 2 + 2 + 13


def normalise(nc, m, out, g, k):
    t = g * 2 + k
    return nc.vector.tensor_scalar(out, tile_of(m.x, t, D), m.mean[0:T, bass.ds(t, 1)], m.rstd[0:T, bass.ds(t, 1)],
                                   ALU.subtract, ALU.mult)


def transpose_group(nc, m, bank, tiles):
    for h in range(KD):
        for k in range(2):
            last = nc.tensor.transpose(m.ps[:, bank, h * GN + k * T:h * GN + (k + 1) * T],
                                       tiles[0:T, k, h * P:(h + 1) * P], m.ident[0:T, 0:T])
    return last


def rows_times(nc, out, xT, w, start=True, stop=True):
    for h in range(KD):
        last = nc.tensor.matmul(out, xT(h), w(h), start=start and h == 0, stop=stop and h == KD - 1)
    return last


def edges_and_mix0(nc, m, sem, a):
    src_i, dst_i, ew, blk, loc, mask, scan, pos = (m.flat[:, n * EC:(n + 1) * EC] for n in range(8))
    src_i, dst_i = src_i.bitcast(I32), dst_i.bitcast(I32)
    addr = src_i
    rec = m.lew[:, :, :].rearrange("p c f -> p (c f)")
    rec2 = rec[:, 0:2 * EC].rearrange("p (e f) -> p e f", f=2)
    small = m.small
    cnt, base, start, tri = small[:, 0:NT], small[:, NT:2 * NT], small[:, 2 * NT:3 * NT], m.rows[:, 0, 0:P]
    chunks, incl = small[:, 3 * NT:4 * NT], small[:, 4 * NT:5 * NT]
    ones, zeros = m.rows[:, 1, 0:P], rec
    flag = m.rows[:, 2:5, :].rearrange("p a b -> p (a b)")[:, 0:KC * NT].rearrange("p (j b) -> p j b", j=KC)
    of, of_i, at = m.hot[:, 0, 0:KC], m.hot[:, 1, 0:KC].bitcast(I32), m.hot[:, 2, 0:KC]
    pads_set, edges_in, zeroed, sorted_zero = sem("pads_set"), sem("edges_in"), sem("zero_set"), sem("sorted_zeroed")
    made, counted, totalled, of_ready, of_out, of_in, x_in, placed = (
        sem("constants_made"), sem("counted"), sem("totalled"), sem("tile_of_chunk"), sem("chunk_tile_out"),
        sem("chunk_tile_in"), sem("x_in"), sem("edges_placed"))
    X_LOADS = 5 + 5 + 7 + 8
    x_dram = a["x"].rearrange("(t p) d -> p t d", p=T)
    W = m.work
    xn, xT = W[:, 0:2, :], W[:, 2:4, 0:GN]
    table_sb, kb, ke, kf = W[:, 4:6, :], W[:, 6:8, :], W[:, 8:10, :], W[:, 10:12, :]
    v = W[:, 12:15, :].rearrange("p a b -> p (a b)")[:, 0:2 * 258].rearrange("p (k c) -> p k c", k=2)
    kvd = W[:, 15, :].rearrange("p (h e) -> p h e", h=2)
    ksd = W[:, 16, :].rearrange("p (h e) -> p h e", h=2)
    same = W[:, 17, 0:P]
    st_addr = W[:, 18, 0:2 * SC].bitcast(I32).rearrange("p (h c) -> p h c", h=2)
    st_rec = W[:, 19, 0:4 * SC].rearrange("p (h c f) -> p h c f", h=2, f=2)
    qe, qf, oT = W[:, 6:8, 0:GN], W[:, 8:10, 0:GN], W[:, 10:12, 0:GN]
    qm, rn = W[:, 4:6, 0:GN], W[:, 12:14, 0:GN]
    ps = m.ps
    staged, scattered = sem("scatter_staged"), [sem(f"scattered{h}") for h in range(2)]
    set_up = sem("set_up0")
    xn_ready, tp_done, xT_ready = sem("xn0"), sem("xn0_transposed"), sem("xT0")
    proj, km_ready, ke_ready, kf_ready, v_ready, kv_done = (
        sem("table_k_v"), sem("k_min"), sem("k_exp"), sem("kf"), sem("v_ready"), sem("kv_summed"))
    table_ready, table_out = sem("table0_ready"), sem("table0_out")
    kvd_ready, qxn, qtp, qxT, q_done, qm_ready, qe_ready, qf_ready, o_done, oT_ready, y_done, y_added = (
        sem("kv_diag"), sem("q_xn"), sem("q_transposed"), sem("q_xT"), sem("q_done"), sem("q_min"), sem("q_exp"),
        sem("qf"), sem("o_done"), sem("oT"), sem("y_done"), sem("y_added"))
    bq = [m.col_bias[:, COL["bq"] + h:COL["bq"] + h + 1] for h in range(2)]

    def scatter(pool, first, h, count, stage_count):
        nc.gpsimd.tensor_copy(st_addr[:, h, 0:count], addr[:, bass.ds(first, count)]).then_inc(staged, 1)
        nc.gpsimd.tensor_copy(st_rec[:, h, 0:count, :].rearrange("p c f -> p (c f)"),
                              rec[:, bass.ds(first * 2, 2 * count)]).then_inc(staged, 1)
        pool.wait_ge(staged, stage_count)
        apart(nc, m)
        for j in range(count):
            nc.gpsimd.indirect_dma_start(
                out=m.sorted, out_offset=bass.IndirectOffsetOnAxis(ap=st_addr[:, h, j:j + 1], axis=0),
                in_=st_rec[:, h, j, :], in_offset=None).then_inc(scattered[h], 16)

    with nc.Block() as block:

        @block.sync
        def _(sp):
            sp.wait_ge(pads_set, 3)
            for src, to in ((a["src"], src_i), (a["dst"], dst_i), (a["edge_weight"], ew)):
                for lo, hi in ((0, 112), (112, P - 1)):
                    sp.dma_start(to[lo:hi, :], src[lo * EC:hi * EC].rearrange("(p c) -> p c", c=EC)).then_inc(edges_in, 16)
                sp.dma_start(to[P - 1:P, 0:TAIL], src[(P - 1) * EC:E].rearrange("(p c) -> p c", c=TAIL)).then_inc(edges_in, 16)
            sp.wait_ge(zeroed, 1)
            sp.dma_start(m.sorted.rearrange("(p c) f -> p (c f)", p=P), zeros[:, 0:2 * CHUNKS]).then_inc(sorted_zero, 16)
            for c in range(5):
                sp.dma_start(m.x[0:T, 10 * c:10 * c + 10, 0:D], x_dram[:, 10 * c:10 * c + 10, :]).then_inc(x_in, 16)
            for n, name in enumerate(("L0_gnn_W", "L0_mix_wk", "L0_mix_wv", "L0_mix_wq", "L0_mix_wo")):
                sp.dma_start(m.w[:, n, :, :], a[name].rearrange("(k p) n -> p k n", p=P)).then_inc(x_in, 16)
            for name, src in (("bk", a["L0_mix_bk"]), ("bv", a["L0_mix_bv"]), ("bo", a["L0_mix_bo"]),
                              ("bk1", a["L1_mix_b_qkv"][D:2 * D]), ("bv1", a["L1_mix_b_qkv"][2 * D:3 * D]),
                              ("fc2", a["L1_mix_b_fc2"]), ("gnn_b2", a["L1_gnn_b2"])):
                sp.dma_start(m.row_bias[:, ROW[name], :], src.rearrange("(a d) -> a d", a=1).to_broadcast([P, D])).then_inc(x_in, 16)
            for name, src, n in (("bq", a["L0_mix_bq"], 2), ("gnn_b", a["L1_gnn_b"], 2), ("gnn_b1", a["L1_gnn_b1"], 2),
                                 ("bq1", a["L1_mix_b_qkv"][0:D], 2), ("norm_g", a["L1_mix_norm_g"], 2),
                                 ("norm_b", a["L1_mix_norm_b"], 2), ("fc1", a["L1_mix_b_fc1"], 6),
                                 ("router_b1", a["L1_ffn_router_b1"], 1)):
                with nc.allow_non_contiguous_dma(reason="a bias, one channel in each partition"):
                    sp.dma_start(m.col_bias[:, COL[name]:COL[name] + n], src.rearrange("(h p) -> p h", p=P)).then_inc(x_in, 16)
            sp.wait_ge(of_ready, 1)
            sp.dma_start(m.chunk_dram.rearrange("(p j) -> p j", p=P), of_i).then_inc(of_out, 16)
            sp.wait_ge(of_out, 16)
            sp.dma_start(m.blk[:, :], m.chunk_dram.rearrange("(a c) -> a c", a=1)).then_inc(of_in, 16)
            sp.wait_ge(of_in, 16)
            to = m.table[0].rearrange("(t p) d -> p t d", p=T)
            with sp.Fori(0, G) as g:
                sp.wait_ge(table_ready, g + 1)
                sp.dma_start(to[:, bass.ds(g * 2, 2), :], table_sb[0:T, :, :]).then_inc(table_out, 16)
            sp.wait_ge(table_out, 16 * G)

        @block.gpsimd
        def _(pool):
            nc.gpsimd.iota(m.iota_i[:, :], [[1, P]], base=0, channel_multiplier=0).then_inc(made, 1)
            nc.gpsimd.memset(m.ident[:, :], 0.0).then_inc(made, 1)
            nc.gpsimd.memset(ones, 1.0).then_inc(made, 1)
            nc.gpsimd.memset(m.x[:, :, D:D + 1], 0.0).then_inc(made, 1)
            nc.gpsimd.iota(of_i, [[1, KC]], base=0, channel_multiplier=KC).then_inc(made, 1)
            pool.wait_ge(made, 5)
            nc.gpsimd.tensor_copy(m.iota[:, :], m.iota_i[:, :]).then_inc(made, 1)
            nc.gpsimd.tensor_copy(at, of_i).then_inc(made, 1)
            nc.gpsimd.affine_select(out=m.ident[:, :], in_=m.ident[:, :], compare_op=ALU.not_equal, fill=1.0,
                                    base=0, pattern=[[-1, P]], channel_multiplier=1).then_inc(made, 1)
            nc.gpsimd.affine_select(out=tri, in_=ones, compare_op=ALU.is_ge, fill=0.0,
                                    base=-1, pattern=[[1, P]], channel_multiplier=-1).then_inc(made, 1)
            nc.gpsimd.memset(zeros, 0.0).then_inc(zeroed, 1)
            pool.wait_ge(sorted_zero, 16)
            pool.wait_ge(placed, 1)
            trips, first = EC // (2 * SC), FIRST // (2 * SC)
            for lo, hi in ((0, first), (first, trips)):
                if lo:
                    pool.wait_ge(placed, 2)
                with pool.Fori(lo, hi) as i:
                    for h in range(2):
                        pool.wait_ge(scattered[h], i * (16 * SC))
                        scatter(pool, i * (2 * SC) + h * SC, h, SC, i * 4 + 2 * (h + 1))
            left = EC - trips * 2 * SC
            for h in range(2):
                count = min(SC, left - h * SC)
                if count > 0:
                    pool.wait_ge(scattered[h], trips * 16 * SC)
                    scatter(pool, trips * 2 * SC + h * SC, h, count, trips * 4 + 2 * (h + 1))
            pool.wait_ge(scattered[0], 16 * (trips * SC + min(SC, left)))
            pool.wait_ge(scattered[1], 16 * (trips * SC + max(0, left - SC)))

        @block.vector
        def _(dve):
            chain = m.chain
            nc.vector.memset(src_i[:, TAIL:EC], N - 1).then_inc(pads_set, 1)
            nc.vector.memset(dst_i[:, TAIL:EC], 0).then_inc(pads_set, 1)
            nc.vector.memset(ew[:, TAIL:EC], 0.0).then_inc(pads_set, 1)
            dve.wait_ge(made, 9)
            dve.wait_ge(edges_in, 16 * 9)
            chain.link(nc.vector.tensor_copy(mask, src_i))
            chain.link(nc.vector.tensor_scalar(blk, mask, 1.0 / T, 0.5 / T - 0.5, ALU.mult, ALU.add))
            chain.link(nc.vector.tensor_scalar(blk, blk, MAGIC, None, ALU.add))
            chain.link(nc.vector.tensor_scalar(blk, blk, -MAGIC, None, ALU.add))
            chain.link(nc.vector.scalar_tensor_tensor(loc, blk, -float(T), mask, ALU.mult, ALU.add))
            with dve.Fori(0, NT) as b:
                chain.begin(b, 1)
                chain.link(nc.vector.tensor_scalar(mask, blk, m.iota[:, bass.ds(b, 1)], None, ALU.is_equal, ALU.add,
                                                   accum_out=cnt[:, bass.ds(b, 1)]))
                chain.end(NT)
            nc.vector.memset(small[:, 5 * NT:5 * NT + 1], 0.0).then_inc(counted, 1)
            dve.wait_ge(totalled, 1)
            chain.link(nc.vector.tensor_scalar(chunks, m.ps[:, 1, 0:NT], 1.0 / P, (P - 1.0) / P - 0.5 + 0.5 / P, ALU.mult, ALU.add))
            chain.link(nc.vector.tensor_scalar(chunks, chunks, MAGIC, None, ALU.add))
            chain.link(nc.vector.tensor_scalar(chunks, chunks, -MAGIC, None, ALU.add))
            chain.link(nc.vector.tensor_tensor_scan(incl, chunks, chunks, 0.0, ALU.add, ALU.bypass))
            chain.link(nc.vector.tensor_tensor(start, incl, chunks, ALU.subtract))
            chain.link(nc.vector.scalar_tensor_tensor(base, start, float(P), m.ps[:, 0, 0:NT], ALU.mult, ALU.add))
            chain.link(nc.vector.tensor_scalar(base, base, -1.0, None, ALU.add))
            chain.link(nc.vector.tensor_tensor(flag, start.unsqueeze(1).to_broadcast([P, KC, NT]),
                                               at.unsqueeze(2).to_broadcast([P, KC, NT]), ALU.is_le))
            chain.link(nc.vector.tensor_reduce(of, flag, AX.X, ALU.add))
            chain.link(nc.vector.tensor_scalar(of, of, -1.0, None, ALU.add))
            nc.vector.tensor_copy(of_i, of).then_inc(of_ready, 1)
            dve.wait_ge(sorted_zero, 16)
            for lo, hi in ((0, FIRST), (FIRST, EC)):
                cols = slice(lo, hi)
                with dve.Fori(0, NT) as b:
                    chain.begin(b, 4)
                    chain.link(nc.vector.tensor_scalar(mask[:, cols], blk[:, cols], m.iota[:, bass.ds(b, 1)], None, ALU.is_equal))
                    chain.link(nc.vector.tensor_tensor_scan(scan[:, cols], mask[:, cols], mask[:, cols], base[:, bass.ds(b, 1)], ALU.add, ALU.bypass))
                    chain.did(nc.vector.tensor_scalar(base[:, bass.ds(b, 1)], scan[:, hi - 1:hi], 0.0, None, ALU.add))
                    chain.apart()
                    chain.link(nc.vector.copy_predicated(pos[:, cols], mask[:, cols].bitcast(U32), scan[:, cols]))
                    chain.end(NT)
                low, high, to = mask[:, cols].bitcast(I32), scan[:, cols].bitcast(I32), addr[:, cols]
                chain.link(nc.vector.tensor_copy(to, pos[:, cols]))
                chain.did(nc.vector.tensor_scalar(high, to, 7, None, ALU.arith_shift_right))
                chain.link(nc.vector.tensor_scalar(low, to, P - 1, None, ALU.bitwise_and))
                chain.link(nc.vector.scalar_tensor_tensor(to, low, float(CHUNKS), high, ALU.mult, ALU.add))
                chain.link(nc.vector.tensor_copy(pos[:, cols], dst_i[:, cols]))
                chain.did(nc.vector.scalar_tensor_tensor(rec2[:, cols, 0], pos[:, cols], float(P), loc[:, cols], ALU.mult, ALU.add))
                chain.link(nc.vector.tensor_copy(rec2[:, cols, 1], ew[:, cols]))
                nc.vector.memset(m.mv[0:1, 0, 0:1], 0.0).then_inc(placed, 1)
                dve.wait_ge(placed, 1 if lo == 0 else 2)
            dve.wait_ge(x_in, 16 * X_LOADS)
            chain.did(nc.vector.memset(same, 0.0))
            for k in range(2):
                for h in range(2):
                    chain.did(nc.vector.memset(v[:, k, 129 * h + P:129 * h + P + 1], 1.0))
            chain.settle()
            for b in range(4):
                chain.did(nc.vector.memset(same[32 * b:32 * b + 32, 32 * b:32 * b + 32], 1.0))
            chain.did(nc.vector.memset(table_sb[:, 0, :], 0.0))
            chain.settle()
            nc.vector.memset(table_sb[:, 1, :], 0.0).then_inc(set_up, 1)
            norm_stats(nc, dve, chain, m)
            with dve.Fori(0, G) as g:
                chain.begin(g, 1)
                dve.wait_ge(tp_done, g)
                for k in range(2):
                    normalise(nc, m, xn[0:T, k, :], g, k).then_inc(xn_ready, 1)
                dve.wait_ge(proj, g * 3 + 2)
                dve.wait_ge(kv_done, g)
                chain.link(nc.vector.tensor_tensor(kb[0:T, :, :], ps[0:T, 2, :].rearrange("p (k d) -> p k d", k=2),
                                                   m.row_bias[0:T, ROW["bk"], :].unsqueeze(1).to_broadcast([T, 2, D]), ALU.add))
                nc.vector.tensor_scalar(kf[0:T, :, :], kb[0:T, :, :], 0.0, None, ALU.min).then_inc(km_ready, 1)
                dve.wait_ge(proj, g * 3 + 3)
                for h in range(2):
                    nc.vector.tensor_tensor(v[0:T, :, 129 * h:129 * h + P],
                                            ps[0:T, 3, :].rearrange("p (k d) -> p k d", k=2)[:, :, h * P:(h + 1) * P],
                                            m.row_bias[0:T, ROW["bv"], h * P:(h + 1) * P].unsqueeze(1).to_broadcast([T, 2, P]),
                                            ALU.add).then_inc(v_ready, 1)
                dve.wait_ge(ke_ready, g + 1)
                nc.vector.scalar_tensor_tensor(kf[0:T, :, :], kb[0:T, :, :], 0.0, ke[0:T, :, :], ALU.max, ALU.add).then_inc(kf_ready, 1)
                chain.end(G)
            dve.wait_ge(kv_done, G)
            for h in range(2):
                nc.vector.tensor_tensor(kvd[:, h, :], ps[:, 4, 129 * h:129 * h + P], same, ALU.mult).then_inc(kvd_ready, 1)
                nc.vector.tensor_scalar(ksd[:, h, :], same, ps[:, 4, 129 * h + P:129 * h + P + 1], None, ALU.mult).then_inc(kvd_ready, 1)
            with dve.Fori(0, G) as g:
                chain.begin(g, 5)
                dve.wait_ge(qtp, g)
                for k in range(2):
                    normalise(nc, m, xn[0:T, k, :], g, k).then_inc(qxn, 1)
                dve.wait_ge(q_done, g + 1)
                for h in range(2):
                    nc.vector.tensor_scalar(qm[:, h, :], ps[:, 2, h * GN:(h + 1) * GN], bq[h], 0.0, ALU.add, ALU.min).then_inc(qm_ready, 1)
                dve.wait_ge(o_done, g)
                for h in range(2):
                    chain.did(nc.vector.tensor_scalar(qf[:, h, :], ps[:, 2, h * GN:(h + 1) * GN], bq[h], 0.0, ALU.add, ALU.max))
                chain.settle()
                dve.wait_ge(qe_ready, g + 1)
                nc.vector.tensor_tensor(qf, qf, qe, ALU.add).then_inc(qf_ready, 1)
                dve.wait_ge(o_done, g + 1)
                chain.link(nc.vector.tensor_scalar(rn, ps[:, 6, 0:2 * GN].rearrange("p (h c) -> p h c", h=2), 1e-6, None, ALU.add))
                chain.link(nc.vector.reciprocal(rn, rn))
                dve.wait_ge(y_done, g)
                nc.vector.tensor_tensor(oT, ps[:, 5, 0:2 * GN].rearrange("p (h c) -> p h c", h=2), rn, ALU.mult).then_inc(oT_ready, 1)
                xg = m.x[0:T, bass.ds(g * 2, 2), 0:D]
                dve.wait_ge(y_done, g + 1)
                chain.link(nc.vector.tensor_tensor(xg, xg, ps[0:T, 7, :].rearrange("p (k d) -> p k d", k=2), ALU.add))
                nc.vector.tensor_tensor(xg, xg, m.row_bias[0:T, ROW["bo"], :].unsqueeze(1).to_broadcast([T, 2, D]), ALU.add).then_inc(y_added, 1)
                chain.end(G)

        @block.scalar
        def _(act):
            with act.Fori(0, G) as g:
                act.wait_ge(tp_done, g + 1)
                act.wait_ge(proj, g * 3)
                nc.scalar.copy(xT, ps[:, 0, 0:2 * GN].rearrange("p (h c) -> p h c", h=2)).then_inc(xT_ready, 1)
                act.wait_ge(proj, g * 3 + 1)
                act.wait_ge(table_out, g * 16)
                nc.scalar.copy(table_sb[0:T, :, :], ps[0:T, 1, :].rearrange("p (k d) -> p k d", k=2)).then_inc(table_ready, 1)
                act.wait_ge(km_ready, g + 1)
                nc.scalar.activation(ke[0:T, :, :], kf[0:T, :, :], ACT.Exp).then_inc(ke_ready, 1)
            act.wait_ge(table_out, 16 * G)
            with act.Fori(0, G) as g:
                act.wait_ge(qtp, g + 1)
                act.wait_ge(q_done, g)
                nc.scalar.copy(xT, ps[:, 0, 0:2 * GN].rearrange("p (h c) -> p h c", h=2)).then_inc(qxT, 1)
                act.wait_ge(qm_ready, g * 2 + 2)
                nc.scalar.activation(qe, qm, ACT.Exp).then_inc(qe_ready, 1)

        @block.tensor
        def _(pe):
            pe.wait_ge(made, 9)
            pe.wait_ge(counted, 1)
            nc.tensor.matmul(m.ps[:, 0, 0:NT], tri, cnt, start=True, stop=True)
            nc.tensor.matmul(m.ps[:, 1, 0:NT], ones, cnt, start=True, stop=True).then_inc(totalled, 1)
            pe.wait_ge(x_in, 16 * X_LOADS)
            pe.wait_ge(set_up, 1)
            nc.tensor.matmul(ps[:, 4, 0:258], table_sb[:, 0, 0:P], table_sb[:, :, :].rearrange("p a b -> p (a b)")[:, 0:258],
                             start=True, stop=False, skip_group_check=True)
            with pe.Fori(0, G) as g:
                pe.wait_ge(xn_ready, g * 2 + 2)
                pe.wait_ge(xT_ready, g)
                transpose_group(nc, m, 0, xn).then_inc(tp_done, 1)
                pe.wait_ge(xT_ready, g + 1)
                pe.wait_ge(table_ready, g)
                for n in range(3):
                    if n == 1:
                        pe.wait_ge(km_ready, g)
                    if n == 2:
                        pe.wait_ge(v_ready, 2 * g)
                    for k in range(2):
                        last = rows_times(nc, ps[0:T, 1 + n, k * D:(k + 1) * D], lambda h: xT[:, h, k * T:(k + 1) * T],
                                          lambda h: m.w[:, n, h, :])
                    last.then_inc(proj, 1)
                pe.wait_ge(kf_ready, g + 1)
                pe.wait_ge(v_ready, 2 * g + 2)
                for k in range(2):
                    for h in range(2):
                        last = nc.tensor.matmul(ps[:, 4, 129 * h:129 * h + 129], kf[0:T, k, h * P:(h + 1) * P],
                                                v[0:T, k, 129 * h:129 * h + 129], start=False, stop=False, skip_group_check=True)
                last.then_inc(kv_done, 1)
            pe.wait_ge(kvd_ready, 4)
            with pe.Fori(0, G) as g:
                pe.wait_ge(qxn, g * 2 + 2)
                pe.wait_ge(qxT, g)
                transpose_group(nc, m, 0, xn).then_inc(qtp, 1)
                pe.wait_ge(qxT, g + 1)
                pe.wait_ge(qf_ready, g)
                for o in range(2):
                    for h in range(2):
                        last = nc.tensor.matmul(ps[:, 2, o * GN:(o + 1) * GN], m.w[:, 3, h, o * P:(o + 1) * P], xT[:, h, :],
                                                start=h == 0, stop=h == 1)
                last.then_inc(q_done, 1)
                pe.wait_ge(qf_ready, g + 1)
                pe.wait_ge(oT_ready, g)
                for bank, mat in ((5, kvd), (6, ksd)):
                    for h in range(2):
                        last = nc.tensor.matmul(ps[:, bank, h * GN:(h + 1) * GN], mat[:, h, :], qf[:, h, :], start=True, stop=True)
                last.then_inc(o_done, 1)
                pe.wait_ge(oT_ready, g + 1)
                pe.wait_ge(y_added, g)
                for k in range(2):
                    last = rows_times(nc, ps[0:T, 7, k * D:(k + 1) * D], lambda h: oT[:, h, k * T:(k + 1) * T],
                                      lambda h: m.w[:, 4, h, :])
                last.then_inc(y_done, 1)


def mix1(nc, m, sem):
    W, ps = m.work, m.ps
    xn, xT, k_sb, v_sb = W[:, 0:2, :], W[:, 2:4, 0:GN], W[:, 4:6, :], W[:, 6:8, :]
    qT, x2, ln, hT = W[:, 4:6, 0:GN], W[:, 6:8, :], W[:, 8:10, :], W[:, 10:12, 0:GN]
    h1 = W[:, 12:18, 0:GN]
    logit, prob = W[:, 18, 0:P].rearrange("p (h e) -> p h e", h=2), W[:, 18, P:2 * P].rearrange("p (h e) -> p h e", h=2)
    diag, attnT = W[:, 19, :].rearrange("p (h e) -> p h e", h=2), W[:, 20, :].rearrange("p (h e) -> p h e", h=2)
    zero = W[:, 21, :]
    rs, mx, sm = m.small[0:T, 8:10], m.small[:, 14:16], m.small[:, 16:18]
    names = ("set xn tp xT k v k_sb v_sb kv logits exp attn attn_tp attnT bxn btp bxT q qT xf x2 ln ln_tp hT fc1 h1 fc2").split()
    s = {n: sem(f"mix1_{n}") for n in names}
    col = lambda name, h: m.col_bias[:, COL[name] + h:COL[name] + h + 1]
    both = lambda bank: ps[0:T, bank, :].rearrange("p (k d) -> p k d", k=2)
    halves = lambda bank: ps[:, bank, 0:2 * GN].rearrange("p (h c) -> p h c", h=2)
    row = lambda name: m.row_bias[0:T, ROW[name], :].unsqueeze(1).to_broadcast([T, 2, D])
    second = G * RING
    last_chunks = second + G * 3 * RING

    def vector(dve, half):
        chain = m.chain
        nc.vector.memset(zero, 0.0).then_inc(s["set"], 1)
        nc.vector.memset(diag, 0.0).then_inc(s["set"], 1)
        with dve.Fori(0, G) as g:
            dve.wait_ge(s["tp"], g)
            for k in range(2):
                normalise(nc, m, xn[0:T, k, :], g, k).then_inc(s["xn"], 1)
            half(g * RING, 0)
            for bank, to, name, bias in ((3, k_sb, "k", "bk1"), (5, v_sb, "v", "bv1")):
                dve.wait_ge(s["kv"], g)
                dve.wait_ge(s[name], g + 1)
                nc.vector.tensor_tensor(to[0:T, :, :], both(bank), row(bias), ALU.add).then_inc(s[name + "_sb"], 1)
            half(g * RING, 1)
        dve.wait_ge(s["kv"], G)
        for h in range(2):
            for b in range(2):
                chain.did(nc.vector.tensor_copy(logit[64 * b:64 * b + 64, h, :],
                                                ps[64 * b:64 * b + 64, 4, h * P + 64 * b:h * P + 64 * b + 64]))
        chain.settle()
        chain.link(nc.vector.tensor_reduce(mx, logit, AX.X, ALU.max))
        nc.vector.tensor_tensor(logit, logit, mx.unsqueeze(2).to_broadcast([P, 2, 64]), ALU.subtract).then_inc(s["logits"], 1)
        dve.wait_ge(s["exp"], 1)
        chain.link(nc.vector.tensor_reduce(sm, prob, AX.X, ALU.add))
        chain.link(nc.vector.reciprocal(sm, sm))
        dve.wait_ge(s["set"], 2)
        for h in range(2):
            for b in range(2):
                lo, hi = 64 * b, 64 * b + 64
                nc.vector.tensor_scalar(diag[lo:hi, h, lo:hi], prob[lo:hi, h, :], sm[lo:hi, h:h + 1], None, ALU.mult).then_inc(s["attn"], 1)
        with dve.Fori(0, G) as g:
            chain.begin(g, 1 + STATS_STEPS + 3)
            dve.wait_ge(s["btp"], g)
            dve.wait_ge(s["x2"], g)
            for k in range(2):
                normalise(nc, m, xn[0:T, k, :], g, k).then_inc(s["bxn"], 1)
            base = g * (3 * RING) + second
            half(base, 0)
            dve.wait_ge(s["xf"], g + 1)
            dve.wait_ge(s["bxn"], g * 2 + 2)
            chain.link(nc.vector.tensor_tensor(x2[0:T, :, :], both(3), xn[0:T, :, :], ALU.add))
            group_stats(nc, chain, m, [x2[0:T, k, :] for k in range(2)], rs)
            dve.wait_ge(s["ln_tp"], g)
            for k in range(2):
                nc.vector.tensor_scalar(ln[0:T, k, :], x2[0:T, k, :], m.mv[0:T, k, 0:1], rs[:, k:k + 1],
                                        ALU.subtract, ALU.mult).then_inc(s["ln"], 1)
            xg = m.x[0:T, bass.ds(g * 2, 2), 0:D]
            dve.wait_ge(s["ln"], 2 * g + 2)
            chain.link(nc.vector.tensor_tensor(x2[0:T, :, :], x2[0:T, :, :], row("fc2"), ALU.add))
            chain.link(nc.vector.tensor_tensor(xg, xg, x2[0:T, :, :], ALU.add))
            for n in (1, 2, 3):
                half(base, n)
            dve.wait_ge(s["fc2"], g + 1)
            chain.link(nc.vector.tensor_tensor(xg, xg, both(3), ALU.add))
            nc.vector.memset(m.small[0:1, 20:21], 0.0).then_inc(s["x2"], 1)
            half(base, 4)
            half(base, 5)
            chain.end(G)
        half(last_chunks, 0)
        half(last_chunks, 1)

    def scalar(act):
        with act.Fori(0, G) as g:
            act.wait_ge(s["tp"], g + 1)
            act.wait_ge(s["v"], g)
            nc.scalar.copy(xT, halves(2)).then_inc(s["xT"], 1)
        act.wait_ge(s["logits"], 1)
        nc.scalar.activation(prob, logit, ACT.Exp, scale=64.0 ** -0.5).then_inc(s["exp"], 1)
        act.wait_ge(s["attn_tp"], 1)
        nc.scalar.copy(attnT, ps[:, 3, 0:2 * P].rearrange("p (h e) -> p h e", h=2)).then_inc(s["attnT"], 1)
        with act.Fori(0, G) as g:
            act.wait_ge(s["btp"], g + 1)
            act.wait_ge(s["q"], g)
            nc.scalar.copy(xT, halves(2)).then_inc(s["bxT"], 1)
            act.wait_ge(s["q"], g + 1)
            act.wait_ge(s["xf"], g)
            for h in range(2):
                nc.scalar.activation(qT[:, h, :], halves(3)[:, h, :], ACT.Identity, bias=col("bq1", h)).then_inc(s["qT"], 1)
            act.wait_ge(s["ln_tp"], g + 1)
            act.wait_ge(s["fc1"], 3 * g)
            for h in range(2):
                nc.scalar.activation(hT[:, h, :], halves(2)[:, h, :], ACT.Identity, bias=col("norm_b", h),
                                     scale=col("norm_g", h)).then_inc(s["hT"], 1)
            act.wait_ge(s["fc2"], g)
            for o in range(6):
                act.wait_ge(s["fc1"], 3 * g + o // 2 + 1)
                nc.scalar.activation(h1[:, o, :], halves(4 + o // 2 % 2)[:, o % 2, :], ACT.Gelu, bias=col("fc1", o)).then_inc(s["h1"], 1)

    def tensor(pe, products):
        pe.wait_ge(s["set"], 2)
        nc.tensor.matmul(ps[:, 4, 0:D], zero[:, 0:P], zero, start=True, stop=False, skip_group_check=True)
        with pe.Fori(0, G) as g:
            pe.wait_ge(s["xn"], g * 2 + 2)
            pe.wait_ge(s["xT"], g)
            transpose_group(nc, m, 2, xn).then_inc(s["tp"], 1)
            products(g * RING, 0, 0, 4)
            pe.wait_ge(s["xT"], g + 1)
            for n, bank, name in ((1, 3, "k"), (2, 5, "v")):
                pe.wait_ge(s[name + "_sb"], g)
                for k in range(2):
                    last = rows_times(nc, ps[0:T, bank, k * D:(k + 1) * D], lambda h: xT[:, h, k * T:(k + 1) * T],
                                      lambda h: m.w[:, 3 + n, h, :])
                last.then_inc(s[name], 1)
            products(g * RING, 0, 4, 8)
            products(g * RING, 1, 0, 2)
            pe.wait_ge(s["k_sb"], g + 1)
            pe.wait_ge(s["v_sb"], g + 1)
            for k in range(2):
                for h in range(2):
                    last = nc.tensor.matmul(ps[:, 4, h * P:(h + 1) * P], k_sb[0:T, k, h * P:(h + 1) * P],
                                            v_sb[0:T, k, h * P:(h + 1) * P], start=False, stop=False, skip_group_check=True)
            last.then_inc(s["kv"], 1)
            products(g * RING, 1, 2, 8)
        pe.wait_ge(s["attn"], 4)
        for h in range(2):
            last = nc.tensor.transpose(ps[:, 3, h * P:(h + 1) * P], diag[:, h, :], m.ident[:, :])
        last.then_inc(s["attn_tp"], 1)
        pe.wait_ge(s["attnT"], 1)
        with pe.Fori(0, G) as g:
            pe.wait_ge(s["bxn"], g * 2 + 2)
            pe.wait_ge(s["hT"], 2 * g)
            base = g * (3 * RING) + second
            transpose_group(nc, m, 2, xn).then_inc(s["btp"], 1)
            products(base, 0, 0, 4)
            pe.wait_ge(s["bxT"], g + 1)
            pe.wait_ge(s["x2"], g)
            for o in range(2):
                for h in range(2):
                    last = nc.tensor.matmul(ps[:, 3, o * GN:(o + 1) * GN], m.w[:, 3, h, o * P:(o + 1) * P], xT[:, h, :],
                                            start=h == 0, stop=h == 1)
            last.then_inc(s["q"], 1)
            products(base, 0, 4, 8)
            pe.wait_ge(s["qT"], 2 * g + 2)
            for k in range(2):
                for h in range(2):
                    last = nc.tensor.matmul(ps[0:T, 3, k * D + h * P:k * D + (h + 1) * P], qT[:, h, k * T:(k + 1) * T],
                                            attnT[:, h, :], start=True, stop=True)
            last.then_inc(s["xf"], 1)
            products(base, 1)
            pe.wait_ge(s["ln"], 2 * g + 2)
            transpose_group(nc, m, 2, ln).then_inc(s["ln_tp"], 1)
            products(base, 2, 0, 4)
            pe.wait_ge(s["hT"], 2 * g + 2)
            for o in range(6):
                if o % 2 == 0:
                    pe.wait_ge(s["h1"], 6 * g + (2 if o == 4 else 0))
                for h in range(2):
                    last = nc.tensor.matmul(halves(4 + o // 2 % 2)[:, o % 2, :], m.w[:, 6 + o // 2, h, (o % 2) * P:(o % 2 + 1) * P],
                                            hT[:, h, :], start=h == 0, stop=h == 1)
                if o % 2:
                    last.then_inc(s["fc1"], 1)
                if o in (1, 3):
                    products(base, 2, 3 + o, 5 + o)
            products(base, 3)
            pe.wait_ge(s["h1"], 6 * g + 6)
            pe.wait_ge(s["x2"], g)
            for k in range(2):
                for c in range(6):
                    last = nc.tensor.matmul(ps[0:T, 3, k * D:(k + 1) * D], h1[:, c, k * T:(k + 1) * T],
                                            m.w[:, 9 + c // 2, c % 2, :], start=c == 0, stop=c == 5)
            last.then_inc(s["fc2"], 1)
            products(base, 4)
            products(base, 5)
        products(last_chunks, 0)
        products(last_chunks, 1)
    return {"vector": vector, "scalar": scalar, "tensor": tensor}


def gather_sums(nc, m, sem, a, layer):
    width = D + 1 if layer == 0 else D
    into = m.x if layer == 0 else m.acc
    banks = (0, 1, 6, 7)
    raw = m.flat[:, 2 * E0 * 2 * D:2 * E0 * 2 * D + 2 * CHUNKS]
    raw_v = raw.rearrange("p (c f) -> p c f", f=2)
    spare = m.work[:, :, :].rearrange("p a b -> p (a b)")
    vi, lo = spare[:, 0:CHUNKS].bitcast(I32), spare[:, CHUNKS:2 * CHUNKS].bitcast(I32)
    loaded, decoded, ones_set, idx_in = sem(f"loaded{layer}"), sem(f"decoded{layer}"), sem(f"ones_set{layer}"), sem(f"idx{layer}")
    row_in, before = m.row_in, 16 * (CHUNKS // RING) * layer
    hot_ready, summed, bank_free = sem(f"hot{layer}"), sem(f"chunk_sum{layer}"), sem(f"bank_free{layer}")
    trips = CHUNKS // RING
    assert trips % 2 == 1
    mix = mix1(nc, m, sem) if layer else None
    with nc.Block() as block:

        @block.sync
        def _(sp):
            if layer == 0:
                sp.dma_start(raw, m.sorted.rearrange("(p c) f -> p (c f)", p=P)).then_inc(loaded, 16)
                sp.wait_ge(loaded, 16)
                for n, name in enumerate(("L0_ffn_w1", "L0_ffn_w2")):
                    sp.dma_start(m.flat[:, n * E0 * 2 * D:(n + 1) * E0 * 2 * D].rearrange("p (e n) -> p e n", n=D),
                                 a[name].rearrange("e (k p) n -> p (e k) n", p=P)).then_inc(loaded, 16)
                sp.wait_ge(loaded, 48)
            else:
                rows = m.table[1].rearrange("(t p) d -> p t d", p=T)
                for n in range(5):
                    sp.dma_start(m.acc[0:T, 10 * n:10 * n + 10, :], rows[:, 10 * n:10 * n + 10, :]).then_inc(loaded, 16)
                sp.wait_ge(loaded, 80)

        @block.gpsimd
        def _(pool):
            nc.gpsimd.memset(m.rows[:, :, D:D + 1], 1.0).then_inc(ones_set, 1)
            pool.wait_ge(decoded, 1)

            def fetch(i, h, used):
                if used is not None:
                    pool.wait_ge(summed, used)
                nc.gpsimd.tensor_copy(m.idx[:, h % 4, :], m.dst[:, bass.ds(i * 4 * HALF + h * HALF, HALF)]).then_inc(idx_in, 1)
                pool.wait_ge(idx_in, i * 4 + h + 1)
                apart(nc, m)
                for j in range(HALF):
                    s = (h % 2) * HALF + j
                    if used is not None and j == HALF // 2:
                        pool.wait_ge(summed, used + HALF // 2)
                        apart(nc, m)
                    nc.gpsimd.indirect_dma_start(
                        out=m.rows[:, s, 0:D], out_offset=None, in_=m.table[layer],
                        in_offset=bass.IndirectOffsetOnAxis(ap=m.idx[:, h % 4, j:j + 1], axis=0)).then_inc(row_in[s], 16)

            fetch(0, 0, None)
            fetch(0, 1, None)
            with pool.Fori(0, (trips - 1) // 2) as i:
                for h in range(2, 6):
                    fetch(i, h, i * 4 * HALF + (h - 2) * HALF + HALF // 2)
            for s in range(RING):
                pool.wait_ge(row_in[s], 16 * trips + before)

        @block.vector
        def _(dve):
            chain = m.chain
            if layer == 0:
                dve.wait_ge(loaded, 16)
                chain.did(nc.vector.memset(m.lew[:, CHUNKS:CHUNKS + HALF, :], 0.0))
                chain.link(nc.vector.tensor_copy(vi, raw_v[:, :, 0]))
                chain.did(nc.vector.tensor_scalar(lo, vi, P - 1, None, ALU.bitwise_and))
                chain.did(nc.vector.tensor_scalar(m.dst, vi, 7, None, ALU.arith_shift_right))
                chain.settle()
                chain.did(nc.vector.tensor_copy(m.lew[:, 0:CHUNKS, 0], lo))
                chain.did(nc.vector.tensor_copy(m.lew[:, 0:CHUNKS, 1], raw_v[:, :, 1]))
                chain.settle()
            for b in range(len(banks)):
                nc.vector.memset(m.small[0:1, b:b + 1], 0.0).then_inc(bank_free, 1)
            nc.vector.memset(m.small[0:1, 4:5], 0.0).then_inc(decoded, 1)

            def build(base, n, j):
                c = base + (n * HALF + j)
                nc.vector.tensor_scalar(m.hot[:, (n % 2) * HALF + j, :], m.iota[:, 0:T],
                                        m.lew[:, bass.ds(c, 1), 0], m.lew[:, bass.ds(c, 1), 1],
                                        ALU.is_equal, ALU.mult).then_inc(hot_ready, 1)

            def half(base, n):
                nc.vector.reg_load(regs, m.blk[0:1, bass.ds(base + n * HALF, HALF)])
                dve.wait_ge(summed, base + n * HALF)
                for j in range(HALF):
                    build(base, n + 1, j)
                    t = nc.vector.snap(regs[j], min_val=0, max_val=NT - 1)
                    c = base + (n * HALF + j)
                    dve.wait_ge(summed, c + 1)
                    dve.wait_ge(bank_free, c + len(banks))
                    to = tile_of(into, t, width)
                    nc.vector.tensor_tensor(to, to, m.ps[0:T, banks[j % 4], 0:width], ALU.add).then_inc(bank_free, 1)

            regs = [nc.vector.alloc_register(f"tile{layer}_{j}") for j in range(HALF)]
            for j in range(HALF):
                build(0, 0, j)
            if layer == 0:
                with dve.Fori(0, trips) as i:
                    half(i * RING, 0)
                    half(i * RING, 1)
            else:
                dve.wait_ge(loaded, 80)
                mix["vector"](dve, half)
            for r in regs:
                nc.vector.free_register(r)

        if layer:
            @block.scalar
            def _(act):
                mix["scalar"](act)

        @block.tensor
        def _(pe):
            pe.wait_ge(ones_set, 1)

            def products(base, n, lo=0, hi=HALF):
                for j in range(lo, hi):
                    c, s = base + (n * HALF + j), (n % 2) * HALF + j
                    pe.wait_ge(row_in[s], base + (n // 2) * RING + 16 + before)
                    pe.wait_ge(hot_ready, c + 1)
                    pe.wait_ge(bank_free, c + 1)
                    nc.tensor.matmul(m.ps[0:T, banks[j % 4], 0:width], m.hot[:, s, :], m.rows[:, s, 0:width],
                                     start=True, stop=True).then_inc(summed, 1)

            if layer == 0:
                with pe.Fori(0, trips) as i:
                    products(i * RING, 0)
                    products(i * RING, 1)
            else:
                mix["tensor"](pe, products)


def experts(nc, m, sem, a, layer, out=None):
    EX, DEEP = (E0, 2) if layer == 0 else (E1, 3)
    W, ps = m.work, m.ps
    w = (m.flat if layer == 0 else m.region)[:, 0:EX * DEEP * 2 * D].rearrange("p (e k n) -> p e k n", k=KD, n=D)
    xn, xT = W[:, 0:2, :], W[:, 2:4, 0:GN]
    hid = [W[:, 4 + 2 * i:6 + 2 * i, 0:GN] for i in range(2)]
    hid2 = [W[:, 8 + 2 * i:10 + 2 * i, 0:GN] for i in range(2)]
    rw = W[:, 12, :].rearrange("p (h n) -> p h n", h=2)
    rw2, rb2, rT = W[:, 13, 0:E1], W[:, 13, 16:16 + E1], W[:, 14, 0:GN]
    b_out = W[0:EX, 15, :]
    cT = W[0:EX, 16, 0:GN]
    r = W[0:T, 17, :]
    lg, best, comb, other = (r[:, 16 * n:16 * n + 16].rearrange("p (k e) -> p k e", k=2) for n in range(4))
    bi = r[:, 64:80].bitcast(U32).rearrange("p (k e) -> p k e", k=2)
    bif = r[:, 80:84].rearrange("p (k e) -> p k e", k=2)
    gap, th, w1, w2, mx, sm = (r[:, 84 + 2 * n:86 + 2 * n] for n in range(6))
    ex = r[:, 100:116].rearrange("p (k e) -> p k e", k=2)
    NR = 128 if layer else EX
    nsteps = EX + DEEP - 1
    agg, aT, h7T = xn, W[:, 18:20, 0:GN], W[:, 20:22, 0:GN]
    y_tab, ry = W[:, 18:20, :], r[:, 116:118]
    root = m.small[0:T, 8:10]
    names = "in xn tp xT logits gap th comb ctp cT u h y added"
    names += " rh rT v h2 stored group agg agg_tp aT h7 h7T hid hidT head" if layer else " table table_out w_in"
    s = {n: sem(f"moe{layer}_{n}") for n in names.split()}
    halves = lambda bank: ps[:, bank, 0:2 * GN].rearrange("p (h c) -> p h c", h=2)
    col = lambda n: m.col_bias[:, COL["expert"] + n:COL["expert"] + n + 1]
    YS = EX + 1
    loads = 0
    if out is not None:
        to = out.rearrange("(t p) d -> p t d", p=T)
    with nc.Block() as block:

        if layer == 0:
            cols = [("L0_ffn_b1", 0)]
            rows = "L0_ffn_b2"
            n_loads = 1 + 1 + 1
        else:
            parts = [("L1_ffn_expert_w1", 0), ("L1_ffn_expert_w2", EX), ("L1_ffn_expert_w3", 2 * EX)]
            cols = [("L1_ffn_expert_b1", 0), ("L1_ffn_expert_b2", 2 * EX)]
            rows = "L1_ffn_expert_b3"
            n_loads = 3 + 2 + 1 + 3

        @block.sync
        def _(sp):
            with nc.allow_non_contiguous_dma(reason="biases and router weights, one channel in each partition"):
                if layer == 0:
                    sp.dma_start(rw[:, :, 0:EX], a["L0_ffn_router_w"].rearrange("(h p) e -> p h e", p=P)).then_inc(s["in"], 16)
                else:
                    sp.dma_start(rw, a["L1_ffn_router_w1"].rearrange("(h p) e -> p h e", p=P)).then_inc(s["in"], 16)
                    sp.dma_start(rw2, a["L1_ffn_router_w2"]).then_inc(s["in"], 16)
                    sp.dma_start(rb2, a["L1_ffn_router_b2"].rearrange("(a e) -> a e", a=1).to_broadcast([P, E1])).then_inc(s["in"], 16)
                for name, at in cols:
                    sp.dma_start(m.col_bias[:, COL["expert"] + at:COL["expert"] + at + 2 * EX],
                                 a[name].rearrange("e (h p) -> p (e h)", p=P)).then_inc(s["in"], 16)
            sp.dma_start(b_out, a[rows]).then_inc(s["in"], 16)
            if layer == 1:
                for name, at in parts:
                    sp.dma_start(w[:, at:at + EX, :, :].rearrange("p e k n -> p (e k) n"),
                                 a[name].rearrange("e (k p) n -> p (e k) n", p=P)).then_inc(s["in"], 16)
            else:
                parts1 = [(n, a[w]) for n, w in enumerate(("L1_gnn_W", "L1_gnn_W1", "L1_gnn_W2"))]
                parts1 += [(3 + n, a["L1_mix_w_qkv"][:, n * D:(n + 1) * D]) for n in range(3)]
                parts1 += [(6 + n, a["L1_mix_w_fc1"][:, n * D:(n + 1) * D]) for n in range(3)]
                parts1 += [(9 + n, a["L1_mix_w_fc2"][n * D:(n + 1) * D, :]) for n in range(3)]
                for n, src in parts1:
                    sp.dma_start(m.w[:, n, :, :], src.rearrange("(k p) n -> p k n", p=P)).then_inc(s["w_in"], 16)
                to_table = m.table[1].rearrange("(t p) d -> p t d", p=T)
                with sp.Fori(0, G) as g:
                    sp.wait_ge(s["table"], 2 * g + 2)
                    sp.dma_start(to_table[:, bass.ds(g * 2, 2), :], y_tab[0:T, :, :]).then_inc(s["table_out"], 16)
                sp.wait_ge(s["table_out"], 16 * G)
                sp.wait_ge(s["w_in"], 16 * len(parts1))
            if out is not None:
                with sp.Fori(0, G) as g:
                    sp.wait_ge(s["group"], g + 1)
                    sp.dma_start(to[:, bass.ds(g * 2, 2), :], m.x[0:T, bass.ds(g * 2, 2), 0:D]).then_inc(s["stored"], 16)
                sp.wait_ge(s["stored"], 16 * G)

        @block.vector
        def _(dve):
            chain = m.chain
            if layer == 0:
                deg, pos = m.small[0:T, 20:20 + NT], m.small[0:T, 70:70 + NT]
                chain.link(nc.vector.tensor_scalar(deg, m.x[0:T, :, D], 1.0, None, ALU.add))
                chain.link(nc.vector.tensor_scalar(pos, deg, 0.0, None, ALU.is_gt))
                chain.link(nc.vector.tensor_scalar(deg, deg, 1e-30, None, ALU.max))
                inverse_root(nc, chain, m.dinv[0:T, :], deg, 0.0, m.small[0:T, 120:120 + NT], m.small[0:T, 170:170 + NT])
                chain.link(nc.vector.tensor_tensor(m.dinv[0:T, :], m.dinv[0:T, :], pos, ALU.mult))
            else:
                chain.link(nc.vector.memset(r[:, 0:64], -1.0))

            def sums(g):
                dve.wait_ge(s["tp"], g)
                for k in range(2):
                    t = g * 2 + k
                    nc.vector.tensor_scalar(agg[0:T, k, :], tile_of(m.acc, t, D), m.dinv[0:T, bass.ds(t, 1)], None, ALU.mult).then_inc(s["agg"], 1)

            def prepare(g):
                if layer == 1:
                    xg = m.x[0:T, bass.ds(g * 2, 2), 0:D]
                    dve.wait_ge(s["head"], g + 1)
                    chain.link(nc.vector.tensor_tensor(xg, xg, ps[0:T, 1, :].rearrange("p (k d) -> p k d", k=2), ALU.add))
                    chain.link(nc.vector.tensor_tensor(xg, xg, m.row_bias[0:T, ROW["gnn_b2"], :].unsqueeze(1).to_broadcast([T, 2, D]), ALU.add))
                group_stats(nc, chain, m, [tile_of(m.x, g * 2 + k, D) for k in range(2)], root)
                dve.wait_ge(s["tp"], g)
                for k in range(2):
                    nc.vector.tensor_scalar(xn[0:T, k, :], tile_of(m.x, g * 2 + k, D), m.mv[0:T, k, 0:1], root[:, k:k + 1],
                                            ALU.subtract, ALU.mult).then_inc(s["xn"], 1)

            def next_table(g):
                group_stats(nc, chain, m, [tile_of(m.x, g * 2 + k, D) for k in range(2)], root)
                both = bass.ds(g * 2, 2)
                chain.did(nc.vector.tensor_scalar(m.mean[0:T, both], m.mv[0:T, :, 0], 0.0, None, ALU.add))
                chain.did(nc.vector.tensor_scalar(m.rstd[0:T, both], root, 0.0, None, ALU.add))
                chain.link(nc.vector.tensor_tensor(ry, root, m.dinv[0:T, both], ALU.mult))
                dve.wait_ge(s["table_out"], 16 * g)
                for k in range(2):
                    nc.vector.tensor_scalar(y_tab[0:T, k, :], tile_of(m.x, g * 2 + k, D), m.mv[0:T, k, 0:1], ry[:, k:k + 1],
                                            ALU.subtract, ALU.mult).then_inc(s["table"], 1)
                dve.wait_ge(s["table"], 2 * g + 2)

            if layer == 1:
                sums(0)
            prepare(0)

            def router(g):
                dve.wait_ge(s["logits"], g + 1)
                both = ps[0:T, 1, 0:16].rearrange("p (k e) -> p k e", k=2)[:, :, 0:EX]
                if layer == 0:
                    chain.link(nc.vector.tensor_copy(lg, both))
                    values = lg
                else:
                    chain.link(nc.vector.tensor_tensor(lg[:, :, 0:EX], both, rb2[0:T, :].unsqueeze(1).to_broadcast([T, 2, EX]), ALU.add))
                    chain.link(nc.vector.tensor_reduce(mx, lg[:, :, 0:EX], AX.X, ALU.max))
                    nc.vector.tensor_tensor(ex[:, :, 0:EX], lg[:, :, 0:EX], mx.unsqueeze(2).to_broadcast([T, 2, EX]), ALU.subtract).then_inc(s["gap"], 1)
                    dve.wait_ge(s["th"], 2 * g + 1)
                    chain.link(nc.vector.tensor_reduce(sm, ex[:, :, 0:EX], AX.X, ALU.add))
                    chain.link(nc.vector.reciprocal(sm, sm))
                    chain.link(nc.vector.tensor_tensor(other[:, :, 0:EX], ex[:, :, 0:EX], sm.unsqueeze(2).to_broadcast([T, 2, EX]), ALU.mult))
                    values = other
                chain.apart()
                for k in range(2):
                    chain.did(nc.vector.max(best[:, k, :], values[:, k, :]))
                chain.settle_apart()
                for k in range(2):
                    chain.did(nc.vector.max_index(bi[:, k, :], best[:, k, :], values[:, k, :]))
                chain.settle()
                chain.did(nc.vector.tensor_copy(bif, bi[:, :, 0:2]))
                nc.vector.tensor_tensor(gap, best[:, :, 0], best[:, :, 1], ALU.subtract).then_inc(s["gap"], 1)
                chain.settle()

            def weigh(g):
                if layer == 0:
                    dve.wait_ge(s["th"], g + 1)
                    chain.did(nc.vector.tensor_scalar(w1, th, 0.5, 0.5, ALU.mult, ALU.add))
                    chain.did(nc.vector.tensor_scalar(w2, th, -0.5, 0.5, ALU.mult, ALU.add))
                    chain.settle()
                else:
                    dve.wait_ge(s["th"], 2 * g + 2)
                    chain.link(nc.vector.tensor_scalar(w1, th, 1.0, None, ALU.add))
                    chain.link(nc.vector.reciprocal(w1, w1))
                    chain.link(nc.vector.tensor_tensor(w2, th, w1, ALU.mult))
                dve.wait_ge(s["ctp"], g)
                for k in range(2):
                    chain.did(nc.vector.tensor_scalar(comb[:, k, :], m.iota[0:T, 0:8], bif[:, k, 0:1], w1[:, k:k + 1], ALU.is_equal, ALU.mult))
                    chain.did(nc.vector.tensor_scalar(lg[:, k, :], m.iota[0:T, 0:8], bif[:, k, 1:2], w2[:, k:k + 1], ALU.is_equal, ALU.mult))
                chain.settle()
                nc.vector.tensor_tensor(comb, comb, lg, ALU.add).then_inc(s["comb"], 1)
                dve.wait_ge(s["comb"], g + 1)

            def turn(g, last):
                xg = m.x[0:T, bass.ds(g * 2, 2), 0:D]
                router(g)
                if layer == 0:
                    chain.link(nc.vector.tensor_tensor(xg, xg, xn[0:T, :, :], ALU.add))
                weigh(g)
                if layer == 1 and not last:
                    sums(g + 1)
                for n in range(YS):
                    if n == 4 and not last:
                        prepare(g + 1)
                    dve.wait_ge(s["y"], g * YS + n + 1)
                    y = ps[0:T, 4 + n % 2, :].rearrange("p (k d) -> p k d", k=2)
                    if n < EX:
                        for k in range(2):
                            to = tile_of(m.x, g * 2 + k, D)
                            chain.did(nc.vector.scalar_tensor_tensor(to, y[:, k, :], comb[:, k, n:n + 1], to, ALU.mult, ALU.add))
                        chain.settle()
                        nc.vector.memset(m.small[0:1, 6:7], 0.0).then_inc(s["added"], 1)
                    else:
                        nc.vector.tensor_tensor(xg, xg, y, ALU.add).then_inc(s["added"], 1)
                        dve.wait_ge(s["added"], g * YS + YS)
                if layer == 1:
                    nc.vector.memset(m.small[0:1, 7:8], 0.0).then_inc(s["group"], 1)
                else:
                    next_table(g)

            steps = (1 if layer == 0 else 5) + 2 + 2 + 1 + (1 if layer == 0 else 0) + (2 if layer == 0 else 3) + 4 + 2 * EX
            steps += STATS_STEPS + (2 if layer == 1 else STATS_STEPS + 3)
            with dve.Fori(0, G - 1) as g:
                chain.begin(g, steps)
                turn(g, False)
                chain.end(G - 1)
            turn(G - 1, True)

        @block.scalar
        def _(act):
            def head(g, stage):
                if stage == 0:
                    act.wait_ge(s["agg_tp"], g + 1)
                    act.wait_ge(s["head"], g)
                    nc.scalar.copy(aT, halves(0)).then_inc(s["aT"], 1)
                elif stage == 1:
                    act.wait_ge(s["h7"], g + 1)
                    act.wait_ge(s["hid"], g)
                    for h in range(2):
                        nc.scalar.activation(h7T[:, h, :], halves(1)[:, h, :], ACT.Identity,
                                             bias=m.col_bias[:, COL["gnn_b"] + h:COL["gnn_b"] + h + 1]).then_inc(s["h7T"], 1)
                else:
                    act.wait_ge(s["hid"], g + 1)
                    for h in range(2):
                        nc.scalar.activation(aT[:, h, :], halves(0)[:, h, :], ACT.Relu,
                                             bias=m.col_bias[:, COL["gnn_b1"] + h:COL["gnn_b1"] + h + 1]).then_inc(s["hidT"], 1)

            if layer == 1:
                for stage in range(3):
                    head(0, stage)
            act.wait_ge(s["tp"], 1)
            nc.scalar.copy(xT, halves(0)).then_inc(s["xT"], 1)

            def evacuate(g, e, bank, to, ready, wrote, readers, func, bias):
                act.wait_ge(s[ready], g * EX + e + 1)
                per, count = readers
                act.wait_ge(s[per], g * count + max(e - 1, 0))
                for h in range(2):
                    ins = nc.scalar.activation(to[:, h, :], halves(bank)[:, h, :], func, bias=col(bias + h))
                ins.then_inc(s[wrote], 1)

            def turn(g, last):
                if layer == 1:
                    act.wait_ge(s["rh"], g + 1)
                    nc.scalar.activation(rT, ps[:, 1, 16:16 + GN], ACT.Relu, bias=m.col_bias[:, COL["router_b1"]:COL["router_b1"] + 1]).then_inc(s["rT"], 1)
                for step in range(nsteps):
                    if step < EX:
                        evacuate(g, step, 2 + step % 2, hid[step % 2], "u", "h", ("y", YS) if DEEP == 2 else ("v", EX),
                                 ACT.Gelu if layer == 0 else ACT.Relu, 2 * step)
                    if DEEP == 3 and 1 <= step <= EX:
                        e = step - 1
                        evacuate(g, e, 6 + e % 2, hid2[e % 2], "v", "h2", ("y", YS), ACT.Relu, 2 * EX + 2 * e)
                    if step == 0:
                        act.wait_ge(s["gap"], (g + 1) if layer == 0 else (2 * g + 1))
                        if layer == 0:
                            nc.scalar.activation(th, gap, ACT.Tanh, scale=0.5).then_inc(s["th"], 1)
                        else:
                            nc.scalar.activation(ex[:, :, 0:EX], ex[:, :, 0:EX], ACT.Exp).then_inc(s["th"], 1)
                            act.wait_ge(s["gap"], 2 * g + 2)
                            nc.scalar.activation(th, gap, ACT.Exp, scale=-1.0).then_inc(s["th"], 1)
                    if step == 2:
                        act.wait_ge(s["ctp"], g + 1)
                        nc.scalar.copy(cT, ps[0:EX, 1, 0:GN]).then_inc(s["cT"], 1)
                    if layer == 1 and step in (3, 4, 5) and not last:
                        head(g + 1, step - 3)
                    if step == nsteps - 1 and not last:
                        act.wait_ge(s["tp"], g + 2)
                        nc.scalar.copy(xT, halves(0)).then_inc(s["xT"], 1)

            with act.Fori(0, G - 1) as g:
                turn(g, False)
            turn(G - 1, True)

        @block.tensor
        def _(pe):
            def head(g, stage):
                if stage == 0:
                    pe.wait_ge(s["agg"], 2 * g + 2)
                    pe.wait_ge(s["xT"], g)
                    transpose_group(nc, m, 0, agg).then_inc(s["agg_tp"], 1)
                elif stage == 3:
                    pe.wait_ge(s["hidT"], 2 * g + 2)
                    for k in range(2):
                        last = rows_times(nc, ps[0:T, 1, k * D:(k + 1) * D], lambda h: aT[:, h, k * T:(k + 1) * T], lambda h: m.w[:, 2, h, :])
                    last.then_inc(s["head"], 1)
                else:
                    if stage == 1:
                        pe.wait_ge(s["aT"], g + 1)
                        pe.wait_ge(s["cT"], g)
                    else:
                        pe.wait_ge(s["h7T"], 2 * g + 2)
                    of, bank, done = (aT, 1, "h7") if stage == 1 else (h7T, 0, "hid")
                    for o in range(2):
                        for h in range(2):
                            last = nc.tensor.matmul(ps[:, bank, o * GN:(o + 1) * GN], m.w[:, stage - 1, h, o * P:(o + 1) * P],
                                                    of[:, h, :], start=h == 0, stop=h == 1)
                    last.then_inc(s[done], 1)

            if layer == 1:
                for stage in range(4):
                    head(0, stage)
            pe.wait_ge(s["xn"], 2)
            transpose_group(nc, m, 0, xn).then_inc(s["tp"], 1)

            def square(g, e, at, of, bank, done, free):
                pe.wait_ge(s[free], g * EX + max(e - 1, 0))
                for o in range(2):
                    for h in range(2):
                        last = nc.tensor.matmul(ps[:, bank, o * GN:(o + 1) * GN], w[:, at + e, h, o * P:(o + 1) * P], of[:, h, :],
                                                start=h == 0, stop=h == 1)
                last.then_inc(s[done], 1)

            def rows_out(g, e):
                pe.wait_ge(s["h" if DEEP == 2 else "h2"], g * EX + e + 1)
                pe.wait_ge(s["added"], g * YS + max(e - 1, 0))
                of = (hid if DEEP == 2 else hid2)[e % 2]
                for k in range(2):
                    last = rows_times(nc, ps[0:T, 4 + e % 2, k * D:(k + 1) * D], lambda h: of[:, h, k * T:(k + 1) * T],
                                      lambda h: w[:, (DEEP - 1) * EX + e, h, :])
                last.then_inc(s["y"], 1)

            pe.wait_ge(s["in"], 16 * n_loads)

            def turn(g, last_turn):
                pe.wait_ge(s["xT"], g + 1)
                pe.wait_ge(s["cT"], g)
                if layer == 1:
                    for h in range(2):
                        last = nc.tensor.matmul(ps[:, 1, 16:16 + GN], rw[:, h, :], xT[:, h, :], start=h == 0, stop=h == 1)
                    last.then_inc(s["rh"], 1)
                    pe.wait_ge(s["rT"], g + 1)
                for k in range(2):
                    if layer == 0:
                        for h in range(2):
                            last = nc.tensor.matmul(ps[0:T, 1, 8 * k:8 * k + EX], xT[:, h, k * T:(k + 1) * T], rw[:, h, 0:EX],
                                                    start=h == 0, stop=h == 1)
                    else:
                        last = nc.tensor.matmul(ps[0:T, 1, 8 * k:8 * k + EX], rT[:, k * T:(k + 1) * T], rw2, start=True, stop=True)
                last.then_inc(s["logits"], 1)
                for step in range(nsteps):
                    if step < EX:
                        square(g, step, 0, xT, 2 + step % 2, "u", "h")
                    if DEEP == 3 and 1 <= step <= EX:
                        e = step - 1
                        pe.wait_ge(s["h"], g * EX + e + 1)
                        square(g, e, EX, hid[e % 2], 6 + e % 2, "v", "h2")
                    if step >= DEEP - 1:
                        rows_out(g, step - DEEP + 1)
                    if step == 2:
                        pe.wait_ge(s["comb"], g + 1)
                        for k in range(2):
                            last = nc.tensor.transpose(ps[0:EX, 1, k * T:(k + 1) * T], comb[:, k, 0:EX], m.ident[0:T, 0:T])
                        last.then_inc(s["ctp"], 1)
                    if layer == 1 and 2 <= step <= 5 and not last_turn:
                        head(g + 1, step - 2)
                if not last_turn:
                    pe.wait_ge(s["xn"], 2 * g + 4)
                    transpose_group(nc, m, 0, xn).then_inc(s["tp"], 1)
                pe.wait_ge(s["cT"], g + 1)
                pe.wait_ge(s["added"], g * YS + EX - 1)
                for k in range(2):
                    last = nc.tensor.matmul(ps[0:T, 4 + EX % 2, k * D:(k + 1) * D], cT[:, k * T:(k + 1) * T], b_out, start=True, stop=True)
                last.then_inc(s["y"], 1)

            with pe.Fori(0, G - 1) as g:
                turn(g, False)
            turn(G - 1, True)


def gps_kernel(nc, a, out):
    ctx = ExitStack()
    with ctx:
        m = Memory(nc, ctx)

        def sem(name):
            return ctx.enter_context(nc.semaphore(name))

        edges_and_mix0(nc, m, sem, a)
        gather_sums(nc, m, sem, a, 0)
        experts(nc, m, sem, a, 0)
        gather_sums(nc, m, sem, a, 1)
        experts(nc, m, sem, a, 1, out)


_INS = ("x src dst edge_weight L0_gnn_W L0_mix_wq L0_mix_bq L0_mix_wk L0_mix_bk L0_mix_wv L0_mix_bv L0_mix_wo L0_mix_bo "
        "L0_ffn_router_w L0_ffn_w1 L0_ffn_b1 L0_ffn_w2 L0_ffn_b2 L1_gnn_W L1_gnn_b L1_gnn_W1 L1_gnn_b1 L1_gnn_W2 L1_gnn_b2 "
        "L1_mix_w_qkv L1_mix_b_qkv L1_mix_norm_g L1_mix_norm_b L1_mix_w_fc1 L1_mix_b_fc1 L1_mix_w_fc2 L1_mix_b_fc2 "
        "L1_ffn_router_w1 L1_ffn_router_b1 L1_ffn_router_w2 L1_ffn_router_b2 L1_ffn_expert_w1 L1_ffn_expert_b1 "
        "L1_ffn_expert_w2 L1_ffn_expert_b2 L1_ffn_expert_w3 L1_ffn_expert_b3").split()


def kernel(**inputs):
    import concourse.bacc as bacc
    from concourse.bass_utils import run_bass_kernel_spmd

    nc = bacc.Bacc("TRN2", target_bir_lowering=False, num_devices=1)
    arrays, a = {}, {}
    for name in _INS:
        v = np.asarray(inputs[name])
        if name in ("L0_gnn_W", "L0_ffn_router_w"):
            v = v.T
        v = np.ascontiguousarray(v)
        arrays[f"in_{name}"] = v
        a[name] = nc.dram_tensor(f"in_{name}", v.shape, mybir.dt.from_np(v.dtype), kind="ExternalInput").ap()
    out = nc.dram_tensor("out", (N, D), F32, kind="ExternalOutput").ap()
    gps_kernel(nc, a, out)
    r = run_bass_kernel_spmd(nc, [arrays], core_ids=[0])
    return r.results[0]["out"]
```

```python
from contextlib import ExitStack

import numpy as np
import concourse.bass as bass
from concourse import mybir

F32, I32, U32 = mybir.dt.float32, mybir.dt.int32, mybir.dt.uint32
ALU = mybir.AluOpType
ACT = mybir.ActivationFunctionType
AX = mybir.AxisListType

P = 128
N, D, E = 6250, 256, 200000
T = 125
NT = N // T
G = NT // 2
GN = 2 * T
KD = D // P
EC = -(-E // P)
TAIL = E - (P - 1) * EC
HALF = 8
RING = 2 * HALF
CAP = 33
PER = 2 * CAP
CHUNKS = NT * CAP
EXTRA = CHUNKS % RING
LONG = 22
BATCH = 6
SLOTS = PER // BATCH
AHEAD = 2 * BATCH
assert CHUNKS * P >= P * EC + NT * (P - 1) and PER % LONG == 0 and PER % BATCH == 0
SC = 24
PARTS = [(0, 4 * SC), (4 * SC, 14 * SC), (14 * SC, EC)]
MAGIC = 1.5 * 2.0 ** 23
EPS = 1e-5
E0, E1 = 8, 6
KC = (P - 1 + CHUNKS) // P


class Chain:

    def __init__(self, engine, sem, spare):
        self.engine, self.sem, self.spare, self.base, self.n = engine, sem, spare, 0, 0

    def begin(self, index, steps):
        self.start, self.steps = self.base + self.n, steps
        self.base, self.n = index * steps + self.start, 0

    def end(self, trips):
        assert self.n == self.steps, (self.n, self.steps)
        self.base, self.n = self.start + trips * self.steps, 0

    def did(self, instruction):
        instruction.then_inc(self.sem, 1)
        self.n += 1

    def settle(self):
        self.engine.wait_ge(self.sem, self.base + self.n)

    def settle_apart(self):
        self.settle()
        self.apart()

    def apart(self):
        self.engine.sem_inc(self.spare, 1)

    def link(self, instruction):
        self.did(instruction)
        self.settle()


def apart(nc, m):
    nc.gpsimd.sem_inc(m.pool_spare, 1)


def tile_of(view, t, width):
    return view[0:T, bass.ds(t, 1), 0:width].rearrange("p a b -> p (a b)")


class Memory:

    def __init__(self, nc, ctx):
        def sb(name, shape, dt=F32):
            return ctx.enter_context(nc.sbuf_tensor(name, shape, dt))

        self.x = sb("x_res", [P, NT, D + 1])
        self.acc = sb("acc", [P, NT, D])
        self.flat = self.acc[:, :, :].rearrange("p a b -> p (a b)")
        parts = (RING * (D + 1), RING * T, CHUNKS, 2 * (CHUNKS + AHEAD))
        self.region = sb("gather_region", [P, sum(parts)])
        at = [sum(parts[:n]) for n in range(5)]
        rows, hot, dst, lew = (self.region[:, at[n]:at[n + 1]] for n in range(4))
        self.rows = rows.rearrange("p (s d) -> p s d", s=RING)
        self.hot = hot.rearrange("p (s n) -> p s n", s=RING)
        self.dst = dst.bitcast(I32)
        self.lew = lew.rearrange("p (c f) -> p c f", f=2)
        self.blk = sb("chunk_tile", [1, KC * P], I32)
        self.long_rows = self.region[:, 0:LONG * (D + 1)].rearrange("p (s d) -> p s d", s=LONG)
        hot_at = max(4 * E0, 6 * E1) * D
        attn_at, sums_at = hot_at + LONG * T, hot_at + LONG * T + D
        assert sums_at + 2 * D <= NT * D
        self.long_hot = self.flat[:, hot_at:attn_at].rearrange("p (s n) -> p s n", s=LONG)
        self.attn = self.flat[:, attn_at:sums_at].rearrange("p (h e) -> p h e", h=KD)
        self.group = self.flat[:, sums_at:sums_at + 2 * D].rearrange("p (k d) -> p k d", k=2)
        self.idx_all = sb("idx_stage", [P, 2 * CAP], I32)[:, :]
        self.idx = self.idx_all[:, 0:4 * HALF].rearrange("p (s j) -> p s j", s=4)
        self.fits = sb("fits", [1, 1], I32)
        self.w = sb("weights", [P, 12, KD, D])
        self.ident = sb("ident", [P, P])
        self.iota = sb("iota_free", [P, P])
        self.iota_i = sb("iota_int", [P, P], I32)
        self.row_bias = sb("row_bias", [P, 7, D])
        self.col_bias = sb("col_bias", [P, 48])
        self.mean = sb("mean", [P, NT])
        self.rstd = sb("rstd", [P, NT])
        self.dinv = sb("dinv", [P, NT])
        self.stats = sb("stats", [P, 2, 6])
        self.mv = sb("mean_var", [P, 2, 2])
        self.work = sb("work", [P, 22, D])
        self.small = sb("small", [P, 256])
        self.pool_spare = ctx.enter_context(nc.semaphore("pool_waited"))
        spare = ctx.enter_context(nc.semaphore("vector_waited"))
        self.chain, self.short_chain, self.long_chain = (
            Chain(nc.vector, ctx.enter_context(nc.semaphore(name)), spare)
            for name in ("vector_done", "vector_done_apart", "vector_done_together"))
        self.row_in = [[ctx.enter_context(nc.semaphore(f"rows_in{n}_{s}")) for s in range(LONG // 2)]
                       for n in range(2)]
        self.ps = ctx.enter_context(nc.psum_tensor("ps", [P, 8, 512], F32))
        self.table = [nc.dram_tensor(f"table{n}", (N, D), F32, kind="Internal").ap() for n in range(2)]
        self.sorted = nc.dram_tensor("sorted_edges", (P * CHUNKS, 2), F32, kind="Internal").ap()
        self.chunk_dram = nc.dram_tensor("chunk_tile_dram", (P * KC,), I32, kind="Internal").ap()


COL = {"bq": 0, "gnn_b": 2, "gnn_b1": 4, "bq1": 6, "norm_g": 8, "norm_b": 10, "fc1": 12,
       "router_b1": 18, "expert": 20}
ROW = {"bk": 0, "bv": 1, "bo": 2, "bk1": 3, "bv1": 4, "fc2": 5, "gnn_b2": 6}


def norm_stats(nc, dve, chain, m):
    var = m.small[:, 0:NT]
    with dve.Fori(0, G) as g:
        chain.begin(g, 6)
        for k in range(2):
            chain.did(nc.vector.bn_stats(m.stats[0:T, k, :], tile_of(m.x, g * 2 + k, D)))
        chain.settle_apart()
        for k in range(2):
            chain.did(nc.vector.bn_aggr(m.mv[0:T, k, :], m.stats[0:T, k, :]))
        chain.settle()
        chain.did(nc.vector.tensor_copy(m.mean[0:T, bass.ds(g * 2, 2)], m.mv[0:T, :, 0]))
        chain.did(nc.vector.tensor_copy(var[0:T, bass.ds(g * 2, 2)], m.mv[0:T, :, 1]))
        chain.settle()
        chain.end(G)
    inverse_root(nc, chain, m.rstd[0:T, :], var[0:T, :], EPS, m.small[0:T, 64:64 + NT], m.small[0:T, 128:128 + NT])


def inverse_root(nc, chain, out, value, add, half, guess):
    chain.link(nc.vector.tensor_scalar(half, value, add, None, ALU.add))
    chain.link(nc.vector.tensor_scalar(guess.bitcast(I32), half.bitcast(I32), 1, None, ALU.arith_shift_right))
    chain.link(nc.vector.tensor_scalar(out.bitcast(I32), guess.bitcast(I32), -1.0, float(0x5F3759DF), ALU.mult, ALU.add))
    chain.link(nc.vector.tensor_scalar(half, half, -0.5, None, ALU.mult))
    for _ in range(3):
        chain.link(nc.vector.tensor_tensor(guess, out, out, ALU.mult))
        chain.link(nc.vector.tensor_tensor(guess, guess, half, ALU.mult))
        chain.link(nc.vector.scalar_tensor_tensor(out, guess, 1.5, out, ALU.add, ALU.mult))


def group_stats(nc, chain, m, tiles, root):
    chain.apart()
    for k in range(2):
        chain.did(nc.vector.bn_stats(m.stats[0:T, k, :], tiles[k]))
    chain.settle_apart()
    for k in range(2):
        chain.did(nc.vector.bn_aggr(m.mv[0:T, k, :], m.stats[0:T, k, :]))
    chain.settle()
    inverse_root(nc, chain, root, m.mv[0:T, :, 1], EPS, m.small[0:T, 10:12], m.small[0:T, 12:14])


STATS_STEPS = 2 + 2 + 13


def normalise(nc, m, out, g, k):
    t = g * 2 + k
    return nc.vector.tensor_scalar(out, tile_of(m.x, t, D), m.mean[0:T, bass.ds(t, 1)], m.rstd[0:T, bass.ds(t, 1)],
                                   ALU.subtract, ALU.mult)


def transpose_group(nc, m, bank, tiles):
    for h in range(KD):
        for k in range(2):
            last = nc.tensor.transpose(m.ps[:, bank, h * GN + k * T:h * GN + (k + 1) * T],
                                       tiles[0:T, k, h * P:(h + 1) * P], m.ident[0:T, 0:T])
    return last


def rows_times(nc, out, xT, w, start=True, stop=True):
    for h in range(KD):
        last = nc.tensor.matmul(out, xT(h), w(h), start=start and h == 0, stop=stop and h == KD - 1)
    return last


def edges_and_mix0(nc, m, sem, a):
    src_i, dst_i, ew, blk, loc, mask, scan, pos = (m.flat[:, n * EC:(n + 1) * EC] for n in range(8))
    src_i, dst_i = src_i.bitcast(I32), dst_i.bitcast(I32)
    addr = src_i
    rec = m.lew[:, :, :].rearrange("p c f -> p (c f)")
    rec2 = rec[:, 0:2 * EC].rearrange("p (e f) -> p e f", f=2)
    small = m.small
    cnt, base, start, tri = small[:, 0:NT], small[:, NT:2 * NT], small[:, 2 * NT:3 * NT], m.rows[:, 0, 0:P]
    chunks, incl = small[:, 3 * NT:4 * NT], small[:, 4 * NT:5 * NT]
    ones, zeros = m.rows[:, 1, 0:P], rec
    flag = m.rows[:, 2:5, :].rearrange("p a b -> p (a b)")[:, 0:KC * NT].rearrange("p (j b) -> p j b", j=KC)
    of, of_i, at = m.hot[:, 0, 0:KC], m.hot[:, 1, 0:KC].bitcast(I32), m.hot[:, 2, 0:KC]
    pads_set, edges_in, zeroed, sorted_zero = sem("pads_set"), sem("edges_in"), sem("zero_set"), sem("sorted_zeroed")
    made, counted, totalled, of_ready, of_out, of_in, x_in, placed = (
        sem("constants_made"), sem("counted"), sem("totalled"), sem("tile_of_chunk"), sem("chunk_tile_out"),
        sem("chunk_tile_in"), sem("x_in"), sem("edges_placed"))
    X_LOADS = 5 + 5 + 7 + 8
    x_dram = a["x"].rearrange("(t p) d -> p t d", p=T)
    W = m.work
    xn, xT = W[:, 0:2, :], W[:, 2:4, 0:GN]
    table_sb, kb, ke, kf = W[:, 4:6, :], W[:, 6:8, :], W[:, 8:10, :], W[:, 10:12, :]
    v = W[:, 12:15, :].rearrange("p a b -> p (a b)")[:, 0:2 * 258].rearrange("p (k c) -> p k c", k=2)
    kvd = W[:, 15, :].rearrange("p (h e) -> p h e", h=2)
    ksd = W[:, 16, :].rearrange("p (h e) -> p h e", h=2)
    same = W[:, 17, 0:P]
    st_addr = W[:, 18, 0:2 * SC].bitcast(I32).rearrange("p (h c) -> p h c", h=2)
    st_rec = W[:, 19, 0:4 * SC].rearrange("p (h c f) -> p h c f", h=2, f=2)
    qe, qf, oT = W[:, 6:8, 0:GN], W[:, 8:10, 0:GN], W[:, 10:12, 0:GN]
    qm, rn = W[:, 4:6, 0:GN], W[:, 12:14, 0:GN]
    ps = m.ps
    staged, scattered = sem("scatter_staged"), [sem(f"scattered{h}") for h in range(2)]
    set_up = sem("set_up0")
    xn_ready, tp_done, xT_ready = sem("xn0"), sem("xn0_transposed"), sem("xT0")
    proj, km_ready, ke_ready, kf_ready, v_ready, kv_done = (
        sem("table_k_v"), sem("k_min"), sem("k_exp"), sem("kf"), sem("v_ready"), sem("kv_summed"))
    table_ready, table_out = sem("table0_ready"), sem("table0_out")
    kvd_ready, qxn, qtp, qxT, q_done, qm_ready, qe_ready, qf_ready, o_done, oT_ready, y_done, y_added = (
        sem("kv_diag"), sem("q_xn"), sem("q_transposed"), sem("q_xT"), sem("q_done"), sem("q_min"), sem("q_exp"),
        sem("qf"), sem("o_done"), sem("oT"), sem("y_done"), sem("y_added"))
    bq = [m.col_bias[:, COL["bq"] + h:COL["bq"] + h + 1] for h in range(2)]

    def scatter(pool, first, h, count, stage_count):
        nc.gpsimd.tensor_copy(st_addr[:, h, 0:count], addr[:, bass.ds(first, count)]).then_inc(staged, 1)
        nc.gpsimd.tensor_copy(st_rec[:, h, 0:count, :].rearrange("p c f -> p (c f)"),
                              rec[:, bass.ds(first * 2, 2 * count)]).then_inc(staged, 1)
        pool.wait_ge(staged, stage_count)
        apart(nc, m)
        for j in range(count):
            nc.gpsimd.indirect_dma_start(
                out=m.sorted, out_offset=bass.IndirectOffsetOnAxis(ap=st_addr[:, h, j:j + 1], axis=0),
                in_=st_rec[:, h, j, :], in_offset=None).then_inc(scattered[h], 16)

    with nc.Block() as block:

        @block.sync
        def _(sp):
            sp.wait_ge(pads_set, 3)
            for src, to in ((a["src"], src_i), (a["dst"], dst_i), (a["edge_weight"], ew)):
                for lo, hi in ((0, 112), (112, P - 1)):
                    sp.dma_start(to[lo:hi, :], src[lo * EC:hi * EC].rearrange("(p c) -> p c", c=EC)).then_inc(edges_in, 16)
                sp.dma_start(to[P - 1:P, 0:TAIL], src[(P - 1) * EC:E].rearrange("(p c) -> p c", c=TAIL)).then_inc(edges_in, 16)
            sp.wait_ge(zeroed, 1)
            sp.dma_start(m.sorted.rearrange("(p c) f -> p (c f)", p=P), zeros[:, 0:2 * CHUNKS]).then_inc(sorted_zero, 16)
            for c in range(5):
                sp.dma_start(m.x[0:T, 10 * c:10 * c + 10, 0:D], x_dram[:, 10 * c:10 * c + 10, :]).then_inc(x_in, 16)
            for n, name in enumerate(("L0_gnn_W", "L0_mix_wk", "L0_mix_wv", "L0_mix_wq", "L0_mix_wo")):
                sp.dma_start(m.w[:, n, :, :], a[name].rearrange("(k p) n -> p k n", p=P)).then_inc(x_in, 16)
            for name, src in (("bk", a["L0_mix_bk"]), ("bv", a["L0_mix_bv"]), ("bo", a["L0_mix_bo"]),
                              ("bk1", a["L1_mix_b_qkv"][D:2 * D]), ("bv1", a["L1_mix_b_qkv"][2 * D:3 * D]),
                              ("fc2", a["L1_mix_b_fc2"]), ("gnn_b2", a["L1_gnn_b2"])):
                sp.dma_start(m.row_bias[:, ROW[name], :], src.rearrange("(a d) -> a d", a=1).to_broadcast([P, D])).then_inc(x_in, 16)
            for name, src, n in (("bq", a["L0_mix_bq"], 2), ("gnn_b", a["L1_gnn_b"], 2), ("gnn_b1", a["L1_gnn_b1"], 2),
                                 ("bq1", a["L1_mix_b_qkv"][0:D], 2), ("norm_g", a["L1_mix_norm_g"], 2),
                                 ("norm_b", a["L1_mix_norm_b"], 2), ("fc1", a["L1_mix_b_fc1"], 6),
                                 ("router_b1", a["L1_ffn_router_b1"], 1)):
                with nc.allow_non_contiguous_dma(reason="a bias, one channel in each partition"):
                    sp.dma_start(m.col_bias[:, COL[name]:COL[name] + n], src.rearrange("(h p) -> p h", p=P)).then_inc(x_in, 16)
            sp.wait_ge(of_ready, 1)
            sp.dma_start(m.chunk_dram.rearrange("(p j) -> p j", p=P), of_i).then_inc(of_out, 16)
            sp.wait_ge(of_out, 16)
            sp.dma_start(m.blk[:, :], m.chunk_dram.rearrange("(a c) -> a c", a=1)).then_inc(of_in, 16)
            sp.wait_ge(of_in, 16)
            to = m.table[0].rearrange("(t p) d -> p t d", p=T)
            with sp.Fori(0, G) as g:
                sp.wait_ge(table_ready, g + 1)
                sp.dma_start(to[:, bass.ds(g * 2, 2), :], table_sb[0:T, :, :]).then_inc(table_out, 16)
            sp.wait_ge(table_out, 16 * G)

        @block.gpsimd
        def _(pool):
            nc.gpsimd.iota(m.iota_i[:, :], [[1, P]], base=0, channel_multiplier=0).then_inc(made, 1)
            nc.gpsimd.memset(m.ident[:, :], 0.0).then_inc(made, 1)
            nc.gpsimd.memset(ones, 1.0).then_inc(made, 1)
            nc.gpsimd.memset(m.x[:, :, D:D + 1], 0.0).then_inc(made, 1)
            nc.gpsimd.iota(of_i, [[1, KC]], base=0, channel_multiplier=KC).then_inc(made, 1)
            pool.wait_ge(made, 5)
            nc.gpsimd.tensor_copy(m.iota[:, :], m.iota_i[:, :]).then_inc(made, 1)
            nc.gpsimd.tensor_copy(at, of_i).then_inc(made, 1)
            nc.gpsimd.affine_select(out=m.ident[:, :], in_=m.ident[:, :], compare_op=ALU.not_equal, fill=1.0,
                                    base=0, pattern=[[-1, P]], channel_multiplier=1).then_inc(made, 1)
            nc.gpsimd.affine_select(out=tri, in_=ones, compare_op=ALU.is_ge, fill=0.0,
                                    base=-1, pattern=[[1, P]], channel_multiplier=-1).then_inc(made, 1)
            nc.gpsimd.memset(zeros, 0.0).then_inc(zeroed, 1)
            pool.wait_ge(sorted_zero, 16)
            trips = EC // (2 * SC)
            for part, (lo, hi) in enumerate(PARTS):
                pool.wait_ge(placed, part + 1)
                with pool.Fori(lo // (2 * SC), hi // (2 * SC)) as i:
                    for h in range(2):
                        pool.wait_ge(scattered[h], i * (16 * SC))
                        scatter(pool, i * (2 * SC) + h * SC, h, SC, i * 4 + 2 * (h + 1))
            left = EC - trips * 2 * SC
            for h in range(2):
                count = min(SC, left - h * SC)
                if count > 0:
                    pool.wait_ge(scattered[h], trips * 16 * SC)
                    scatter(pool, trips * 2 * SC + h * SC, h, count, trips * 4 + 2 * (h + 1))
            pool.wait_ge(scattered[0], 16 * (trips * SC + min(SC, left)))
            pool.wait_ge(scattered[1], 16 * (trips * SC + max(0, left - SC)))

        @block.vector
        def _(dve):
            chain = m.chain
            nc.vector.memset(src_i[:, TAIL:EC], N - 1).then_inc(pads_set, 1)
            nc.vector.memset(dst_i[:, TAIL:EC], 0).then_inc(pads_set, 1)
            nc.vector.memset(ew[:, TAIL:EC], 0.0).then_inc(pads_set, 1)
            dve.wait_ge(made, 9)
            dve.wait_ge(edges_in, 16 * 9)
            chain.link(nc.vector.tensor_copy(mask, src_i))
            chain.link(nc.vector.tensor_scalar(blk, mask, 1.0 / T, 0.5 / T - 0.5, ALU.mult, ALU.add))
            chain.link(nc.vector.tensor_scalar(blk, blk, MAGIC, None, ALU.add))
            chain.link(nc.vector.tensor_scalar(blk, blk, -MAGIC, None, ALU.add))
            chain.link(nc.vector.scalar_tensor_tensor(loc, blk, -float(T), mask, ALU.mult, ALU.add))
            with dve.Fori(0, NT) as b:
                chain.begin(b, 1)
                chain.link(nc.vector.tensor_scalar(mask, blk, m.iota[:, bass.ds(b, 1)], None, ALU.is_equal, ALU.add,
                                                   accum_out=cnt[:, bass.ds(b, 1)]))
                chain.end(NT)
            nc.vector.memset(small[:, 5 * NT:5 * NT + 1], 0.0).then_inc(counted, 1)
            dve.wait_ge(totalled, 1)
            chain.link(nc.vector.tensor_scalar(chunks, m.ps[:, 1, 0:NT], 1.0 / P, (P - 1.0) / P - 0.5 + 0.5 / P, ALU.mult, ALU.add))
            chain.link(nc.vector.tensor_scalar(chunks, chunks, MAGIC, None, ALU.add))
            chain.link(nc.vector.tensor_scalar(chunks, chunks, -MAGIC, None, ALU.add))
            chain.link(nc.vector.tensor_tensor_scan(incl, chunks, chunks, 0.0, ALU.add, ALU.bypass))
            chain.link(nc.vector.tensor_tensor(start, incl, chunks, ALU.subtract))
            fits = small[:, 5 * NT + 1:5 * NT + 2]
            chain.link(nc.vector.tensor_reduce(fits, chunks, AX.X, ALU.max))
            chain.link(nc.vector.tensor_scalar(fits, fits, float(CAP), None, ALU.is_le))
            chain.did(nc.vector.tensor_copy(m.fits[0:1, 0:1], fits[0:1, :]))
            chain.link(nc.vector.scalar_tensor_tensor(incl, m.iota[:, 0:NT], float(CAP), start, ALU.mult, ALU.subtract))
            chain.link(nc.vector.tensor_scalar(incl, incl, fits, None, ALU.mult))
            chain.link(nc.vector.tensor_tensor(start, start, incl, ALU.add))
            chain.link(nc.vector.scalar_tensor_tensor(base, start, float(P), m.ps[:, 0, 0:NT], ALU.mult, ALU.add))
            chain.link(nc.vector.tensor_scalar(base, base, -1.0, None, ALU.add))
            chain.link(nc.vector.tensor_tensor(flag, start.unsqueeze(1).to_broadcast([P, KC, NT]),
                                               at.unsqueeze(2).to_broadcast([P, KC, NT]), ALU.is_le))
            chain.link(nc.vector.tensor_reduce(of, flag, AX.X, ALU.add))
            chain.link(nc.vector.tensor_scalar(of, of, -1.0, None, ALU.add))
            nc.vector.tensor_copy(of_i, of).then_inc(of_ready, 1)
            dve.wait_ge(sorted_zero, 16)
            for part, (lo, hi) in enumerate(PARTS):
                cols = slice(lo, hi)
                with dve.Fori(0, NT) as b:
                    chain.begin(b, 4)
                    chain.link(nc.vector.tensor_scalar(mask[:, cols], blk[:, cols], m.iota[:, bass.ds(b, 1)], None, ALU.is_equal))
                    chain.link(nc.vector.tensor_tensor_scan(scan[:, cols], mask[:, cols], mask[:, cols], base[:, bass.ds(b, 1)], ALU.add, ALU.bypass))
                    chain.did(nc.vector.tensor_scalar(base[:, bass.ds(b, 1)], scan[:, hi - 1:hi], 0.0, None, ALU.add))
                    chain.apart()
                    chain.link(nc.vector.copy_predicated(pos[:, cols], mask[:, cols].bitcast(U32), scan[:, cols]))
                    chain.end(NT)
                low, high, to = mask[:, cols].bitcast(I32), scan[:, cols].bitcast(I32), addr[:, cols]
                chain.link(nc.vector.tensor_copy(to, pos[:, cols]))
                chain.did(nc.vector.tensor_scalar(high, to, 7, None, ALU.arith_shift_right))
                chain.link(nc.vector.tensor_scalar(low, to, P - 1, None, ALU.bitwise_and))
                chain.link(nc.vector.scalar_tensor_tensor(to, low, float(CHUNKS), high, ALU.mult, ALU.add))
                chain.link(nc.vector.tensor_copy(pos[:, cols], dst_i[:, cols]))
                chain.did(nc.vector.scalar_tensor_tensor(rec2[:, cols, 0], pos[:, cols], float(P), loc[:, cols], ALU.mult, ALU.add))
                chain.link(nc.vector.tensor_copy(rec2[:, cols, 1], ew[:, cols]))
                nc.vector.memset(m.mv[0:1, 0, 0:1], 0.0).then_inc(placed, 1)
                dve.wait_ge(placed, part + 1)
            dve.wait_ge(x_in, 16 * X_LOADS)
            chain.did(nc.vector.memset(same, 0.0))
            for k in range(2):
                for h in range(2):
                    chain.did(nc.vector.memset(v[:, k, 129 * h + P:129 * h + P + 1], 1.0))
            chain.settle()
            for b in range(4):
                chain.did(nc.vector.memset(same[32 * b:32 * b + 32, 32 * b:32 * b + 32], 1.0))
            chain.did(nc.vector.memset(table_sb[:, 0, :], 0.0))
            chain.settle()
            nc.vector.memset(table_sb[:, 1, :], 0.0).then_inc(set_up, 1)
            norm_stats(nc, dve, chain, m)
            with dve.Fori(0, G) as g:
                chain.begin(g, 1)
                dve.wait_ge(tp_done, g)
                for k in range(2):
                    normalise(nc, m, xn[0:T, k, :], g, k).then_inc(xn_ready, 1)
                dve.wait_ge(proj, g * 3 + 2)
                dve.wait_ge(kv_done, g)
                chain.link(nc.vector.tensor_tensor(kb[0:T, :, :], ps[0:T, 2, :].rearrange("p (k d) -> p k d", k=2),
                                                   m.row_bias[0:T, ROW["bk"], :].unsqueeze(1).to_broadcast([T, 2, D]), ALU.add))
                nc.vector.tensor_scalar(kf[0:T, :, :], kb[0:T, :, :], 0.0, None, ALU.min).then_inc(km_ready, 1)
                dve.wait_ge(proj, g * 3 + 3)
                for h in range(2):
                    nc.vector.tensor_tensor(v[0:T, :, 129 * h:129 * h + P],
                                            ps[0:T, 3, :].rearrange("p (k d) -> p k d", k=2)[:, :, h * P:(h + 1) * P],
                                            m.row_bias[0:T, ROW["bv"], h * P:(h + 1) * P].unsqueeze(1).to_broadcast([T, 2, P]),
                                            ALU.add).then_inc(v_ready, 1)
                dve.wait_ge(ke_ready, g + 1)
                nc.vector.scalar_tensor_tensor(kf[0:T, :, :], kb[0:T, :, :], 0.0, ke[0:T, :, :], ALU.max, ALU.add).then_inc(kf_ready, 1)
                chain.end(G)
            dve.wait_ge(kv_done, G)
            for h in range(2):
                nc.vector.tensor_tensor(kvd[:, h, :], ps[:, 4, 129 * h:129 * h + P], same, ALU.mult).then_inc(kvd_ready, 1)
                nc.vector.tensor_scalar(ksd[:, h, :], same, ps[:, 4, 129 * h + P:129 * h + P + 1], None, ALU.mult).then_inc(kvd_ready, 1)
            with dve.Fori(0, G) as g:
                chain.begin(g, 5)
                dve.wait_ge(qtp, g)
                for k in range(2):
                    normalise(nc, m, xn[0:T, k, :], g, k).then_inc(qxn, 1)
                dve.wait_ge(q_done, g + 1)
                for h in range(2):
                    nc.vector.tensor_scalar(qm[:, h, :], ps[:, 2, h * GN:(h + 1) * GN], bq[h], 0.0, ALU.add, ALU.min).then_inc(qm_ready, 1)
                dve.wait_ge(o_done, g)
                for h in range(2):
                    chain.did(nc.vector.tensor_scalar(qf[:, h, :], ps[:, 2, h * GN:(h + 1) * GN], bq[h], 0.0, ALU.add, ALU.max))
                chain.settle()
                dve.wait_ge(qe_ready, g + 1)
                nc.vector.tensor_tensor(qf, qf, qe, ALU.add).then_inc(qf_ready, 1)
                dve.wait_ge(o_done, g + 1)
                chain.link(nc.vector.tensor_scalar(rn, ps[:, 6, 0:2 * GN].rearrange("p (h c) -> p h c", h=2), 1e-6, None, ALU.add))
                chain.link(nc.vector.reciprocal(rn, rn))
                dve.wait_ge(y_done, g)
                nc.vector.tensor_tensor(oT, ps[:, 5, 0:2 * GN].rearrange("p (h c) -> p h c", h=2), rn, ALU.mult).then_inc(oT_ready, 1)
                xg = m.x[0:T, bass.ds(g * 2, 2), 0:D]
                dve.wait_ge(y_done, g + 1)
                chain.link(nc.vector.tensor_tensor(xg, xg, ps[0:T, 7, :].rearrange("p (k d) -> p k d", k=2), ALU.add))
                nc.vector.tensor_tensor(xg, xg, m.row_bias[0:T, ROW["bo"], :].unsqueeze(1).to_broadcast([T, 2, D]), ALU.add).then_inc(y_added, 1)
                chain.end(G)

        @block.scalar
        def _(act):
            with act.Fori(0, G) as g:
                act.wait_ge(tp_done, g + 1)
                act.wait_ge(proj, g * 3)
                nc.scalar.copy(xT, ps[:, 0, 0:2 * GN].rearrange("p (h c) -> p h c", h=2)).then_inc(xT_ready, 1)
                act.wait_ge(proj, g * 3 + 1)
                act.wait_ge(table_out, g * 16)
                nc.scalar.copy(table_sb[0:T, :, :], ps[0:T, 1, :].rearrange("p (k d) -> p k d", k=2)).then_inc(table_ready, 1)
                act.wait_ge(km_ready, g + 1)
                nc.scalar.activation(ke[0:T, :, :], kf[0:T, :, :], ACT.Exp).then_inc(ke_ready, 1)
            act.wait_ge(table_out, 16 * G)
            with act.Fori(0, G) as g:
                act.wait_ge(qtp, g + 1)
                act.wait_ge(q_done, g)
                nc.scalar.copy(xT, ps[:, 0, 0:2 * GN].rearrange("p (h c) -> p h c", h=2)).then_inc(qxT, 1)
                act.wait_ge(qm_ready, g * 2 + 2)
                nc.scalar.activation(qe, qm, ACT.Exp).then_inc(qe_ready, 1)

        @block.tensor
        def _(pe):
            pe.wait_ge(made, 9)
            pe.wait_ge(counted, 1)
            nc.tensor.matmul(m.ps[:, 0, 0:NT], tri, cnt, start=True, stop=True)
            nc.tensor.matmul(m.ps[:, 1, 0:NT], ones, cnt, start=True, stop=True).then_inc(totalled, 1)
            pe.wait_ge(x_in, 16 * X_LOADS)
            pe.wait_ge(set_up, 1)
            nc.tensor.matmul(ps[:, 4, 0:258], table_sb[:, 0, 0:P], table_sb[:, :, :].rearrange("p a b -> p (a b)")[:, 0:258],
                             start=True, stop=False, skip_group_check=True)
            with pe.Fori(0, G) as g:
                pe.wait_ge(xn_ready, g * 2 + 2)
                pe.wait_ge(xT_ready, g)
                transpose_group(nc, m, 0, xn).then_inc(tp_done, 1)
                pe.wait_ge(xT_ready, g + 1)
                pe.wait_ge(table_ready, g)
                for n in range(3):
                    if n == 1:
                        pe.wait_ge(km_ready, g)
                    if n == 2:
                        pe.wait_ge(v_ready, 2 * g)
                    for k in range(2):
                        last = rows_times(nc, ps[0:T, 1 + n, k * D:(k + 1) * D], lambda h: xT[:, h, k * T:(k + 1) * T],
                                          lambda h: m.w[:, n, h, :])
                    last.then_inc(proj, 1)
                pe.wait_ge(kf_ready, g + 1)
                pe.wait_ge(v_ready, 2 * g + 2)
                for k in range(2):
                    for h in range(2):
                        last = nc.tensor.matmul(ps[:, 4, 129 * h:129 * h + 129], kf[0:T, k, h * P:(h + 1) * P],
                                                v[0:T, k, 129 * h:129 * h + 129], start=False, stop=False, skip_group_check=True)
                last.then_inc(kv_done, 1)
            pe.wait_ge(kvd_ready, 4)
            with pe.Fori(0, G) as g:
                pe.wait_ge(qxn, g * 2 + 2)
                pe.wait_ge(qxT, g)
                transpose_group(nc, m, 0, xn).then_inc(qtp, 1)
                pe.wait_ge(qxT, g + 1)
                pe.wait_ge(qf_ready, g)
                for o in range(2):
                    for h in range(2):
                        last = nc.tensor.matmul(ps[:, 2, o * GN:(o + 1) * GN], m.w[:, 3, h, o * P:(o + 1) * P], xT[:, h, :],
                                                start=h == 0, stop=h == 1)
                last.then_inc(q_done, 1)
                pe.wait_ge(qf_ready, g + 1)
                pe.wait_ge(oT_ready, g)
                for bank, mat in ((5, kvd), (6, ksd)):
                    for h in range(2):
                        last = nc.tensor.matmul(ps[:, bank, h * GN:(h + 1) * GN], mat[:, h, :], qf[:, h, :], start=True, stop=True)
                last.then_inc(o_done, 1)
                pe.wait_ge(oT_ready, g + 1)
                pe.wait_ge(y_added, g)
                for k in range(2):
                    last = rows_times(nc, ps[0:T, 7, k * D:(k + 1) * D], lambda h: oT[:, h, k * T:(k + 1) * T],
                                      lambda h: m.w[:, 4, h, :])
                last.then_inc(y_done, 1)


def mix1(nc, m, s, chain, e=None):
    W, ps = m.work, m.ps
    xn, xT, k_sb, v_sb = W[:, 0:2, :], W[:, 2:4, 0:GN], W[:, 4:6, :], W[:, 6:8, :]
    logit, prob = W[:, 18, 0:P].rearrange("p (h e) -> p h e", h=2), W[:, 18, P:2 * P].rearrange("p (h e) -> p h e", h=2)
    diag, zero = W[:, 19, :].rearrange("p (h e) -> p h e", h=2), W[:, 21, :]
    if e:
        xn = W[:, 8:10, :]
        bxn = x2 = ln = W[:, 18:20, :]
        bxT = hT = W[:, 20:22, 0:GN]
        qT, h1, attnT = W[:, 4:6, 0:GN], W[:, 6:12, 0:GN], m.attn
    else:
        bxn, x2, ln = xn, W[:, 6:8, :], W[:, 8:10, :]
        bxT, hT = xT, W[:, 10:12, 0:GN]
        qT, h1, attnT = W[:, 4:6, 0:GN], W[:, 12:18, 0:GN], W[:, 20, :].rearrange("p (h e) -> p h e", h=2)
    rs, mx, sm = m.small[0:T, 8:10], m.small[:, 14:16], m.small[:, 16:18]
    col = lambda name, h: m.col_bias[:, COL[name] + h:COL[name] + h + 1]
    both = lambda bank: ps[0:T, bank, :].rearrange("p (k d) -> p k d", k=2)
    halves = lambda bank: ps[:, bank, 0:2 * GN].rearrange("p (h c) -> p h c", h=2)
    row = lambda name: m.row_bias[0:T, ROW[name], :].unsqueeze(1).to_broadcast([T, 2, D])

    def set_up(dve):
        nc.vector.memset(zero, 0.0).then_inc(s["set"], 1)
        nc.vector.memset(diag, 0.0).then_inc(s["set"], 1)

    def first_vector(dve, g, between):
        dve.wait_ge(s["tp"], g)
        for k in range(2):
            normalise(nc, m, xn[0:T, k, :], g, k).then_inc(s["xn"], 1)
        between(0)
        for bank, to, name, bias in ((3, k_sb, "k", "bk1"), (5, v_sb, "v", "bv1")):
            dve.wait_ge(s["kv"], g)
            dve.wait_ge(s[name], g + 1)
            nc.vector.tensor_tensor(to[0:T, :, :], both(bank), row(bias), ALU.add).then_inc(s[name + "_sb"], 1)
        between(1)

    def softmax(dve):
        dve.wait_ge(s["kv"], G)
        for h in range(2):
            for b in range(2):
                chain.did(nc.vector.tensor_copy(logit[64 * b:64 * b + 64, h, :],
                                                ps[64 * b:64 * b + 64, 4, h * P + 64 * b:h * P + 64 * b + 64]))
        chain.settle()
        chain.link(nc.vector.tensor_reduce(mx, logit, AX.X, ALU.max))
        nc.vector.tensor_tensor(logit, logit, mx.unsqueeze(2).to_broadcast([P, 2, 64]), ALU.subtract).then_inc(s["logits"], 1)
        dve.wait_ge(s["exp"], 1)
        chain.link(nc.vector.tensor_reduce(sm, prob, AX.X, ALU.add))
        chain.link(nc.vector.reciprocal(sm, sm))
        dve.wait_ge(s["set"], 2)
        for h in range(2):
            for b in range(2):
                lo, hi = 64 * b, 64 * b + 64
                nc.vector.tensor_scalar(diag[lo:hi, h, lo:hi], prob[lo:hi, h, :], sm[lo:hi, h:h + 1], None, ALU.mult).then_inc(s["attn"], 1)
        dve.wait_ge(s["attn_tp"], 1)

    def second_start(dve, g):
        dve.wait_ge(s["btp"], g)
        dve.wait_ge(s["ln_tp"], g)
        dve.wait_ge(s["x2"], g)
        for k in range(2):
            normalise(nc, m, bxn[0:T, k, :], g, k).then_inc(s["bxn"], 1)

    def second_vector(dve, g, between):
        between(0)
        dve.wait_ge(s["xf"], g + 1)
        dve.wait_ge(s["bxn"], g * 2 + 2)
        if e:
            dve.wait_ge(s["btp"], g + 1)
        chain.link(nc.vector.tensor_tensor(x2[0:T, :, :], both(3), bxn[0:T, :, :], ALU.add))
        group_stats(nc, chain, m, [x2[0:T, k, :] for k in range(2)], rs)
        xg = m.x[0:T, bass.ds(g * 2, 2), 0:D]
        chain.link(nc.vector.tensor_tensor(xg, xg, x2[0:T, :, :], ALU.add))
        for k in range(2):
            nc.vector.tensor_scalar(ln[0:T, k, :], x2[0:T, k, :], m.mv[0:T, k, 0:1], rs[:, k:k + 1],
                                    ALU.subtract, ALU.mult).then_inc(s["ln"], 1)
        dve.wait_ge(s["ln"], 2 * g + 2)
        chain.link(nc.vector.tensor_tensor(xg, xg, row("fc2"), ALU.add))
        between(1)
        dve.wait_ge(s["fc2"], g + 1)
        chain.link(nc.vector.tensor_tensor(xg, xg, both(3), ALU.add))
        nc.vector.memset(m.small[0:1, 30:31], 0.0).then_inc(s["x2"], 1)
        between(2)

    def first_scalar(act, g):
        act.wait_ge(s["tp"], g + 1)
        act.wait_ge(s["v"], g)
        nc.scalar.copy(xT, halves(2)).then_inc(s["xT"], 1)

    def scalar_between(act):
        act.wait_ge(s["logits"], 1)
        nc.scalar.activation(prob, logit, ACT.Exp, scale=64.0 ** -0.5).then_inc(s["exp"], 1)
        act.wait_ge(s["attn_tp"], 1)
        nc.scalar.copy(attnT, ps[:, 3, 0:2 * P].rearrange("p (h e) -> p h e", h=2)).then_inc(s["attnT"], 1)

    def second_scalar(act, g, turns=None):
        act.wait_ge(s["btp"], g + 1)
        act.wait_ge(s["q"], g)
        nc.scalar.copy(bxT, halves(2)).then_inc(s["bxT"], 1)
        act.wait_ge(s["q"], g + 1)
        act.wait_ge(s["xf"], g)
        if turns is not None:
            act.wait_ge(e["y"], turns * (E1 + 1))
        for h in range(2):
            nc.scalar.activation(qT[:, h, :], halves(3)[:, h, :], ACT.Identity, bias=col("bq1", h)).then_inc(s["qT"], 1)
        act.wait_ge(s["ln_tp"], g + 1)
        act.wait_ge(s["fc1"], 3 * g)
        for h in range(2):
            nc.scalar.activation(hT[:, h, :], halves(2)[:, h, :], ACT.Identity, bias=col("norm_b", h),
                                 scale=col("norm_g", h)).then_inc(s["hT"], 1)
        act.wait_ge(s["fc2"], g)
        for o in range(6):
            act.wait_ge(s["fc1"], 3 * g + o // 2 + 1)
            nc.scalar.activation(h1[:, o, :], halves(4 + o // 2 % 2)[:, o % 2, :], ACT.Gelu, bias=col("fc1", o)).then_inc(s["h1"], 1)

    def start_tensor(pe):
        pe.wait_ge(s["set"], 2)
        nc.tensor.matmul(ps[:, 4, 0:D], zero[:, 0:P], zero, start=True, stop=False, skip_group_check=True)

    def first_tensor(pe, g, between):
        pe.wait_ge(s["xn"], g * 2 + 2)
        pe.wait_ge(s["xT"], g)
        transpose_group(nc, m, 2, xn).then_inc(s["tp"], 1)
        between(0)
        pe.wait_ge(s["xT"], g + 1)
        for n, bank, name in ((1, 3, "k"), (2, 5, "v")):
            pe.wait_ge(s[name + "_sb"], g)
            for k in range(2):
                last = rows_times(nc, ps[0:T, bank, k * D:(k + 1) * D], lambda h: xT[:, h, k * T:(k + 1) * T],
                                  lambda h: m.w[:, 3 + n, h, :])
            last.then_inc(s[name], 1)
        between(1)
        pe.wait_ge(s["k_sb"], g + 1)
        pe.wait_ge(s["v_sb"], g + 1)
        for k in range(2):
            for h in range(2):
                last = nc.tensor.matmul(ps[:, 4, h * P:(h + 1) * P], k_sb[0:T, k, h * P:(h + 1) * P],
                                        v_sb[0:T, k, h * P:(h + 1) * P], start=False, stop=False, skip_group_check=True)
        last.then_inc(s["kv"], 1)
        between(2)

    def tensor_between(pe):
        pe.wait_ge(s["attn"], 4)
        for h in range(2):
            last = nc.tensor.transpose(ps[:, 3, h * P:(h + 1) * P], diag[:, h, :], m.ident[:, :])
        last.then_inc(s["attn_tp"], 1)
        pe.wait_ge(s["attnT"], 1)

    def second_tensor(pe, g, between, turns=None):
        if turns is not None:
            pe.wait_ge(e["h"], turns * E1)
            pe.wait_ge(e["h2"], turns * E1)
            pe.wait_ge(e["added"], turns * (E1 + 1))
        pe.wait_ge(s["bxn"], g * 2 + 2)
        pe.wait_ge(s["hT"], 2 * g)
        transpose_group(nc, m, 2, bxn).then_inc(s["btp"], 1)
        between(0)
        pe.wait_ge(s["bxT"], g + 1)
        pe.wait_ge(s["x2"], g)
        for o in range(2):
            for h in range(2):
                last = nc.tensor.matmul(ps[:, 3, o * GN:(o + 1) * GN], m.w[:, 3, h, o * P:(o + 1) * P], bxT[:, h, :],
                                        start=h == 0, stop=h == 1)
        last.then_inc(s["q"], 1)
        between(1)
        pe.wait_ge(s["qT"], 2 * g + 2)
        for k in range(2):
            for h in range(2):
                last = nc.tensor.matmul(ps[0:T, 3, k * D + h * P:k * D + (h + 1) * P], qT[:, h, k * T:(k + 1) * T],
                                        attnT[:, h, :], start=True, stop=True)
        last.then_inc(s["xf"], 1)
        between(2)
        pe.wait_ge(s["ln"], 2 * g + 2)
        transpose_group(nc, m, 2, ln).then_inc(s["ln_tp"], 1)
        between(3)
        pe.wait_ge(s["hT"], 2 * g + 2)
        for o in range(6):
            if o % 2 == 0:
                pe.wait_ge(s["h1"], 6 * g + (2 if o == 4 else 0))
            for h in range(2):
                last = nc.tensor.matmul(halves(4 + o // 2 % 2)[:, o % 2, :], m.w[:, 6 + o // 2, h, (o % 2) * P:(o % 2 + 1) * P],
                                        hT[:, h, :], start=h == 0, stop=h == 1)
            if o % 2:
                last.then_inc(s["fc1"], 1)
                between(4 + o // 2)
        pe.wait_ge(s["h1"], 6 * g + 6)
        pe.wait_ge(s["x2"], g)
        for k in range(2):
            for c in range(6):
                last = nc.tensor.matmul(ps[0:T, 3, k * D:(k + 1) * D], h1[:, c, k * T:(k + 1) * T],
                                        m.w[:, 9 + c // 2, c % 2, :], start=c == 0, stop=c == 5)
        last.then_inc(s["fc2"], 1)
        between(7)

    return {"set_up": set_up, "first_vector": first_vector, "softmax": softmax, "second_start": second_start,
            "second_vector": second_vector,
            "first_scalar": first_scalar, "scalar_between": scalar_between, "second_scalar": second_scalar,
            "start_tensor": start_tensor, "first_tensor": first_tensor, "tensor_between": tensor_between,
            "second_tensor": second_tensor, "marks": s}


SECOND = G * RING
LAST = SECOND + G * 3 * RING
LAST_HALVES = (CHUNKS - EXTRA - LAST) // HALF


def mix1_vector(dve, mix, chain, half):
    mix["set_up"](dve)
    with dve.Fori(0, G) as g:
        mix["first_vector"](dve, g, lambda n: half(g * RING, n))
    mix["softmax"](dve)
    with dve.Fori(0, G) as g:
        chain.begin(g, 1 + STATS_STEPS + 3)
        base = g * (3 * RING) + SECOND

        def between(n):
            for i in ((0,), (1, 2, 3), (4, 5))[n]:
                half(base, i)

        mix["second_start"](dve, g)
        mix["second_vector"](dve, g, between)
        chain.end(G)
    for n in range(LAST_HALVES):
        half(LAST, n)
    half(LAST, LAST_HALVES, EXTRA)


def mix1_scalar(act, mix):
    with act.Fori(0, G) as g:
        mix["first_scalar"](act, g)
    mix["scalar_between"](act)
    with act.Fori(0, G) as g:
        mix["second_scalar"](act, g)


def mix1_tensor(pe, mix, products):
    mix["start_tensor"](pe)
    with pe.Fori(0, G) as g:
        def between(n):
            for i, lo, hi in (((0, 0, 4),), ((0, 4, 8), (1, 0, 2)), ((1, 2, 8),))[n]:
                products(g * RING, i, lo, hi)

        mix["first_tensor"](pe, g, between)
    mix["tensor_between"](pe)
    with pe.Fori(0, G) as g:
        def between(n):
            for i, lo, hi in (((0, 0, 4),), ((0, 4, 8),), ((1, 0, 8),), ((2, 0, 4),), ((2, 4, 6),), ((2, 6, 8),),
                              ((3, 0, 8),), ((4, 0, 8), (5, 0, 8)))[n]:
                products(g * (3 * RING) + SECOND, i, lo, hi)

        mix["second_tensor"](pe, g, between)
    for n in range(LAST_HALVES):
        products(LAST, n)
    products(LAST, LAST_HALVES, 0, EXTRA)


def sorted_edges(m):
    return m.flat[:, 4 * E0 * D:4 * E0 * D + 2 * CHUNKS]


def load_edges_and_experts(nc, m, a, sp, loaded):
    sp.dma_start(sorted_edges(m), m.sorted.rearrange("(p c) f -> p (c f)", p=P)).then_inc(loaded, 16)
    sp.wait_ge(loaded, 16)
    for n, name in enumerate(("L0_ffn_w1", "L0_ffn_w2")):
        sp.dma_start(m.flat[:, n * 2 * E0 * D:(n + 1) * 2 * E0 * D].rearrange("p (e n) -> p e n", n=D),
                     a[name].rearrange("e (k p) n -> p (e k) n", p=P)).then_inc(loaded, 16)


def decode(nc, m, dve, chain, loaded):
    raw = sorted_edges(m).rearrange("p (c f) -> p c f", f=2)
    spare = m.work[:, :, :].rearrange("p a b -> p (a b)")
    node, local = spare[:, 0:CHUNKS].bitcast(I32), spare[:, CHUNKS:2 * CHUNKS].bitcast(I32)
    dve.wait_ge(loaded, 16)
    chain.did(nc.vector.memset(m.lew[:, CHUNKS:CHUNKS + AHEAD, :], 0.0))
    chain.link(nc.vector.tensor_copy(node, raw[:, :, 0]))
    chain.did(nc.vector.tensor_scalar(local, node, P - 1, None, ALU.bitwise_and))
    chain.did(nc.vector.tensor_scalar(m.dst, node, 7, None, ALU.arith_shift_right))
    chain.settle()
    chain.did(nc.vector.tensor_copy(m.lew[:, 0:CHUNKS, 0], local))
    chain.did(nc.vector.tensor_copy(m.lew[:, 0:CHUNKS, 1], raw[:, :, 1]))
    chain.settle()


def group_sums(nc, m, layer, marks, chain):
    width = D + 1 if layer == 0 else D
    loaded, decoded, ones_set, idx_in = marks["loaded"], marks["decoded"], marks["ones_set"], marks["idx"]
    hot_ready, summed, added, row_in = marks["hot"], marks["summed"], marks["bank_free"], m.row_in[layer]
    STAGE, PART = CAP, 4
    idx = m.idx_all.rearrange("p (s j) -> p s j", s=2)
    assert STAGE > LONG

    def gpsimd(pool):
        if layer == 0:
            nc.gpsimd.memset(m.long_rows[:, :, D:D + 1], 1.0).then_inc(ones_set, 1)
            pool.wait_ge(decoded, 1)

        def fetch(f, first):
            for b in range(PER // STAGE):
                for j in range(STAGE):
                    n = b * STAGE + j
                    new = first and n + PART <= LONG
                    if j % PART == 0 and not new:
                        pool.wait_ge(summed, f * PER + (min(n + PART, (b + 1) * STAGE) - LONG))
                    if j == 0:
                        nc.gpsimd.tensor_copy(idx[:, b % 2, :], m.dst[:, bass.ds(f * PER + n, STAGE)]).then_inc(idx_in, 1)
                        pool.wait_ge(idx_in, f * (PER // STAGE) + b + 1)
                        apart(nc, m)
                    elif j % PART == 0 and not new:
                        apart(nc, m)
                    nc.gpsimd.indirect_dma_start(
                        out=m.long_rows[:, n % LONG, 0:D], out_offset=None, in_=m.table[layer],
                        in_offset=bass.IndirectOffsetOnAxis(ap=idx[:, b % 2, j:j + 1], axis=0)).then_inc(row_in[n % LONG // 2], 16)

        fetch(0, True)
        with pool.Fori(1, G) as f:
            fetch(f, False)
        for pair in row_in:
            pool.wait_ge(pair, 32 * (CHUNKS // LONG))

    def build(dve, f, b, first=False):
        if not first:
            dve.wait_ge(summed, f * PER + ((b + 1) * BATCH - LONG))
        for j in range(b * BATCH, (b + 1) * BATCH):
            nc.vector.tensor_scalar(m.long_hot[:, j % LONG, :], m.iota[:, 0:T], m.lew[:, bass.ds(f * PER + j, 1), 0],
                                    m.lew[:, bass.ds(f * PER + j, 1), 1], ALU.is_equal, ALU.mult).then_inc(hot_ready, 1)

    def add(dve, f, k):
        dve.wait_ge(summed, f * PER + (k + 1) * CAP)
        if layer == 1 and k == 0:
            dve.wait_ge(loaded, f * 16 + 16)
        to = tile_of(m.x, f * 2 + k, D + 1) if layer == 0 else m.group[0:T, k, :]
        nc.vector.tensor_tensor(to, to, m.ps[0:T, 6 + k, 0:width], ALU.add).then_inc(added, 1)

    def vector(dve, f, slot, first=False):
        if slot == 1 and not first:
            add(dve, f - 1, 1)
        if slot == SLOTS - 3:
            add(dve, f, 0)
        build(dve, f, slot + AHEAD // BATCH, first and (slot + AHEAD // BATCH + 1) * BATCH <= LONG)

    def tensor(pe, f, slot, first=False, lo=0, hi=BATCH):
        for j in range(slot * BATCH + lo, slot * BATCH + hi):
            pe.wait_ge(row_in[j % LONG // 2], f * (PER // LONG * 32) + (j // LONG * 32 + 32))
            pe.wait_ge(hot_ready, f * PER + j + 1)
            if j % CAP == 0 and not first:
                pe.wait_ge(added, f * 2 + (j // CAP - 1))
            nc.tensor.matmul(m.ps[0:T, 6 + j // CAP, 0:width], m.long_hot[:, j % LONG, :], m.long_rows[:, j % LONG, 0:width],
                             start=j % CAP == 0, stop=j % CAP == CAP - 1).then_inc(summed, 1)

    def start_vector(dve, first_done=None, between=None):
        if layer == 0:
            decode(nc, m, dve, chain, loaded)
            nc.vector.memset(m.small[0:1, 4:5], 0.0).then_inc(decoded, 1)
        for b in range(AHEAD // BATCH):
            build(dve, 0, b, True)
        for f in range(2):
            for slot in range(SLOTS):
                vector(dve, f, slot, f == 0)
                if f == 1 and slot == 1 and first_done:
                    first_done(0)
                if between:
                    between(f * SLOTS + slot)

    def start_tensor(pe, beside=None):
        if layer == 0:
            pe.wait_ge(ones_set, 1)
        for f in range(2):
            for slot in range(SLOTS):
                if beside:
                    beside(f * SLOTS + slot, lambda n: tensor(pe, f, slot, f == 0, 2 * n, 2 * n + 2))
                else:
                    tensor(pe, f, slot, f == 0)
        if layer == 0:
            pe.wait_ge(loaded, 48)

    return {"gpsimd": gpsimd, "vector": vector, "tensor": tensor, "start_vector": start_vector,
            "start_tensor": start_tensor, "add": add, "added": added, "loaded": loaded, "decoded": decoded}


def gather_sums(nc, m, a, layer, marks, mix, chain):
    width = D + 1 if layer == 0 else D
    into = m.x if layer == 0 else m.acc
    banks = (0, 1, 6, 7)
    loaded, decoded, ones_set, idx_in = marks["loaded"], marks["decoded"], marks["ones_set"], marks["idx"]
    row_in = m.row_in[layer]
    hot_ready, summed, bank_free = marks["hot"], marks["summed"], marks["bank_free"]
    trips = CHUNKS // RING
    assert trips % 2 == 1 and EXTRA % 2 == 0

    def sync(sp):
        if layer == 0:
            load_edges_and_experts(nc, m, a, sp, loaded)
            sp.wait_ge(loaded, 48)
        else:
            rows = m.table[1].rearrange("(t p) d -> p t d", p=T)
            for n in range(5):
                sp.dma_start(m.acc[0:T, 10 * n:10 * n + 10, :], rows[:, 10 * n:10 * n + 10, :]).then_inc(loaded, 16)
            sp.wait_ge(loaded, 80)

    def gpsimd(pool):
        nc.gpsimd.memset(m.rows[:, :, D:D + 1], 1.0).then_inc(ones_set, 1)
        pool.wait_ge(decoded, 1)

        def fetch(i, h, used, count=HALF):
            if used is not None:
                pool.wait_ge(summed, used)
            nc.gpsimd.tensor_copy(m.idx[:, h % 4, 0:count], m.dst[:, bass.ds(i * 4 * HALF + h * HALF, count)]).then_inc(idx_in, 1)
            pool.wait_ge(idx_in, i * 4 + h + 1)
            apart(nc, m)
            for j in range(count):
                s = (h % 2) * HALF + j
                if used is not None and j == HALF // 2:
                    pool.wait_ge(summed, used + HALF // 2)
                    apart(nc, m)
                nc.gpsimd.indirect_dma_start(
                    out=m.rows[:, s, 0:D], out_offset=None, in_=m.table[layer],
                    in_offset=bass.IndirectOffsetOnAxis(ap=m.idx[:, h % 4, j:j + 1], axis=0)).then_inc(row_in[s // 2], 16)

        fetch(0, 0, None)
        fetch(0, 1, None)
        with pool.Fori(0, (trips - 1) // 2) as i:
            for h in range(2, 6):
                fetch(i, h, i * 4 * HALF + (h - 2) * HALF + HALF // 2)
        fetch((trips - 1) // 2, 2, (trips - 1) * RING + HALF // 2, EXTRA)
        for s in range(RING // 2):
            pool.wait_ge(row_in[s], 32 * trips + 16 * min(2, max(0, EXTRA - 2 * s)))

    def vector(dve):
        if layer == 0:
            decode(nc, m, dve, chain, loaded)
        for b in range(len(banks)):
            nc.vector.memset(m.small[0:1, b:b + 1], 0.0).then_inc(bank_free, 1)
        nc.vector.memset(m.small[0:1, 4:5], 0.0).then_inc(decoded, 1)

        def build(base, n, j):
            c = base + (n * HALF + j)
            nc.vector.tensor_scalar(m.hot[:, (n % 2) * HALF + j, :], m.iota[:, 0:T],
                                    m.lew[:, bass.ds(c, 1), 0], m.lew[:, bass.ds(c, 1), 1],
                                    ALU.is_equal, ALU.mult).then_inc(hot_ready, 1)

        def half(base, n, count=HALF):
            nc.vector.reg_load(regs, m.blk[0:1, bass.ds(base + n * HALF, HALF)])
            dve.wait_ge(summed, base + n * HALF)
            for j in range(count):
                if count == HALF:
                    build(base, n + 1, j)
                t = nc.vector.snap(regs[j], min_val=0, max_val=NT - 1)
                c = base + (n * HALF + j)
                dve.wait_ge(summed, c + 1)
                dve.wait_ge(bank_free, c + len(banks))
                to = tile_of(into, t, width)
                nc.vector.tensor_tensor(to, to, m.ps[0:T, banks[j % 4], 0:width], ALU.add).then_inc(bank_free, 1)

        regs = [nc.vector.alloc_register(f"tile{layer}_{j}") for j in range(HALF)]
        for j in range(HALF):
            build(0, 0, j)
        if layer == 0:
            with dve.Fori(0, trips) as i:
                half(i * RING, 0)
                half(i * RING, 1)
            half(trips * RING, 0, EXTRA)
        else:
            dve.wait_ge(loaded, 80)
            mix1_vector(dve, mix, chain, half)
        for r in regs:
            nc.vector.free_register(r)

    def scalar(act):
        if layer:
            mix1_scalar(act, mix)

    def tensor(pe):
        pe.wait_ge(ones_set, 1)

        def products(base, n, lo=0, hi=HALF):
            for j in range(lo, hi):
                c, s = base + (n * HALF + j), (n % 2) * HALF + j
                pe.wait_ge(row_in[s // 2], base * (32 // RING) + (n // 2) * 32 + 32)
                pe.wait_ge(hot_ready, c + 1)
                pe.wait_ge(bank_free, c + 1)
                nc.tensor.matmul(m.ps[0:T, banks[j % 4], 0:width], m.hot[:, s, :], m.rows[:, s, 0:width],
                                 start=True, stop=True).then_inc(summed, 1)

        if layer == 0:
            with pe.Fori(0, trips) as i:
                products(i * RING, 0)
                products(i * RING, 1)
            products(trips * RING, 0, 0, EXTRA)
        else:
            mix1_tensor(pe, mix, products)

    return {"sync": sync, "gpsimd": gpsimd, "vector": vector, "scalar": scalar, "tensor": tensor}


def experts(nc, m, a, layer, s, chain, out=None, group_part=None, mix=None):
    EX, DEEP = (E0, 2) if layer == 0 else (E1, 3)
    W, ps = m.work, m.ps
    w = (m.flat if layer == 0 or group_part else m.region)[:, 0:EX * DEEP * 2 * D].rearrange("p (e k n) -> p e k n", k=KD, n=D)
    xn, xT = W[:, 0:2, :], W[:, 2:4, 0:GN]
    hid = [W[:, 4 + 2 * i:6 + 2 * i, 0:GN] for i in range(2)]
    hid2 = [W[:, 8 + 2 * i:10 + 2 * i, 0:GN] for i in range(2)]
    rw = W[:, 12, :].rearrange("p (h n) -> p h n", h=2)
    rw2, rb2, rT = W[:, 13, 0:E1], W[:, 13, 16:16 + E1], W[:, 14, 0:GN]
    b_out = W[0:EX, 15, :]
    cT = W[0:EX, 16, 0:GN]
    r = W[0:T, 17, :]
    lg, best, comb, other = (r[:, 16 * n:16 * n + 16].rearrange("p (k e) -> p k e", k=2) for n in range(4))
    bi = r[:, 64:80].bitcast(U32).rearrange("p (k e) -> p k e", k=2)
    bif = r[:, 80:84].rearrange("p (k e) -> p k e", k=2)
    gap, th, w1, w2, mx, sm = (r[:, 84 + 2 * n:86 + 2 * n] for n in range(6))
    ex = r[:, 100:116].rearrange("p (k e) -> p k e", k=2)
    nsteps = EX + DEEP - 1
    u_bank = (lambda e: 2) if mix else (lambda e: 2 + e % 2)
    v_bank = (lambda e: 3) if mix else (lambda e: 6 + e % 2)
    if layer == 0:
        pe_slots = dve_slots = {n: (n + 2,) for n in range(SLOTS - 2)}
        ahead, pe_behind, dve_behind = (0,), (1,), (1,)
    else:
        ahead, pe_behind, dve_behind = (), (6,), (6,)
        pe_slots, dve_slots = {0: (7,), 2: (8,), 4: (9,), 5: (10,)}, {n: (n + 7,) for n in range(4)}
    agg, aT, h7T = xn, W[:, 18:20, 0:GN], W[:, 20:22, 0:GN]
    y_tab, ry = W[:, 18:20, :], r[:, 116:118]
    root = m.small[0:T, 8:10]
    halves = lambda bank: ps[:, bank, 0:2 * GN].rearrange("p (h c) -> p h c", h=2)
    col = lambda n: m.col_bias[:, COL["expert"] + n:COL["expert"] + n + 1]
    YS = EX + 1
    if out is not None:
        to = out.rearrange("(t p) d -> p t d", p=T)

    if layer == 0:
        cols = [("L0_ffn_b1", 0)]
        rows = "L0_ffn_b2"
        n_loads = 1 + 1 + 1
    else:
        parts = [("L1_ffn_expert_w1", 0), ("L1_ffn_expert_w2", EX), ("L1_ffn_expert_w3", 2 * EX)]
        cols = [("L1_ffn_expert_b1", 0), ("L1_ffn_expert_b2", 2 * EX)]
        rows = "L1_ffn_expert_b3"
        n_loads = 3 + 2 + 1 + 3

    def sync(sp):
        if group_part and layer == 0:
            load_edges_and_experts(nc, m, a, sp, group_part["loaded"])
            sp.wait_ge(group_part["loaded"], 48)
            sp.wait_ge(group_part["decoded"], 1)
        elif group_part:
            rows_dram = m.table[1].rearrange("(t p) d -> p t d", p=T)
            sp.dma_start(m.group[0:T, :, :], rows_dram[:, 0:2, :]).then_inc(group_part["loaded"], 16)
        with nc.allow_non_contiguous_dma(reason="biases and router weights, one channel in each partition"):
            if layer == 0:
                sp.dma_start(rw[:, :, 0:EX], a["L0_ffn_router_w"].rearrange("(h p) e -> p h e", p=P)).then_inc(s["in"], 16)
            else:
                sp.dma_start(rw, a["L1_ffn_router_w1"].rearrange("(h p) e -> p h e", p=P)).then_inc(s["in"], 16)
                sp.dma_start(rw2, a["L1_ffn_router_w2"]).then_inc(s["in"], 16)
                sp.dma_start(rb2, a["L1_ffn_router_b2"].rearrange("(a e) -> a e", a=1).to_broadcast([P, E1])).then_inc(s["in"], 16)
            for name, at in cols:
                sp.dma_start(m.col_bias[:, COL["expert"] + at:COL["expert"] + at + 2 * EX],
                             a[name].rearrange("e (h p) -> p (e h)", p=P)).then_inc(s["in"], 16)
        sp.dma_start(b_out, a[rows]).then_inc(s["in"], 16)
        if layer == 1:
            for name, at in parts:
                sp.dma_start(w[:, at:at + EX, :, :].rearrange("p e k n -> p (e k) n"),
                             a[name].rearrange("e (k p) n -> p (e k) n", p=P)).then_inc(s["in"], 16)
        else:
            parts1 = [(n, a[w]) for n, w in enumerate(("L1_gnn_W", "L1_gnn_W1", "L1_gnn_W2"))]
            parts1 += [(3 + n, a["L1_mix_w_qkv"][:, n * D:(n + 1) * D]) for n in range(3)]
            parts1 += [(6 + n, a["L1_mix_w_fc1"][:, n * D:(n + 1) * D]) for n in range(3)]
            parts1 += [(9 + n, a["L1_mix_w_fc2"][n * D:(n + 1) * D, :]) for n in range(3)]
            for n, src in parts1:
                sp.dma_start(m.w[:, n, :, :], src.rearrange("(k p) n -> p k n", p=P)).then_inc(s["w_in"], 16)
            to_table = m.table[1].rearrange("(t p) d -> p t d", p=T)
            with sp.Fori(0, G) as g:
                sp.wait_ge(s["table"], 2 * g + 2)
                sp.dma_start(to_table[:, bass.ds(g * 2, 2), :], y_tab[0:T, :, :]).then_inc(s["table_out"], 16)
            sp.wait_ge(s["table_out"], 16 * G)
            sp.wait_ge(s["w_in"], 16 * len(parts1))
        if layer == 1:
            def store(g):
                sp.wait_ge(s["group"], g + 1)
                sp.dma_start(to[:, bass.ds(g * 2, 2), :], m.x[0:T, bass.ds(g * 2, 2), 0:D]).then_inc(s["stored"], 16)

            def self_loops(f):
                sp.wait_ge(s["agg"], f * 2)
                sp.dma_start(m.group[0:T, :, :], rows_dram[:, bass.ds(f * 2, 2), :]).then_inc(group_part["loaded"], 16)

            if group_part:
                self_loops(1)
                with sp.Fori(0, G - 2) as g:
                    self_loops(g + 2)
                    store(g)
                store(G - 2)
                store(G - 1)
                sp.wait_ge(group_part["loaded"], 16 * G)
            else:
                with sp.Fori(0, G) as g:
                    store(g)
            sp.wait_ge(s["stored"], 16 * G)

    def vector(dve):
        if layer == 1:
            chain.link(nc.vector.memset(r[:, 0:64], -1.0))

        def sums(g):
            dve.wait_ge(s["tp"], g)
            if group_part:
                dve.wait_ge(group_part["added"], 2 * g + 2)
            for k in range(2):
                t = g * 2 + k
                of = m.group[0:T, k, :] if group_part else tile_of(m.acc, t, D)
                nc.vector.tensor_scalar(agg[0:T, k, :], of, m.dinv[0:T, bass.ds(t, 1)], None, ALU.mult).then_inc(s["agg"], 1)

        def prepare(g):
            if layer == 1:
                xg = m.x[0:T, bass.ds(g * 2, 2), 0:D]
                dve.wait_ge(s["head"], g + 1)
                chain.link(nc.vector.tensor_tensor(xg, xg, ps[0:T, 1, :].rearrange("p (k d) -> p k d", k=2), ALU.add))
                chain.link(nc.vector.tensor_tensor(xg, xg, m.row_bias[0:T, ROW["gnn_b2"], :].unsqueeze(1).to_broadcast([T, 2, D]), ALU.add))
            if group_part and layer == 0:
                dve.wait_ge(group_part["added"], 2 * g + 2)
            group_stats(nc, chain, m, [tile_of(m.x, g * 2 + k, D) for k in range(2)], root)
            dve.wait_ge(s["tp"], g)
            for k in range(2):
                nc.vector.tensor_scalar(xn[0:T, k, :], tile_of(m.x, g * 2 + k, D), m.mv[0:T, k, 0:1], root[:, k:k + 1],
                                        ALU.subtract, ALU.mult).then_inc(s["xn"], 1)

        def next_table(g):
            group_stats(nc, chain, m, [tile_of(m.x, g * 2 + k, D) for k in range(2)], root)
            both = bass.ds(g * 2, 2)
            deg, pos, inv = (m.small[0:T, n:n + 2] for n in (20, 22, 28))
            chain.link(nc.vector.tensor_scalar(deg, m.x[0:T, both, D], 1.0, None, ALU.add))
            chain.link(nc.vector.tensor_scalar(pos, deg, 0.0, None, ALU.is_gt))
            chain.link(nc.vector.tensor_scalar(deg, deg, 1e-30, None, ALU.max))
            inverse_root(nc, chain, inv, deg, 0.0, m.small[0:T, 24:26], m.small[0:T, 26:28])
            chain.link(nc.vector.tensor_tensor(m.dinv[0:T, both], inv, pos, ALU.mult))
            chain.did(nc.vector.tensor_scalar(m.mean[0:T, both], m.mv[0:T, :, 0], 0.0, None, ALU.add))
            chain.did(nc.vector.tensor_scalar(m.rstd[0:T, both], root, 0.0, None, ALU.add))
            chain.link(nc.vector.tensor_tensor(ry, root, m.dinv[0:T, both], ALU.mult))
            dve.wait_ge(s["table_out"], 16 * g)
            for k in range(2):
                nc.vector.tensor_scalar(y_tab[0:T, k, :], tile_of(m.x, g * 2 + k, D), m.mv[0:T, k, 0:1], ry[:, k:k + 1],
                                        ALU.subtract, ALU.mult).then_inc(s["table"], 1)
            dve.wait_ge(s["table"], 2 * g + 2)

        if mix:
            mix["set_up"](dve)
            group_part["start_vector"](dve, sums, lambda n: mix["first_vector"](dve, n, nothing))
            with dve.Fori(2 * SLOTS, G) as g:
                mix["first_vector"](dve, g, nothing)
            mix["softmax"](dve)
            mix["second_start"](dve, 0)
            mix["second_vector"](dve, 0, nothing)
        elif group_part:
            group_part["start_vector"](dve)
        elif layer == 1:
            sums(0)
        prepare(0)
        if mix:
            mix["second_start"](dve, 1)

        def router(g):
            dve.wait_ge(s["logits"], g + 1)
            both = ps[0:T, 1, 0:16].rearrange("p (k e) -> p k e", k=2)[:, :, 0:EX]
            if layer == 0:
                chain.link(nc.vector.tensor_copy(lg, both))
                values = lg
            else:
                chain.link(nc.vector.tensor_tensor(lg[:, :, 0:EX], both, rb2[0:T, :].unsqueeze(1).to_broadcast([T, 2, EX]), ALU.add))
                chain.link(nc.vector.tensor_reduce(mx, lg[:, :, 0:EX], AX.X, ALU.max))
                nc.vector.tensor_tensor(ex[:, :, 0:EX], lg[:, :, 0:EX], mx.unsqueeze(2).to_broadcast([T, 2, EX]), ALU.subtract).then_inc(s["gap"], 1)
                dve.wait_ge(s["th"], 2 * g + 1)
                chain.link(nc.vector.tensor_reduce(sm, ex[:, :, 0:EX], AX.X, ALU.add))
                chain.link(nc.vector.reciprocal(sm, sm))
                chain.link(nc.vector.tensor_tensor(other[:, :, 0:EX], ex[:, :, 0:EX], sm.unsqueeze(2).to_broadcast([T, 2, EX]), ALU.mult))
                values = other
            chain.apart()
            for k in range(2):
                chain.did(nc.vector.max(best[:, k, :], values[:, k, :]))
            chain.settle_apart()
            for k in range(2):
                chain.did(nc.vector.max_index(bi[:, k, :], best[:, k, :], values[:, k, :]))
            chain.settle()
            chain.did(nc.vector.tensor_copy(bif, bi[:, :, 0:2]))
            nc.vector.tensor_tensor(gap, best[:, :, 0], best[:, :, 1], ALU.subtract).then_inc(s["gap"], 1)
            chain.settle()

        def weigh(g):
            if layer == 0:
                dve.wait_ge(s["th"], g + 1)
                chain.did(nc.vector.tensor_scalar(w1, th, 0.5, 0.5, ALU.mult, ALU.add))
                chain.did(nc.vector.tensor_scalar(w2, th, -0.5, 0.5, ALU.mult, ALU.add))
                chain.settle()
            else:
                dve.wait_ge(s["th"], 2 * g + 2)
                chain.link(nc.vector.tensor_scalar(w1, th, 1.0, None, ALU.add))
                chain.link(nc.vector.reciprocal(w1, w1))
                chain.link(nc.vector.tensor_tensor(w2, th, w1, ALU.mult))
            dve.wait_ge(s["ctp"], g)
            for k in range(2):
                chain.did(nc.vector.tensor_scalar(comb[:, k, :], m.iota[0:T, 0:8], bif[:, k, 0:1], w1[:, k:k + 1], ALU.is_equal, ALU.mult))
                chain.did(nc.vector.tensor_scalar(lg[:, k, :], m.iota[0:T, 0:8], bif[:, k, 1:2], w2[:, k:k + 1], ALU.is_equal, ALU.mult))
            chain.settle()
            nc.vector.tensor_tensor(comb, comb, lg, ALU.add).then_inc(s["comb"], 1)
            dve.wait_ge(s["comb"], g + 1)

        def turn(g, last, fed=True, first_unfed=False):
            xg = m.x[0:T, bass.ds(g * 2, 2), 0:D]
            slot = (lambda n: group_part["vector"](dve, g + 2, n)) if group_part and fed else (lambda n: None)
            for n in ahead:
                slot(n)
            if first_unfed:
                group_part["add"](dve, G - 1, 1)
            if mix and not last:
                mix["second_vector"](dve, g + 1, lambda n: each(slot, ((0, 1), (2, 3, 4, 5), ())[n]))
            router(g)
            if layer == 0:
                chain.link(nc.vector.tensor_tensor(xg, xg, xn[0:T, :, :], ALU.add))
            for n in dve_behind:
                slot(n)
            weigh(g)
            if layer == 1 and not last:
                sums(g + 1)
            for n in range(YS):
                if n == 4 and not last:
                    prepare(g + 1)
                    if mix and fed:
                        mix["second_start"](dve, g + 2)
                for i in dve_slots.get(n, ()):
                    slot(i)
                dve.wait_ge(s["y"], g * YS + n + 1)
                y = ps[0:T, 4 + n % 2, :].rearrange("p (k d) -> p k d", k=2)
                if n < EX:
                    for k in range(2):
                        to = tile_of(m.x, g * 2 + k, D)
                        chain.did(nc.vector.scalar_tensor_tensor(to, y[:, k, :], comb[:, k, n:n + 1], to, ALU.mult, ALU.add))
                    chain.settle()
                    nc.vector.memset(m.small[0:1, 6:7], 0.0).then_inc(s["added"], 1)
                else:
                    nc.vector.tensor_tensor(xg, xg, y, ALU.add).then_inc(s["added"], 1)
                    dve.wait_ge(s["added"], g * YS + YS)
            if layer == 1:
                nc.vector.memset(m.small[0:1, 7:8], 0.0).then_inc(s["group"], 1)
            else:
                next_table(g)

        steps = (1 if layer == 0 else 5) + 2 + 2 + 1 + (1 if layer == 0 else 0) + (2 if layer == 0 else 3) + 4 + 2 * EX
        steps += STATS_STEPS + (2 if layer == 1 else STATS_STEPS + 3 + 3 + 13 + 1)
        steps += 1 + STATS_STEPS + 3 if mix else 0
        fed = G - 2 if group_part else G - 1
        with dve.Fori(0, fed) as g:
            chain.begin(g, steps)
            turn(g, False)
            chain.end(fed)
        if group_part:
            turn(G - 2, False, False, True)
        turn(G - 1, True, False)

    def scalar(act):
        def head(g, stage):
            if stage == 0:
                act.wait_ge(s["agg_tp"], g + 1)
                act.wait_ge(s["head"], g)
                nc.scalar.copy(aT, halves(0)).then_inc(s["aT"], 1)
            elif stage == 1:
                act.wait_ge(s["h7"], g + 1)
                act.wait_ge(s["hid"], g)
                for h in range(2):
                    nc.scalar.activation(h7T[:, h, :], halves(1)[:, h, :], ACT.Identity,
                                         bias=m.col_bias[:, COL["gnn_b"] + h:COL["gnn_b"] + h + 1]).then_inc(s["h7T"], 1)
            else:
                act.wait_ge(s["hid"], g + 1)
                for h in range(2):
                    nc.scalar.activation(aT[:, h, :], halves(0)[:, h, :], ACT.Relu,
                                         bias=m.col_bias[:, COL["gnn_b1"] + h:COL["gnn_b1"] + h + 1]).then_inc(s["hidT"], 1)

        if mix:
            with act.Fori(0, G) as g:
                mix["first_scalar"](act, g)
            mix["scalar_between"](act)
            mix["second_scalar"](act, 0)
        if layer == 1:
            for stage in range(3):
                head(0, stage)
        act.wait_ge(s["tp"], 1)
        nc.scalar.copy(xT, halves(0)).then_inc(s["xT"], 1)

        def evacuate(g, e, bank, to, ready, wrote, readers, func, bias):
            act.wait_ge(s[ready], g * EX + e + 1)
            per, count = readers
            act.wait_ge(s[per], g * count + max(e - 1, 0))
            for h in range(2):
                ins = nc.scalar.activation(to[:, h, :], halves(bank)[:, h, :], func, bias=col(bias + h))
            ins.then_inc(s[wrote], 1)

        def turn(g, last):
            if mix and not last:
                mix["second_scalar"](act, g + 1, g)
                act.wait_ge(mix["marks"]["fc2"], g + 2)
            if layer == 1:
                act.wait_ge(s["rh"], g + 1)
                nc.scalar.activation(rT, ps[:, 1, 16:16 + GN], ACT.Relu, bias=m.col_bias[:, COL["router_b1"]:COL["router_b1"] + 1]).then_inc(s["rT"], 1)
            for step in range(nsteps):
                if step < EX:
                    evacuate(g, step, u_bank(step), hid[step % 2], "u", "h", ("y", YS) if DEEP == 2 else ("v", EX),
                             ACT.Gelu if layer == 0 else ACT.Relu, 2 * step)
                if DEEP == 3 and 1 <= step <= EX:
                    e = step - 1
                    evacuate(g, e, v_bank(e), hid2[e % 2], "v", "h2", ("y", YS), ACT.Relu, 2 * EX + 2 * e)
                if step == 0:
                    act.wait_ge(s["gap"], (g + 1) if layer == 0 else (2 * g + 1))
                    if layer == 0:
                        nc.scalar.activation(th, gap, ACT.Tanh, scale=0.5).then_inc(s["th"], 1)
                    else:
                        nc.scalar.activation(ex[:, :, 0:EX], ex[:, :, 0:EX], ACT.Exp).then_inc(s["th"], 1)
                        act.wait_ge(s["gap"], 2 * g + 2)
                        nc.scalar.activation(th, gap, ACT.Exp, scale=-1.0).then_inc(s["th"], 1)
                if step == 2:
                    act.wait_ge(s["ctp"], g + 1)
                    nc.scalar.copy(cT, ps[0:EX, 1, 0:GN]).then_inc(s["cT"], 1)
                if layer == 1 and step in (3, 4, 5) and not last:
                    head(g + 1, step - 3)
                if step == nsteps - 1 and not last:
                    act.wait_ge(s["tp"], g + 2)
                    nc.scalar.copy(xT, halves(0)).then_inc(s["xT"], 1)

        if mix:
            nc.scalar.activation(m.small[0:1, 32:33], m.ident[0:1, 0:1], ACT.Exp)
        with act.Fori(0, G - 1) as g:
            turn(g, False)
        turn(G - 1, True)

    def tensor(pe):
        def head(g, stage):
            if stage == 0:
                pe.wait_ge(s["agg"], 2 * g + 2)
                pe.wait_ge(s["xT"], g)
                transpose_group(nc, m, 0, agg).then_inc(s["agg_tp"], 1)
            elif stage == 3:
                pe.wait_ge(s["hidT"], 2 * g + 2)
                for k in range(2):
                    last = rows_times(nc, ps[0:T, 1, k * D:(k + 1) * D], lambda h: aT[:, h, k * T:(k + 1) * T], lambda h: m.w[:, 2, h, :])
                last.then_inc(s["head"], 1)
            else:
                if stage == 1:
                    pe.wait_ge(s["aT"], g + 1)
                    pe.wait_ge(s["cT"], g)
                else:
                    pe.wait_ge(s["h7T"], 2 * g + 2)
                of, bank, done = (aT, 1, "h7") if stage == 1 else (h7T, 0, "hid")
                for o in range(2):
                    for h in range(2):
                        last = nc.tensor.matmul(ps[:, bank, o * GN:(o + 1) * GN], m.w[:, stage - 1, h, o * P:(o + 1) * P],
                                                of[:, h, :], start=h == 0, stop=h == 1)
                last.then_inc(s[done], 1)

        if mix:
            mix["start_tensor"](pe)
            group_part["start_tensor"](pe, lambda n, part: mix["first_tensor"](pe, n, part))
            with pe.Fori(2 * SLOTS, G) as g:
                mix["first_tensor"](pe, g, nothing)
            mix["tensor_between"](pe)
            mix["second_tensor"](pe, 0, nothing)
        elif group_part:
            group_part["start_tensor"](pe)
        if layer == 1:
            for stage in range(4):
                head(0, stage)
        pe.wait_ge(s["xn"], 2)
        transpose_group(nc, m, 0, xn).then_inc(s["tp"], 1)

        def square(g, e, at, of, bank, done, free):
            pe.wait_ge(s[free], g * EX + (e if mix else max(e - 1, 0)))
            for o in range(2):
                for h in range(2):
                    last = nc.tensor.matmul(ps[:, bank, o * GN:(o + 1) * GN], w[:, at + e, h, o * P:(o + 1) * P], of[:, h, :],
                                            start=h == 0, stop=h == 1)
            last.then_inc(s[done], 1)

        def rows_out(g, e):
            pe.wait_ge(s["h" if DEEP == 2 else "h2"], g * EX + e + 1)
            pe.wait_ge(s["added"], g * YS + max(e - 1, 0))
            of = (hid if DEEP == 2 else hid2)[e % 2]
            for k in range(2):
                last = rows_times(nc, ps[0:T, 4 + e % 2, k * D:(k + 1) * D], lambda h: of[:, h, k * T:(k + 1) * T],
                                  lambda h: w[:, (DEEP - 1) * EX + e, h, :])
            last.then_inc(s["y"], 1)

        pe.wait_ge(s["in"], 16 * n_loads)

        def turn(g, last_turn, fed=True):
            slot = (lambda n: group_part["tensor"](pe, g + 2, n)) if group_part and fed else (lambda n: None)
            for n in ahead:
                slot(n)
            if mix and not last_turn:
                mix["second_tensor"](pe, g + 1, lambda n: each(slot, ((0,), (1,), (2, 3), (4,), (), (), (5,), ())[n]), g)
            pe.wait_ge(s["xT"], g + 1)
            pe.wait_ge(s["cT"], g)
            if layer == 1:
                for h in range(2):
                    last = nc.tensor.matmul(ps[:, 1, 16:16 + GN], rw[:, h, :], xT[:, h, :], start=h == 0, stop=h == 1)
                last.then_inc(s["rh"], 1)
                for n in pe_behind:
                    slot(n)
                pe.wait_ge(s["rT"], g + 1)
            for k in range(2):
                if layer == 0:
                    for h in range(2):
                        last = nc.tensor.matmul(ps[0:T, 1, 8 * k:8 * k + EX], xT[:, h, k * T:(k + 1) * T], rw[:, h, 0:EX],
                                                start=h == 0, stop=h == 1)
                else:
                    last = nc.tensor.matmul(ps[0:T, 1, 8 * k:8 * k + EX], rT[:, k * T:(k + 1) * T], rw2, start=True, stop=True)
            last.then_inc(s["logits"], 1)
            for n in pe_behind if layer == 0 else ():
                slot(n)
            for step in range(nsteps):
                if mix and step == 1:
                    pe.wait_ge(mix["marks"]["x2"], (g + 1 if last_turn else g + 2))
                if step < EX:
                    square(g, step, 0, xT, u_bank(step), "u", "h")
                if DEEP == 3 and 1 <= step <= EX:
                    e = step - 1
                    pe.wait_ge(s["h"], g * EX + e + 1)
                    square(g, e, EX, hid[e % 2], v_bank(e), "v", "h2")
                if step >= DEEP - 1:
                    rows_out(g, step - DEEP + 1)
                if step == 2:
                    pe.wait_ge(s["comb"], g + 1)
                    for k in range(2):
                        last = nc.tensor.transpose(ps[0:EX, 1, k * T:(k + 1) * T], comb[:, k, 0:EX], m.ident[0:T, 0:T])
                    last.then_inc(s["ctp"], 1)
                if layer == 1 and 2 <= step <= 5 and not last_turn:
                    head(g + 1, step - 2)
                for i in pe_slots.get(step, ()):
                    slot(i)
            if not last_turn:
                pe.wait_ge(s["xn"], 2 * g + 4)
                transpose_group(nc, m, 0, xn).then_inc(s["tp"], 1)
            pe.wait_ge(s["cT"], g + 1)
            pe.wait_ge(s["added"], g * YS + EX - 1)
            for k in range(2):
                last = nc.tensor.matmul(ps[0:T, 4 + EX % 2, k * D:(k + 1) * D], cT[:, k * T:(k + 1) * T], b_out, start=True, stop=True)
            last.then_inc(s["y"], 1)

        fed = G - 2 if group_part else G - 1
        with pe.Fori(0, fed) as g:
            turn(g, False)
        if group_part:
            turn(G - 2, False, False)
        turn(G - 1, True, False)

    return {"sync": sync, "vector": vector, "scalar": scalar, "tensor": tensor}


def nothing(n):
    pass


def each(slot, numbers):
    for n in numbers:
        slot(n)


def where_edges_fit(m, engine, fit, otherwise, n):
    value = engine.alloc_register(f"fits{n}")
    engine.reg_load([value], m.fits[0:1, 0:1])
    fits = engine.snap(value, min_val=0, max_val=1)
    if fit:
        with engine.If(fits > 0):
            fit(engine)
        with engine.Else():
            if otherwise:
                otherwise(engine)
    elif otherwise:
        with engine.If(fits < 1):
            otherwise(engine)
    engine.free_register(value)


def step(nc, m, fit, otherwise, n):
    with nc.Block() as block:

        @block.sync
        def _(sp):
            where_edges_fit(m, sp, fit.get("sync"), otherwise.get("sync"), n)

        @block.gpsimd
        def _(pool):
            where_edges_fit(m, pool, fit.get("gpsimd"), otherwise.get("gpsimd"), n)

        @block.vector
        def _(dve):
            where_edges_fit(m, dve, fit.get("vector"), otherwise.get("vector"), n)

        @block.scalar
        def _(act):
            where_edges_fit(m, act, fit.get("scalar"), otherwise.get("scalar"), n)

        @block.tensor
        def _(pe):
            where_edges_fit(m, pe, fit.get("tensor"), otherwise.get("tensor"), n)


def gps_kernel(nc, a, out):
    ctx = ExitStack()
    with ctx:
        m = Memory(nc, ctx)

        def sem(name):
            return ctx.enter_context(nc.semaphore(name))

        gather_marks = [{n: sem(f"{n}{layer}") for n in "loaded decoded ones_set idx hot summed bank_free".split()}
                        for layer in range(2)]
        common = "in xn tp xT logits gap th comb ctp cT u h y added"
        extra = (" table table_out w_in", " rh rT v h2 stored group agg agg_tp aT h7 h7T hid hidT head")
        expert_marks = [{n: sem(f"moe{layer}_{n}") for n in (common + extra[layer]).split()} for layer in range(2)]

        mix_marks = {n: sem(f"mix1_{n}") for n in ("set xn tp xT k v k_sb v_sb kv logits exp attn attn_tp attnT bxn btp "
                                                   "bxT q qT xf x2 ln ln_tp hT fc1 h1 fc2").split()}

        edges_and_mix0(nc, m, sem, a)

        one, two = m.long_chain, m.short_chain
        chunks = [group_sums(nc, m, layer, gather_marks[layer], one) for layer in range(2)]
        fit = [experts(nc, m, a, 0, expert_marks[0], one, group_part=chunks[0]),
               experts(nc, m, a, 1, expert_marks[1], one, out, chunks[1], mix1(nc, m, mix_marks, one, expert_marks[1]))]
        for layer in range(2):
            fit[layer]["gpsimd"] = chunks[layer]["gpsimd"]
        otherwise = [gather_sums(nc, m, a, 0, gather_marks[0], None, two),
                     experts(nc, m, a, 0, expert_marks[0], two),
                     gather_sums(nc, m, a, 1, gather_marks[1], mix1(nc, m, mix_marks, two), two),
                     experts(nc, m, a, 1, expert_marks[1], two, out)]
        for n in range(4):
            step(nc, m, fit[n] if n < 2 else {}, otherwise[n], n)


_INS = ("x src dst edge_weight L0_gnn_W L0_mix_wq L0_mix_bq L0_mix_wk L0_mix_bk L0_mix_wv L0_mix_bv L0_mix_wo L0_mix_bo "
        "L0_ffn_router_w L0_ffn_w1 L0_ffn_b1 L0_ffn_w2 L0_ffn_b2 L1_gnn_W L1_gnn_b L1_gnn_W1 L1_gnn_b1 L1_gnn_W2 L1_gnn_b2 "
        "L1_mix_w_qkv L1_mix_b_qkv L1_mix_norm_g L1_mix_norm_b L1_mix_w_fc1 L1_mix_b_fc1 L1_mix_w_fc2 L1_mix_b_fc2 "
        "L1_ffn_router_w1 L1_ffn_router_b1 L1_ffn_router_w2 L1_ffn_router_b2 L1_ffn_expert_w1 L1_ffn_expert_b1 "
        "L1_ffn_expert_w2 L1_ffn_expert_b2 L1_ffn_expert_w3 L1_ffn_expert_b3").split()


def kernel(**inputs):
    import concourse.bacc as bacc
    from concourse.bass_utils import run_bass_kernel_spmd

    nc = bacc.Bacc("TRN2", target_bir_lowering=False, num_devices=1)
    arrays, a = {}, {}
    for name in _INS:
        v = np.asarray(inputs[name])
        if name in ("L0_gnn_W", "L0_ffn_router_w"):
            v = v.T
        v = np.ascontiguousarray(v)
        arrays[f"in_{name}"] = v
        a[name] = nc.dram_tensor(f"in_{name}", v.shape, mybir.dt.from_np(v.dtype), kind="ExternalInput").ap()
    out = nc.dram_tensor("out", (N, D), F32, kind="ExternalOutput").ap()
    gps_kernel(nc, a, out)
    r = run_bass_kernel_spmd(nc, [arrays], core_ids=[0])
    return r.results[0]["out"]
```
